# Optimizing a Trainium2 kernel written in Bass

```python
import numpy as np
import jax
import jax.numpy as jnp

def _softmax(x, axis=-1):
    return jax.nn.softmax(x, axis=axis)

def _gelu(x):
    return jax.nn.gelu(x, approximate=True)

def _silu(x):
    return jax.nn.silu(x)

def _sigmoid(x):
    return jax.nn.sigmoid(x)

def _layernorm(x, axis=-1, eps=1e-05):
    m = jnp.mean(x, axis=axis, keepdims=True)
    v = jnp.var(x, axis=axis, keepdims=True)
    return (x - m) / jnp.sqrt(v + eps)

def _scatter_add(tgt, idx, src, axis=0):
    return tgt.at[idx].add(src)

def _segment_sum(src, seg, n):
    return jax.ops.segment_sum(src, seg, n)
kernel_name = 'mk_sandwich_d1_jaxref_r4_a9de32'

def setup_inputs(seed: int=0):
    np.random.seed(seed)
    _w = jnp.asarray

    def _L0_attn_setup():
        import jax, jax.numpy as jnp
        import numpy as np
        B, S, D, H = (2, 512, 512, 16)
        HD = D // H
        SCALE = 1.0 / np.sqrt(D).astype(np.float32)
        key = jax.random.key(seed)
        k1, k2, k3 = jax.random.split(key, 3)
        x = jax.random.normal(k1, (B, S, D), dtype=jnp.float32)
        W_qkv = jax.random.normal(k2, (3 * D, D), dtype=jnp.float32) * (1.0 / np.sqrt(D))
        W_proj = jax.random.normal(k3, (D, D), dtype=jnp.float32) * (1.0 / np.sqrt(D))
        return {'x': x, 'W_qkv': W_qkv, 'W_proj': W_proj}
    _L0_attn_in = _L0_attn_setup()

    def _L0_ffn_setup():
        import jax, jax.numpy as jnp
        import numpy as np
        B, S, D = (2, 512, 512)
        MOE_D = 352
        E = 16
        K = 6
        ALPHA = 0.001

        def _moe_forward(x, gate_w, w_gate, w_up, w_down):
            b, s, d = x.shape
            T = b * s
            h = x.reshape(T, d)
            logits = h @ gate_w.T
            scores = jax.nn.softmax(logits.astype(jnp.float32), axis=-1)
            topk_w, topk_idx = jax.lax.top_k(scores, K)
            cw = jnp.zeros((T, E), jnp.float32)
            cw = cw.at[jnp.arange(T)[:, None], topk_idx].add(topk_w)
            y = jnp.zeros((T, d), x.dtype)
            for e in range(E):
                g = h @ w_gate[e].T
                u = h @ w_up[e].T
                out = jax.nn.silu(g) * u @ w_down[e].T
                y = y + cw[:, e:e + 1].astype(x.dtype) * out
            counts = jnp.sum(jax.nn.one_hot(topk_idx.reshape(b, s * K), E, dtype=jnp.float32), axis=1)
            ce = counts * (E / (s * K))
            scores_bse = scores.reshape(b, s, E)
            aux = jnp.mean(jnp.sum(ce * scores_bse.mean(axis=1), axis=1)) * ALPHA
            return (y.reshape(b, s, d), aux)
        key = jax.random.key(seed)
        ks = jax.random.split(key, 5)
        sd = 1.0 / np.sqrt(D)
        sm = 1.0 / np.sqrt(MOE_D)
        return {'x': jax.random.normal(ks[0], (B, S, D), jnp.float32), 'gate_w': jax.random.normal(ks[1], (E, D), jnp.float32) * sd, 'w_gate': jax.random.normal(ks[2], (E, MOE_D, D), jnp.float32) * sd, 'w_up': jax.random.normal(ks[3], (E, MOE_D, D), jnp.float32) * sd, 'w_down': jax.random.normal(ks[4], (E, D, MOE_D), jnp.float32) * sm}
    _L0_ffn_in = _L0_ffn_setup()
    _d = {'L0_attn_x': _L0_attn_in['x'], 'L0_attn_W_qkv': _L0_attn_in['W_qkv'], 'L0_attn_W_proj': _L0_attn_in['W_proj'], 'L0_ffn_gate_w': _L0_ffn_in['gate_w'], 'L0_ffn_w_gate': _L0_ffn_in['w_gate'], 'L0_ffn_w_up': _L0_ffn_in['w_up'], 'L0_ffn_w_down': _L0_ffn_in['w_down']}
    _x0 = _d['L0_attn_x']
    _d['L0_attn_x'] = jax.random.normal(jax.random.fold_in(jax.random.key(seed), 1), (1, 2048, 512), dtype=_x0.dtype)
    del _x0
    return _d

def reference(L0_attn_x, L0_attn_W_qkv, L0_attn_W_proj, L0_ffn_gate_w, L0_ffn_w_gate, L0_ffn_w_up, L0_ffn_w_down):

    def _L0_attn_ref(x, W_qkv, W_proj):
        import jax, jax.numpy as jnp
        import numpy as np
        B, S, D, H = (2, 512, 512, 16)
        HD = D // H
        SCALE = 1.0 / np.sqrt(D).astype(np.float32)
        b, s, d = x.shape
        qkv = x @ W_qkv.T
        q, k, v = jnp.split(qkv, 3, axis=-1)
        q = q.reshape(b, s, H, HD).transpose(0, 2, 1, 3)
        k = k.reshape(b, s, H, HD).transpose(0, 2, 1, 3)
        v = v.reshape(b, s, H, HD).transpose(0, 2, 1, 3)
        attn = jnp.einsum('bhqd,bhkd->bhqk', q, k) * SCALE
        causal = jnp.tril(jnp.ones((s, s), dtype=bool))
        attn = jnp.where(causal[None, None], attn, -jnp.inf)
        probs = jax.nn.softmax(attn, axis=-1)
        out = jnp.einsum('bhqk,bhkd->bhqd', probs, v)
        out = out.transpose(0, 2, 1, 3).reshape(b, s, d)
        return out @ W_proj.T

    def _L0_ffn_ref(x, gate_w, w_gate, w_up, w_down):
        import jax, jax.numpy as jnp
        import numpy as np
        B, S, D = (2, 512, 512)
        MOE_D = 352
        E = 16
        K = 6
        ALPHA = 0.001

        def _moe_forward(x, gate_w, w_gate, w_up, w_down):
            b, s, d = x.shape
            T = b * s
            h = x.reshape(T, d)
            logits = h @ gate_w.T
            scores = jax.nn.softmax(logits.astype(jnp.float32), axis=-1)
            topk_w, topk_idx = jax.lax.top_k(scores, K)
            cw = jnp.zeros((T, E), jnp.float32)
            cw = cw.at[jnp.arange(T)[:, None], topk_idx].add(topk_w)
            y = jnp.zeros((T, d), x.dtype)
            for e in range(E):
                g = h @ w_gate[e].T
                u = h @ w_up[e].T
                out = jax.nn.silu(g) * u @ w_down[e].T
                y = y + cw[:, e:e + 1].astype(x.dtype) * out
            counts = jnp.sum(jax.nn.one_hot(topk_idx.reshape(b, s * K), E, dtype=jnp.float32), axis=1)
            ce = counts * (E / (s * K))
            scores_bse = scores.reshape(b, s, E)
            aux = jnp.mean(jnp.sum(ce * scores_bse.mean(axis=1), axis=1)) * ALPHA
            return (y.reshape(b, s, d), aux)
        y, _aux = _moe_forward(x, gate_w, w_gate, w_up, w_down)
        return y
    x = L0_attn_x
    x = x + _layernorm(_L0_attn_ref(_layernorm(x, axis=-1), L0_attn_W_qkv, L0_attn_W_proj), axis=-1)
    x = x + _layernorm(_L0_ffn_ref(_layernorm(x, axis=-1), L0_ffn_gate_w, L0_ffn_w_gate, L0_ffn_w_up, L0_ffn_w_down), axis=-1)
    return x

_drawn_inputs = setup_inputs


def setup_inputs(seed=0):
    import zlib

    import numpy as np

    out = dict(_drawn_inputs(seed))
    spreads = {}
    factors = {}
    for name, (base, spread) in spreads.items():
        noise = np.random.default_rng([zlib.crc32(name.encode()), seed]).standard_normal(out[name].shape)
        drawn = base * np.exp(spread * noise) if base else spread * noise
        out[name] = jnp.asarray(drawn.astype(out[name].dtype))
    for name, factor in factors.items():
        out[name] = (out[name] * factor).astype(out[name].dtype)
    return out
```

```python
from contextlib import ExitStack

import numpy as np

import concourse.bass as bass
from concourse import mybir

F32 = mybir.dt.float32
F32R = mybir.dt.float32r
ALU = mybir.AluOpType
ACT = mybir.ActivationFunctionType
AX_X = mybir.AxisListType.X

P = 128
T, D, H = 2048, 512, 16
HD = D // H
E, F, TOPK = 16, 352, 6
KC = D // P
NT = T // P
NB = 512
NTB = T // NB
EPS = 1e-5
SCALE = float(1.0 / np.sqrt(D))
MASKED = -1e30
LOWEST = -3e38
VW = 2 * HD + 1
PIECE = 256
VPIECES = D // PIECE
QK_PIECES = 2 * D // PIECE
PIECE_UNITS = PIECE // P * NTB
CHUNKS = E * F // P
PAIRS = CHUNKS // 2
GROUP = 32
NGROUPS = E * F // GROUP
GPE = F // GROUP
assert F % GROUP == 0 and E * F % (2 * P) == 0 and D == NB


def stepped(eng, first, loops, unroll, total, step):
    for t in range(first):
        step(t, t)
    with eng.Fori(0, loops) as i:
        for k in range(unroll):
            step(i * unroll + (first + k), first + k)
    for t in range(first + loops * unroll, total):
        step(t, t)


def inside(t, offset, total):
    return not isinstance(t, int) or 0 <= t + offset < total


def f32(ap):
    return ap.bitcast(F32)


def one(ap, t):
    return ap[bass.ds(t, 1)].rearrange("a p d -> (a p) d")


def three_passes(nc, out, pairs, chunks):
    n = 0
    for c in range(chunks):
        a_hi, a_lo, b_hi, b_lo = pairs(c)
        for a, b in ((a_hi, b_hi), (a_hi, b_lo), (a_lo, b_hi)):
            last = nc.tensor.matmul(out, a, b, start=n == 0, stop=n == 3 * chunks - 1)
            n += 1
    return last


def stage_embed_qkv(nc, x_dram, wqkv_dram, rows, v_all, ident, ln_consts, qk_dram):
    with ExitStack() as ctx:
        sb = lambda n, s, d: ctx.enter_context(nc.sbuf_tensor(n, s, d))
        pb = lambda n, s: ctx.enter_context(nc.psum_tensor(n, s, F32))
        sem = lambda n: ctx.enter_context(nc.semaphore(n))

        w_raw = rows[:, 0:12, :].rearrange("p a b -> p (a b)").rearrange("p (k n) -> p k n", k=KC)
        x_in = rows[:, 12:16, :]
        xn = sb("xn", [P, 2, D], F32)
        st = sb("e_st", [P, 2, 6], F32)
        mv = sb("e_mv", [P, 2, 2], F32)
        rstd = sb("e_rstd", [P, 2, 1], F32)
        veps = sb("e_veps", [P, 1], F32)
        xt_hi = sb("xt_hi", [P, 2, KC, P], F32R)
        xt_lo = sb("xt_lo", [P, 2, KC, P], F32R)
        xT_hi = sb("xT_hi", [P, KC, T], F32R)
        xT_lo = sb("xT_lo", [P, KC, T], F32R)
        w_hi = sb("e_w_hi", [P, 3, KC, PIECE], F32R)
        w_lo = sb("e_w_lo", [P, 3, KC, PIECE], F32R)
        qk_hi = sb("qk_hi", [P, 2, NB], F32R)
        qk_lo = sb("qk_lo", [P, 2, NB], F32R)
        tp = pb("e_tp", [P, 2, KC, P])
        vp = pb("e_vp", [P, 2, NB])
        qp = pb("e_qp", [P, 2, NB])

        ident_made, ones_set = sem("e_ident_made"), sem("e_ones_set")
        x_landed = [sem(f"e_x_landed{i}") for i in range(4)]
        wv_landed, wqk_landed = sem("e_wv_landed"), sem("e_wqk_landed")
        stats, aggr, rstd_done = sem("e_stats"), sem("e_aggr"), sem("e_rstd_done")
        veps_done = sem("e_veps_done")
        xn_ready, tp_ready = sem("e_xn_ready"), sem("e_tp_ready")
        xt_hi_done, xt_lo_done, xT_copied = sem("e_xt_hi_done"), sem("e_xt_lo_done"), [sem(f"e_xT_copied{i}") for i in range(2)]
        v_ready, v_hi_done, v_lo_done = sem("e_v_ready"), sem("e_v_hi_done"), sem("e_v_lo_done")
        wv_hi_done, wv_lo_done = sem("e_wv_hi_done"), sem("e_wv_lo_done")
        wqk_hi_done, wqk_lo_done = sem("e_wqk_hi_done"), sem("e_wqk_lo_done")
        unit_ready, unit_hi_done, unit_lo_done = sem("e_unit_ready"), sem("e_unit_hi"), sem("e_unit_lo")
        parked = [sem(f"e_parked{i}") for i in range(2)]
        block = ctx.enter_context(nc.Block())

        def slot_of(q):
            return (VPIECES + q) % 3

        def qk_units(eng, unit):
            for q in range(QK_PIECES):
                for f in range(PIECE // P):
                    base = (q * (PIECE // P) + f) * NTB
                    if base == 0:
                        for n in range(NTB):
                            unit(n, n % 2, q, f, n)
                    else:
                        with eng.Fori(0, NTB // 2) as i:
                            for k in range(2):
                                unit(i * 2 + (base + k), k, q, f, i * 2 + k)

        @block.sync
        def _(sp):
            for s in range(4):
                sp.dma_start(x_in[:, s, :], x_dram[s]).then_inc(x_landed[s], 16)
            sp.dma_start(w_raw[:, :, 2 * D:3 * D], wqkv_dram[:, :, 2 * D:3 * D]).then_inc(wv_landed, 16)

            def tile(t, k):
                if inside(t, 4, NT):
                    sp.wait_ge(xn_ready, t + 1)
                    sp.dma_start(x_in[:, k % 4, :], one(x_dram, t + 4)).then_inc(x_landed[k % 4], 16)
                sp.wait_ge(xt_lo_done, t + 1)
                toks = bass.ds(t * P, P)
                sp.dma_start(f32(xT_hi[:, :, toks]), f32(xt_hi[:, k % 2])).then_inc(xT_copied[k % 2], 16)
                sp.dma_start(f32(xT_lo[:, :, toks]), f32(xt_lo[:, k % 2])).then_inc(xT_copied[k % 2], 16)
            stepped(sp, 4, 2, 4, NT, tile)
            sp.dma_start(w_raw[:, :, 0:2 * D], wqkv_dram[:, :, 0:2 * D]).then_inc(wqk_landed, 16)

            def park(n, k, q, f, tb):
                which, row = q // 2, (q % 2) * PIECE + f * P
                sp.wait_ge(unit_lo_done, n + 1)
                for part, src in enumerate((qk_hi, qk_lo)):
                    sp.dma_start(qk_dram[2 * which + part, row:row + P, bass.ds(tb * NB, NB)],
                                 f32(src[:, k, :])).then_inc(parked[k], 16)
            qk_units(sp, park)
            for k in range(2):
                sp.wait_ge(parked[k], 16 * QK_PIECES * PIECE_UNITS)

        @block.gpsimd
        def _(pool):
            nc.gpsimd.memset(ident[:], 0.0).then_inc(ident_made, 1)
            pool.wait_ge(ident_made, 1)
            nc.gpsimd.affine_select(out=ident[:], in_=ident[:], compare_op=ALU.not_equal, fill=1.0, base=0,
                                    pattern=[[-1, P]], channel_multiplier=1).then_inc(ident_made, 1)
            nc.gpsimd.memset(ln_consts[:, 0:1], EPS).then_inc(ident_made, 1)
            nc.gpsimd.memset(ln_consts[:, 1:2], -0.5).then_inc(ident_made, 1)
            pool.wait_ge(ident_made, 4)
            nc.gpsimd.memset(f32(v_all[:, :, :, 2 * HD:VW]), 1.0).then_inc(ones_set, 1)

            def inverse_deviation(t, k):
                pool.wait_ge(aggr, t + 1)
                if inside(t, -1, NT):
                    pool.wait_ge(rstd_done, t)
                nc.gpsimd.tensor_tensor(veps[:], mv[:, k % 2, 1:2], ln_consts[:, 0:1], ALU.add).then_inc(veps_done, 1)
                pool.wait_ge(veps_done, t + 1)
                nc.gpsimd.tensor_tensor(rstd[:, k % 2], veps[:], ln_consts[:, 1:2], ALU.pow).then_inc(rstd_done, 1)

            stepped(pool, 4, 2, 4, NT, inverse_deviation)

            pool.wait_ge(wqk_landed, 16)
            for q in range(QK_PIECES):
                if 1 <= q <= VPIECES:
                    pool.wait_ge(v_ready, NT)
                if q > VPIECES:
                    pool.wait_ge(unit_ready, (q - 2) * PIECE_UNITS)
                raw = w_raw[:, :, q * PIECE:(q + 1) * PIECE]
                nc.gpsimd.tensor_copy(w_hi[:, slot_of(q)], raw).then_inc(wqk_hi_done, 1)
                pool.wait_ge(wqk_hi_done, q + 1)
                nc.gpsimd.tensor_tensor(w_lo[:, slot_of(q)], raw, f32(w_hi[:, slot_of(q)]),
                                        ALU.subtract).then_inc(wqk_lo_done, 1)

        @block.scalar
        def _(act):
            act.wait_ge(wv_landed, 16)
            for v in range(VPIECES):
                nc.scalar.activation(w_hi[:, v], w_raw[:, :, 2 * D + v * PIECE:2 * D + (v + 1) * PIECE],
                                     ACT.Copy).then_inc(wv_hi_done, 1)
            act.wait_ge(ones_set, 1)

            def high_parts(t, k):
                if inside(t, 0, NT):
                    act.wait_ge(tp_ready, t + 1)
                    if inside(t, -2, NT):
                        act.wait_ge(xT_copied[k % 2], (t - k % 2) * 16)
                        act.wait_ge(v_ready, t - 1)
                    nc.scalar.activation(xt_hi[:, k % 2], tp[:, k % 2], ACT.Copy).then_inc(xt_hi_done, 1)
                if inside(t, -1, NT):
                    act.wait_ge(v_ready, t)
                    nc.scalar.activation(v_all[:, :, bass.ds(t - 1, 1), 0:HD].rearrange("p h a c -> p (h a) c"),
                                         vp[:, (k - 1) % 2, :].rearrange("p (h c) -> p h c", h=H),
                                         ACT.Copy).then_inc(v_hi_done, 1)
            stepped(act, 4, 2, 4, NT + 1, high_parts)

            def unit_high(n, k, q, f, tb):
                act.wait_ge(unit_ready, n + 1)
                if not isinstance(n, int) or n >= 2:
                    act.wait_ge(parked[k], (n - k) * 16)
                nc.scalar.activation(qk_hi[:, k, :], qp[:, k, :], ACT.Copy).then_inc(unit_hi_done, 1)
            qk_units(act, unit_high)

        @block.vector
        def _(dve):
            def statistics(t, k):
                s, j = k % 4, k % 2
                dve.wait_ge(x_landed[s], (t - s) * 4 + 16)
                nc.vector.bn_stats(st[:, j], x_in[:, s, :]).then_inc(stats, 1)

            def aggregate(t, k):
                nc.vector.bn_aggr(mv[:, k % 2], st[:, k % 2]).then_inc(aggr, 1)

            def normalise(t, k):
                dve.wait_ge(rstd_done, t + 1)
                if inside(t, -2, NT):
                    dve.wait_ge(tp_ready, t - 1)
                nc.vector.tensor_scalar(xn[:, k % 2], x_in[:, k % 4, :], mv[:, k % 2, 0:1], rstd[:, k % 2, 0:1],
                                        ALU.subtract, ALU.mult).then_inc(xn_ready, 1)

            def low_parts(t, k):
                if inside(t, 2, NT):
                    statistics(t + 2, k + 2)
                    dve.wait_ge(stats, t + 3)
                if inside(t, 1, NT):
                    normalise(t + 1, k + 1)
                if inside(t, 2, NT):
                    aggregate(t + 2, k + 2)
                if inside(t, 0, NT):
                    dve.wait_ge(xt_hi_done, t + 1)
                    nc.vector.tensor_tensor(xt_lo[:, k % 2], tp[:, k % 2], f32(xt_hi[:, k % 2]),
                                            ALU.subtract).then_inc(xt_lo_done, 1)
                if inside(t, -1, NT):
                    dve.wait_ge(v_hi_done, t)
                    v_tile = v_all[:, :, bass.ds(t - 1, 1), :].rearrange("p h a c -> p (h a) c")
                    nc.vector.tensor_tensor(v_tile[:, :, HD:2 * HD],
                                            vp[:, (k - 1) % 2, :].rearrange("p (h c) -> p h c", h=H),
                                            f32(v_tile[:, :, 0:HD]), ALU.subtract).then_inc(v_lo_done, 1)
            for t in range(2):
                statistics(t, t)
                dve.wait_ge(stats, t + 1)
                aggregate(t, t)
            normalise(0, 0)
            for v in range(VPIECES):
                dve.wait_ge(wv_hi_done, v + 1)
                nc.vector.tensor_tensor(w_lo[:, v], w_raw[:, :, 2 * D + v * PIECE:2 * D + (v + 1) * PIECE],
                                        f32(w_hi[:, v]), ALU.subtract).then_inc(wv_lo_done, 1)
            stepped(dve, 4, 2, 4, NT + 1, low_parts)

            def unit_low(n, k, q, f, tb):
                dve.wait_ge(unit_hi_done, n + 1)
                nc.vector.tensor_tensor(qk_lo[:, k, :], qp[:, k, :], f32(qk_hi[:, k, :]),
                                        ALU.subtract).then_inc(unit_lo_done, 1)
            qk_units(dve, unit_low)

        @block.tensor
        def _(pe):
            pe.wait_ge(ident_made, 2)

            def transpose_tile(t, k):
                pe.wait_ge(xn_ready, t + 1)
                if inside(t, -2, NT):
                    pe.wait_ge(xt_lo_done, t - 1)
                for c in range(KC):
                    last = nc.tensor.transpose(tp[:, k % 2, c, :], xn[:, k % 2, c * P:(c + 1) * P], ident[:])
                last.then_inc(tp_ready, 1)

            def values(t, k):
                if inside(t, 1, NT):
                    transpose_tile(t + 1, k + 1)
                pe.wait_ge(xt_lo_done, t + 1)
                if isinstance(t, int) and t == 0:
                    pe.wait_ge(wv_lo_done, VPIECES)
                if inside(t, -2, NT):
                    pe.wait_ge(v_lo_done, t - 1)
                for v in range(VPIECES):
                    last = three_passes(nc, vp[:, k % 2, v * PIECE:(v + 1) * PIECE],
                                        lambda c: (xt_hi[:, k % 2, c], xt_lo[:, k % 2, c], w_hi[:, v, c], w_lo[:, v, c]), KC)
                last.then_inc(v_ready, 1)
            transpose_tile(0, 0)
            stepped(pe, 4, 2, 4, NT, values)

            def unit(n, k, q, f, tb):
                if isinstance(n, int) and n == 0:
                    for slot in range(2):
                        pe.wait_ge(xT_copied[slot], 32 * NT // 2)
                pe.wait_ge(wqk_lo_done, q + 1)
                if not isinstance(n, int) or n >= 2:
                    pe.wait_ge(unit_lo_done, n - 1)
                cols, toks = slice(f * P, (f + 1) * P), bass.ds(tb * NB, NB)
                three_passes(nc, qp[:, k, :],
                             lambda c: (w_hi[:, slot_of(q), c, cols], w_lo[:, slot_of(q), c, cols],
                                        xT_hi[:, c, toks], xT_lo[:, c, toks]), KC).then_inc(unit_ready, 1)
            qk_units(pe, unit)


S_TILES = [(j, kp, 2 * P * max(0, kp - 2 * j)) for j in range(NTB) for kp in range(2 * j + 2)]
NS = len(S_TILES)
J_FIRST = [next(t for t, s in enumerate(S_TILES) if s[0] == j) for j in range(NTB)]
J_LAST = [max(t for t, s in enumerate(S_TILES) if s[0] == j) for j in range(NTB)]
LAG = 3
RING = 4
PIECES = [(qb, kb) for qb in range(NT) for kb in range(qb // 4 + 1)]
NPC = len(PIECES)
QA = 12
NPC_A = sum(1 for qb, _ in PIECES if qb < QA)
PIECES_AT = [0] * 5 + [3] * 10 + [2] * 5
assert sum(PIECES_AT) == NPC and NS == len(PIECES_AT) and NS % RING == 0 and sum(PIECES_AT[:13]) == NPC_A
SHARED_AT = {1: "max_b", 4: 3, 6: 0, 10: 1, 14: "max_a", 16: 2}
PIECES_AT_A = 13
KQ_LOADS = 6
FW = HD + 2
CONSTS = 11
HI_DVE = {t for t in range(NS) if t % 3 == 2}
LO_POOL = {t for t in range(NS) if t % 3 == 1}


def count_before(which, t):
    return sum(1 for s in which if s < t)


def stage_attention(nc, rows, v_all, ident, qk_dram):
    with ExitStack() as ctx:
        sb = lambda n, s, d: ctx.enter_context(nc.sbuf_tensor(n, s, d))
        pb = lambda n, s: ctx.enter_context(nc.psum_tensor(n, s, F32))
        sem = lambda n: ctx.enter_context(nc.semaphore(n))

        K_ROWS, ROW_MAX = 3 * HD, 3 * HD
        ks = [sb(f"k_stack{p}", [P, T], F32R) for p in range(2)]
        qs = [sb(f"q_stack{p}", [P, T], F32R) for p in range(2)]
        vs = [sb(f"v_head{p}", [P, NT, VW], F32R) for p in range(2)]
        prob = sb("prob", [P, RING, 2, NB], F32)
        prob_hi = sb("prob_hi", [P, RING, 2, NB], F32R)
        prob_lo = sb("prob_lo", [P, RING, 2, NB], F32R)
        o_sb = sb("o_sb", [VW, 2, NB], F32)
        fold = sb("fold", [VW, HD + 2], F32)
        neg_ident = sb("neg_ident", [P, P], F32)
        ident_r = sb("ident_r", [P, P], F32R)
        mask_q = sb("mask_q", [P, P], F32R)
        mask_k = sb("mask_k", [P, 2 * P], F32R)
        mask_f = sb("mask_f", [P, 2 * P], F32)
        part_max = sb("part_max", [P, NT, NTB], F32)
        row_max = sb("row_max", [P, NT], F32)
        max_rows = sb("max_rows", [QA, P], F32R)
        max_rows_b = sb("max_rows_b", [NT - QA, P], F32R)
        recip = sb("recip", [P, NTB, 1], F32)

        mp = pb("a_mp", [P, 2, NB])
        sp_ = pb("a_sp", [P, 2, 2, NB])
        op = pb("a_op", [P, NB])
        shared = pb("a_shared", [P, NB])

        consts, dve_consts = sem("a_consts"), sem("a_dve_consts")
        kq_landed = [sem(f"a_kq_landed{p}") for p in range(2)]
        v_landed = [sem(f"a_v_landed{p}") for p in range(2)]
        max_a_landed = [sem(f"a_max_a_landed{p}") for p in range(2)]
        max_b_landed = [sem(f"a_max_b_landed{p}") for p in range(2)]
        piece_ready, piece_done = sem("a_piece_ready"), sem("a_piece_done")
        row_max_a, row_max_b = sem("a_row_max_a"), sem("a_row_max_b")
        max_a_out, max_b_out = sem("a_max_a_out"), sem("a_max_b_out")
        scores_ready, prob_ready = sem("a_scores_ready"), sem("a_prob_ready")
        hi_act, hi_dve = sem("a_hi_act"), sem("a_hi_dve")
        lo_dve, lo_pool = sem("a_lo_dve"), sem("a_lo_pool")
        pv_done, out_copied = sem("a_pv_done"), sem("a_out_copied")
        max_turned, out_turned, out_stored = sem("a_max_turned"), sem("a_out_turned"), sem("a_out_stored")
        recip_done = sem("a_recip_done")
        block = ctx.enter_context(nc.Block())

        def heads(eng, head):
            head(0, 0, 0, True, False)
            with eng.Fori(0, (H - 2) // 2) as i:
                head(i * 2 + 1, 1, i, False, False)
                head(i * 2 + 2, 0, i + 1, False, False)
            head(H - 1, 1, (H - 1) // 2, False, True)

        def wait_hi(eng, h, t):
            if t in HI_DVE:
                eng.wait_ge(hi_dve, h * len(HI_DVE) + (count_before(HI_DVE, t) + 1))
            else:
                eng.wait_ge(hi_act, h * (NS - len(HI_DVE)) + (t - count_before(HI_DVE, t) + 1))

        def wait_lo(eng, h, t):
            if t in LO_POOL:
                eng.wait_ge(lo_pool, h * len(LO_POOL) + (count_before(LO_POOL, t) + 1))
            else:
                eng.wait_ge(lo_dve, h * (NS - len(LO_POOL)) + (t - count_before(LO_POOL, t) + 1))

        @block.sync
        def _(sp):
            def load_head(h, p):
                for dst, parts in ((ks[p], (2, 3, 2)), (qs[p], (0, 0, 1))):
                    for n, part in enumerate(parts):
                        sp.dma_start(f32(dst[n * HD:(n + 1) * HD, :]),
                                     qk_dram[part, bass.ds(h * HD, HD), :]).then_inc(kq_landed[p], 16)
            def load_v(h, p):
                sp.dma_start(f32(vs[p][:]), f32(v_all[:, bass.ds(h, 1), :, :]).rearrange("p a t c -> p (a t) c")
                             ).then_inc(v_landed[p], 16)

            def send_max_a(p):
                sp.dma_start(f32(qs[p][ROW_MAX:ROW_MAX + 1, 0:QA * P]).rearrange("a (t q) -> a t q", t=QA),
                             f32(max_rows[:, :])).then_inc(max_a_landed[p], 16)

            def send_max_b(p):
                sp.dma_start(f32(qs[p][ROW_MAX:ROW_MAX + 1, QA * P:T]).rearrange("a (t q) -> a t q", t=NT - QA),
                             f32(max_rows_b[:, :])).then_inc(max_b_landed[p], 16)

            load_head(0, 0)
            load_v(0, 0)
            sp.wait_ge(max_a_out, 1)
            send_max_a(0)
            sp.wait_ge(max_b_out, 1)
            send_max_b(0)

            def head(h, p, visit, first, last):
                if not last:
                    if not first:
                        sp.wait_ge(scores_ready, h * NS)
                    load_head(h + 1, 1 - p)
                    if not first:
                        sp.wait_ge(pv_done, h * NS)
                    load_v(h + 1, 1 - p)
                if not first:
                    sp.wait_ge(max_b_out, h + 1)
                    send_max_b(p)
                if not last:
                    sp.wait_ge(max_a_out, h + 2)
                    send_max_a(1 - p)
            heads(sp, head)

        @block.gpsimd
        def _(pool):
            made = [0]

            def make(ins):
                made[0] += 1
                ins.then_inc(consts, 1)
                pool.wait_ge(consts, made[0])

            make(nc.gpsimd.memset(fold[:], 0.0))
            for off in (0, HD):
                make(nc.gpsimd.affine_select(out=fold[:, 0:HD], in_=fold[:, 0:HD], compare_op=ALU.not_equal, fill=1.0,
                                             base=-off, pattern=[[-1, HD]], channel_multiplier=1))
            make(nc.gpsimd.memset(fold[2 * HD:VW, HD:HD + 1], 1.0))
            make(nc.gpsimd.tensor_copy(ident_r[:], ident[:]))
            make(nc.gpsimd.memset(mask_f[:], 0.0))
            make(nc.gpsimd.affine_select(out=mask_f[:, 0:P], in_=mask_f[:, 0:P], compare_op=ALU.is_ge, fill=MASKED,
                                         base=0, pattern=[[-1, P]], channel_multiplier=1))
            make(nc.gpsimd.tensor_copy(mask_q[:], mask_f[:, 0:P]))
            make(nc.gpsimd.memset(mask_f[:, 0:P], 0.0))
            make(nc.gpsimd.affine_select(out=mask_f[:], in_=mask_f[:], compare_op=ALU.is_ge, fill=MASKED,
                                         base=-P, pattern=[[1, 2 * P]], channel_multiplier=-1))
            make(nc.gpsimd.tensor_copy(mask_k[:], mask_f[:]))
            assert made[0] == CONSTS

            def head(h, p, visit, first, last):
                for t in sorted(LO_POOL):
                    j, kp, c0 = S_TILES[t]
                    pool.wait_ge(prob_ready, h * NS + (t + 1))
                    wait_hi(pool, h, t)
                    nc.gpsimd.tensor_tensor(prob_lo[:, t % RING, :, c0:NB], prob[:, t % RING, :, c0:NB],
                                            f32(prob_hi[:, t % RING, :, c0:NB]), ALU.subtract).then_inc(lo_pool, 1)
            heads(pool, head)

        @block.scalar
        def _(act):
            def copy_out(g, j, done):
                act.wait_ge(pv_done, done)
                if not (isinstance(g, int) and g < 2):
                    act.wait_ge(out_turned, g - 1)
                nc.scalar.activation(o_sb[:, j % 2, :], op[0:VW, :], ACT.Copy).then_inc(out_copied, 1)

            def head(h, p, visit, first, last):
                for t, (j, kp, c0) in enumerate(S_TILES):
                    act.wait_ge(scores_ready, h * NS + (t + 1))
                    if not (first and t < RING):
                        act.wait_ge(pv_done, h * NS + (t + 1 - RING))
                    nc.scalar.activation(prob[:, t % RING, :, c0:NB], sp_[:, t % 2, :, c0:NB], ACT.Exp,
                                         scale=SCALE).then_inc(prob_ready, 1)
                    if t not in HI_DVE:
                        act.wait_ge(prob_ready, h * NS + (t + 1))
                        nc.scalar.activation(prob_hi[:, t % RING, :, c0:NB], prob[:, t % RING, :, c0:NB],
                                             ACT.Copy).then_inc(hi_act, 1)
                    if t == J_LAST[-1] + LAG - NS and not first:
                        copy_out(h * NTB - 1, NTB - 1, h * NS)
                    for jj in range(NTB - 1):
                        if t == J_LAST[jj] + LAG:
                            copy_out(h * NTB + jj, jj, h * NS + (J_LAST[jj] + 1))
            heads(act, head)
            copy_out(H * NTB - 1, NTB - 1, H * NS)

        @block.vector
        def _(dve):
            nc.vector.memset(part_max[:], LOWEST).then_inc(dve_consts, 1)
            nc.vector.tensor_scalar(neg_ident[:], ident[:], -1.0, None, ALU.mult).then_inc(dve_consts, 1)
            for p in range(2):
                nc.vector.memset(f32(ks[p][ROW_MAX:ROW_MAX + 1, :]), 1.0).then_inc(dve_consts, 1)
            dve.wait_ge(dve_consts, 4)

            def piece(h, n):
                qb, kb = PIECES[n]
                width = min(NB, (qb + 1) * P - kb * NB)
                dve.wait_ge(piece_ready, h * NPC + (n + 1))
                nc.vector.reduce_max(part_max[:, qb, kb:kb + 1], mp[:, n % 2, 0:width], AX_X).then_inc(piece_done, 1)

            def row_maxima(h, part):
                tiles, count, done = ((slice(0, QA), NPC_A, row_max_a) if part == "a" else
                                      (slice(QA, NT), NPC, row_max_b))
                dve.wait_ge(piece_done, h * NPC + count)
                nc.vector.tensor_reduce(row_max[:, tiles], part_max[:, tiles, :], AX_X, ALU.max).then_inc(done, 1)

            def maxima_out(h, part):
                dst, done = (max_rows, max_a_out) if part == "a" else (max_rows_b, max_b_out)
                dve.wait_ge(max_turned, h * 2 + (1 if part == "a" else 2))
                nc.vector.tensor_copy(dst[:, :], shared[0:dst.shape[0], 0:P]).then_inc(done, 1)

            def store_out(h, g, j):
                dve.wait_ge(out_turned, g + 1)
                turned = shared[:, 0:NTB * FW].rearrange("p (a c) -> p a c", c=FW)
                nc.vector.reciprocal(recip[:], turned[:, :, HD:HD + 1]).then_inc(recip_done, 1)
                dve.wait_ge(recip_done, g + 1)
                nc.vector.tensor_tensor(rows[:, NTB * j:NTB * (j + 1), bass.ds(h * HD, HD)], turned[:, :, 0:HD],
                                        recip[:].to_broadcast([P, NTB, HD]), ALU.mult).then_inc(out_stored, 1)

            def low_part(h, t):
                if t in LO_POOL:
                    return
                c0 = S_TILES[t][2]
                wait_hi(dve, h, t)
                nc.vector.tensor_tensor(prob_lo[:, t % RING, :, c0:NB], prob[:, t % RING, :, c0:NB],
                                        f32(prob_hi[:, t % RING, :, c0:NB]), ALU.subtract).then_inc(lo_dve, 1)

            for n in range(NPC_A):
                piece(0, n)
            row_maxima(0, "a")
            maxima_out(0, "a")
            for n in range(NPC_A, NPC):
                piece(0, n)
            row_maxima(0, "b")
            maxima_out(0, "b")

            def head(h, p, visit, first, last):
                for t, (j, kp, c0) in enumerate(S_TILES):
                    if t == 0 and not first:
                        row_maxima(h, "b")
                    if t == PIECES_AT_A and not last:
                        row_maxima(h + 1, "a")
                    if not last:
                        for n in range(sum(PIECES_AT[:t]), sum(PIECES_AT[:t + 1])):
                            piece(h + 1, n)
                    if t in HI_DVE:
                        dve.wait_ge(prob_ready, h * NS + (t + 1))
                        nc.vector.tensor_copy(prob_hi[:, t % RING, :, c0:NB], prob[:, t % RING, :, c0:NB]
                                              ).then_inc(hi_dve, 1)
                    if t > 0:
                        low_part(h, t - 1)
                    elif not first:
                        low_part(h - 1, NS - 1)
                    what = SHARED_AT.get(t)
                    if what == "max_b" and not first:
                        maxima_out(h, "b")
                    if what == "max_a" and not last:
                        maxima_out(h + 1, "a")
                    if what == NTB - 1 and not first:
                        store_out(h - 1, h * NTB - 1, NTB - 1)
                    if what in range(NTB - 1):
                        store_out(h, h * NTB + what, what)
            heads(dve, head)
            low_part(H - 1, NS - 1)
            store_out(H - 1, H * NTB - 1, NTB - 1)

        @block.tensor
        def _(pe):
            def piece(h, p, n):
                qb, kb = PIECES[n]
                k0, k1 = kb * NB, min((kb + 1) * NB, (qb + 1) * P)
                if not (isinstance(h, int) and h == 0 and n < 2):
                    pe.wait_ge(piece_done, h * NPC + (n - 1))
                diagonal = k1 == (qb + 1) * P
                last = nc.tensor.matmul(mp[:, n % 2, 0:k1 - k0], qs[p][0:K_ROWS, qb * P:(qb + 1) * P],
                                        ks[p][0:K_ROWS, k0:k1], start=True, stop=not diagonal)
                if diagonal:
                    last = nc.tensor.matmul(mp[:, n % 2, k1 - k0 - P:k1 - k0], ident_r[:], mask_q[:],
                                            start=False, stop=True)
                last.then_inc(piece_ready, 1)

            def turn_maxima(h, part):
                tiles, done = (slice(0, QA), row_max_a) if part == "a" else (slice(QA, NT), row_max_b)
                pe.wait_ge(done, h + 1)
                nc.tensor.matmul(shared[0:tiles.stop - tiles.start, 0:P], row_max[:, tiles], neg_ident[:],
                                 start=True, stop=True).then_inc(max_turned, 1)

            def turn_out(g, j):
                pe.wait_ge(out_copied, g + 1)
                for q in range(NTB):
                    last = nc.tensor.matmul(shared[:, q * FW:q * FW + HD + 1], o_sb[:, j % 2, q * P:(q + 1) * P],
                                            fold[:, 0:HD + 1], start=True, stop=True)
                last.then_inc(out_turned, 1)

            def times_v(h, p, t):
                j, kp, c0 = S_TILES[t]
                if t == J_FIRST[j] and not (isinstance(h, int) and h == 0 and j == 0):
                    pe.wait_ge(out_copied, h * NTB + j)
                wait_hi(pe, h, t)
                n, total = 0, 4
                for part, wait in ((prob_hi, None), (prob_lo, wait_lo)):
                    if wait is not None:
                        wait(pe, h, t)
                    for b in range(2):
                        cols = slice(c0 + (P if b and kp >= 2 * j else 0), NB)
                        last = nc.tensor.matmul(op[0:VW, cols], vs[p][:, 2 * kp + b, :], part[:, t % RING, b, cols],
                                                start=t == J_FIRST[j] and n == 0, stop=t == J_LAST[j] and n == total - 1)
                        n += 1
                last.then_inc(pv_done, 1)

            def scores(h, p, t):
                j, kp, c0 = S_TILES[t]
                if not (isinstance(h, int) and h == 0 and t < 2):
                    pe.wait_ge(prob_ready, h * NS + (t - 1))
                for b in range(2):
                    kb = 2 * kp + b
                    diagonal = kp >= 2 * j
                    last = nc.tensor.matmul(sp_[:, t % 2, b, c0:NB], ks[p][0:ROW_MAX + 1, kb * P:(kb + 1) * P],
                                            qs[p][0:ROW_MAX + 1, j * NB + c0:(j + 1) * NB], start=True, stop=not diagonal)
                    if diagonal:
                        mask = mask_k[:, :] if b else mask_k[:, P:2 * P]
                        last = nc.tensor.matmul(sp_[:, t % 2, b, c0:c0 + mask.shape[1]], ident_r[:], mask,
                                                start=False, stop=True)
                last.then_inc(scores_ready, 1)

            pe.wait_ge(consts, CONSTS)
            pe.wait_ge(dve_consts, 4)
            pe.wait_ge(kq_landed[0], 16 * KQ_LOADS)
            for n in range(NPC_A):
                piece(0, 0, n)
            turn_maxima(0, "a")
            for n in range(NPC_A, NPC):
                piece(0, 0, n)
            pe.wait_ge(max_a_out, 1)
            turn_maxima(0, "b")

            def head(h, p, visit, first, last):
                for t, (j, kp, c0) in enumerate(S_TILES):
                    if t == 0:
                        pe.wait_ge(max_a_landed[p], visit * 16 + 16)
                    if t == J_FIRST[NTB - 1]:
                        pe.wait_ge(max_b_landed[p], visit * 16 + 16)
                    scores(h, p, t)
                    if t >= LAG:
                        if t == LAG:
                            pe.wait_ge(v_landed[p], visit * 16 + 16)
                        times_v(h, p, t - LAG)
                    elif not first:
                        times_v(h - 1, 1 - p, NS - LAG + t)
                    if not last:
                        if PIECES_AT[t] and not any(PIECES_AT[:t]):
                            pe.wait_ge(kq_landed[1 - p], (visit + p) * (16 * KQ_LOADS) + 16 * KQ_LOADS)
                        for n in range(sum(PIECES_AT[:t]), sum(PIECES_AT[:t + 1])):
                            piece(h + 1, 1 - p, n)
                    what = SHARED_AT.get(t)
                    if what == "max_b" and not first:
                        pe.wait_ge(out_stored, h * NTB - 1)
                        turn_maxima(h, "b")
                    if what == NTB - 1 and not first:
                        pe.wait_ge(max_b_out, h + 1)
                        turn_out(h * NTB - 1, NTB - 1)
                    if what == 0:
                        if first:
                            pe.wait_ge(max_b_out, 1)
                        else:
                            pe.wait_ge(out_stored, h * NTB)
                        turn_out(h * NTB, 0)
                    if what == 1:
                        pe.wait_ge(out_stored, h * NTB + 1)
                        turn_out(h * NTB + 1, 1)
                    if what == "max_a" and not last:
                        pe.wait_ge(out_stored, h * NTB + 2)
                        turn_maxima(h + 1, "a")
                    if what == 2:
                        if last:
                            pe.wait_ge(out_stored, h * NTB + 2)
                        else:
                            pe.wait_ge(max_a_out, h + 2)
                        turn_out(h * NTB + 2, 2)
            heads(pe, head)
            for t in range(NS - LAG, NS):
                times_v(H - 1, (H - 1) % 2, t)
            pe.wait_ge(out_stored, H * NTB - 1)
            turn_out(H * NTB - 1, NTB - 1)


def stage_project_route(nc, x_dram, wproj_dram, wgate_dram, rows, ident, ln_consts, h_hi, h_lo, x1_dram,
                        cw_dram):
    with ExitStack() as ctx:
        sb = lambda n, s, d: ctx.enter_context(nc.sbuf_tensor(n, s, d))
        pb = lambda n, s: ctx.enter_context(nc.psum_tensor(n, s, F32))
        sem = lambda n: ctx.enter_context(nc.semaphore(n))

        w_raw = sb("p_w_raw", [P, KC, D + E], F32)
        w_hi = sb("p_w_hi", [P, KC, D + E], F32R)
        w_lo = sb("p_w_lo", [P, KC, D + E], F32R)
        a_in = sb("a_in", [P, 2, D], F32)
        at_hi = sb("at_hi", [P, 2, KC, P], F32R)
        at_lo = sb("at_lo", [P, 2, KC, P], F32R)
        ht_hi = sb("ht_hi", [P, 2, KC, P], F32R)
        ht_lo = sb("ht_lo", [P, 2, KC, P], F32R)
        x_in = sb("p_x_in", [P, 4, D], F32)
        branch = sb("branch", [P, 2, D], F32)
        x1 = sb("x1", [P, 4, D], F32)
        hn = sb("hn", [P, 2, D], F32)
        st = sb("p_st", [P, 2, 2, 6], F32)
        mv = sb("p_mv", [P, 2, 2, 2], F32)
        rstd = sb("p_rstd", [P, 2, 2, 1], F32)
        veps = sb("p_veps", [P, 2, 1], F32)
        logits = sb("logits", [P, NT, E], F32)
        top = sb("top", [P, NT, 1], F32)
        total = sb("total", [P, NT, 1], F32)
        SW = E + 2
        scores = sb("scores", [P, NT, SW], F32)
        best = sb("best", [P, NT, 8], F32)
        rest = sb("rest", [P, NT, SW], F32)
        cw = sb("cw", [P, NT, E], F32)
        cwT = sb("cwT", [E, T], F32)
        tps = pb("p_tps", [P, 4, NB])
        prj = pb("p_prj", [P, 2, NB])
        lg = pb("p_lg", [P, 2, NB])

        w_landed, w_hi_done, w_lo_done = sem("p_w_landed"), sem("p_w_hi_done"), sem("p_w_lo_done")
        x_landed = [sem(f"p_x_landed{i}") for i in range(4)]
        x1_stored = [sem(f"p_x1_stored{i}") for i in range(4)]
        a_copied, at_ready, at_hi_done, at_lo_done = (sem("p_a_copied"), sem("p_at_ready"), sem("p_at_hi_done"),
                                                      sem("p_at_lo_done"))
        veps_done = [sem(f"p_veps_done{i}") for i in range(2)]
        proj_ready, x1_ready = sem("p_proj_ready"), sem("p_x1_ready")
        stats1, aggr1, rstd1, branch_ready = sem("p_stats1"), sem("p_aggr1"), sem("p_rstd1"), sem("p_branch_ready")
        stats2, aggr2, rstd2, hn_ready = sem("p_stats2"), sem("p_aggr2"), sem("p_rstd2"), sem("p_hn_ready")
        ht_ready, ht_hi_done, ht_lo_done, h_copied = (sem("p_ht_ready"), sem("p_ht_hi_done"), sem("p_ht_lo_done"),
                                                      [sem(f"p_h_copied{i}") for i in range(2)])
        logits_ready, logits_copied = sem("p_logits_ready"), sem("p_logits_copied")
        marks_set, route, exp_done = sem("p_marks_set"), sem("p_route"), sem("p_exp_done")
        cw_ready, cwT_turned, cwT_ready, cw_stored = sem("p_cw_ready"), sem("p_cwT_turned"), sem("p_cwT_ready"), sem("p_cw_stored")
        block = ctx.enter_context(nc.Block())

        STEPS = NT + 3
        AHEAD = 1

        @block.sync
        def _(sp):
            sp.dma_start(w_raw[:, :, 0:D], wproj_dram).then_inc(w_landed, 16)
            sp.dma_start(w_raw[:, :, D:D + E], wgate_dram).then_inc(w_landed, 16)
            for s in range(4):
                sp.dma_start(x_in[:, s, :], x_dram[s]).then_inc(x_landed[s], 16)

            def step(t, k):
                if inside(t, 0, NT):
                    store(t, k)
                if inside(t, -2, NT):
                    sp.wait_ge(ht_lo_done, t - 1)
                    toks = bass.ds((t - 2) * P, P)
                    sp.dma_start(f32(h_hi[:, :, toks]), f32(ht_hi[:, k % 2])).then_inc(h_copied[k % 2], 16)
                    sp.dma_start(f32(h_lo[:, :, toks]), f32(ht_lo[:, k % 2])).then_inc(h_copied[k % 2], 16)

            def store(t, k):
                sp.wait_ge(x1_ready, t + 1)
                sp.dma_start(one(x1_dram, t), x1[:, k % 4, :]).then_inc(x1_stored[k % 4], 16)
                if inside(t, 4, NT):
                    sp.dma_start(x_in[:, k % 4, :], one(x_dram, t + 4)).then_inc(x_landed[k % 4], 16)
            stepped(sp, 4, 2, 4, STEPS, step)
            sp.wait_ge(cwT_ready, 4)
            groups = cw_dram.rearrange("(e g) t -> e g t", g=GPE)
            sp.dma_start(groups, cwT[:, :].unsqueeze(1).to_broadcast([E, GPE, T])).then_inc(cw_stored, 16)
            sp.wait_ge(cw_stored, 16)
            for s in range(4):
                sp.wait_ge(x1_stored[s], 16 * NT // 4)
            for slot in range(2):
                sp.wait_ge(h_copied[slot], 32 * NT // 2)

        @block.gpsimd
        def _(pool):
            nc.gpsimd.memset(scores[:, :, E:E + 1], -1.0).then_inc(marks_set, 1)
            nc.gpsimd.memset(scores[:, :, E + 1:E + 2], -2.0).then_inc(marks_set, 1)

            def copy_in(t, k):
                if inside(t, -2, NT):
                    pool.wait_ge(at_ready, t - 1)
                nc.gpsimd.tensor_copy(a_in[:, k % 2, :], rows[:, bass.ds(t, 1), :].rearrange("p a d -> p (a d)")
                                      ).then_inc(a_copied, 1)
            copy_in(0, 0)
            copy_in(1, 1)

            def inverse_deviation(t, which, j, aggr, done):
                pool.wait_ge(aggr, t + 1)
                if inside(t, -1, NT):
                    pool.wait_ge(done, t)
                nc.gpsimd.tensor_tensor(veps[:, which], mv[:, which, j, 1:2], ln_consts[:, 0:1], ALU.add).then_inc(veps_done[which], 1)
                pool.wait_ge(veps_done[which], t + 1)
                nc.gpsimd.tensor_tensor(rstd[:, which, j], veps[:, which], ln_consts[:, 1:2], ALU.pow).then_inc(done, 1)

            def step(t, k):
                if inside(t, 2, NT):
                    copy_in(t + 2, k + 2)
                if inside(t, 0, NT):
                    inverse_deviation(t, 0, k % 2, aggr1, rstd1)
                if inside(t, -1, NT):
                    inverse_deviation(t - 1, 1, (k - 1) % 2, aggr2, rstd2)
                if inside(t, 0, NT):
                    pool.wait_ge(branch_ready, t + 1)
                    pool.wait_ge(x_landed[k % 4], (t - k % 4) * 4 + 16)
                    if inside(t, -4, NT):
                        pool.wait_ge(x1_stored[k % 4], (t - k % 4) * 4)
                    nc.gpsimd.tensor_tensor(x1[:, k % 4, :], branch[:, k % 2, :], x_in[:, k % 4, :],
                                            ALU.add).then_inc(x1_ready, 1)
            stepped(pool, 4, 2, 4, STEPS, step)

        @block.scalar
        def _(act):
            act.wait_ge(w_landed, 32)
            nc.scalar.activation(w_hi[:], w_raw[:], ACT.Copy).then_inc(w_hi_done, 1)

            def attention_high(t, k):
                act.wait_ge(at_ready, t + 1)
                if inside(t, -2, NT):
                    act.wait_ge(proj_ready, t - 1)
                nc.scalar.activation(at_hi[:, k % 2].rearrange("p c q -> p (c q)"), tps[:, k % 2, :],
                                     ACT.Copy).then_inc(at_hi_done, 1)
            attention_high(0, 0)

            def step(t, k):
                if inside(t, AHEAD, NT):
                    attention_high(t + 1, k + 1)
                if inside(t, -2, NT):
                    act.wait_ge(ht_ready, t - 1)
                    if inside(t, -4, NT):
                        act.wait_ge(h_copied[k % 2], (t - k % 2) * 16 - 32)
                        act.wait_ge(logits_ready, t - 3)
                    nc.scalar.activation(ht_hi[:, k % 2].rearrange("p c q -> p (c q)"), tps[:, 2 + k % 2, :],
                                         ACT.Copy).then_inc(ht_hi_done, 1)
            stepped(act, 4, 2, 4, STEPS, step)
            act.wait_ge(route, 2)
            nc.scalar.activation(logits[:], logits[:], ACT.Exp).then_inc(exp_done, 1)
            for b in range(NTB):
                act.wait_ge(cwT_turned, b + 1)
                nc.scalar.activation(cwT[:, b * NB:(b + 1) * NB], tps[0:E, b, :], ACT.Copy).then_inc(cwT_ready, 1)

        @block.vector
        def _(dve):
            dve.wait_ge(w_hi_done, 1)
            nc.vector.tensor_tensor(w_lo[:], w_raw[:], f32(w_hi[:]), ALU.subtract).then_inc(w_lo_done, 1)

            def attention_low(t, k):
                dve.wait_ge(at_hi_done, t + 1)
                nc.vector.tensor_tensor(at_lo[:, k % 2].rearrange("p c q -> p (c q)"), tps[:, k % 2, :],
                                        f32(at_hi[:, k % 2]).rearrange("p c q -> p (c q)"),
                                        ALU.subtract).then_inc(at_lo_done, 1)

            def statistics(t, which, j, src, stats):
                nc.vector.bn_stats(st[:, which, j], src).then_inc(stats, 1)

            def aggregate(t, which, j, aggr):
                nc.vector.bn_aggr(mv[:, which, j], st[:, which, j]).then_inc(aggr, 1)

            def normalise(t, which, j, src, dst, rstd_done, done):
                dve.wait_ge(rstd_done, t + 1)
                nc.vector.tensor_scalar(dst, src, mv[:, which, j, 0:1], rstd[:, which, j, 0:1],
                                        ALU.subtract, ALU.mult).then_inc(done, 1)
            attention_low(0, 0)

            def step(t, k):
                if inside(t, AHEAD, NT):
                    attention_low(t + 1, k + 1)
                if inside(t, 0, NT):
                    dve.wait_ge(proj_ready, t + 1)
                    statistics(t, 0, k % 2, prj[:, k % 2, :], stats1)
                    dve.wait_ge(stats1, t + 1)
                if inside(t, -2, NT):
                    dve.wait_ge(ht_hi_done, t - 1)
                    nc.vector.tensor_tensor(ht_lo[:, k % 2].rearrange("p c q -> p (c q)"), tps[:, 2 + k % 2, :],
                                            f32(ht_hi[:, k % 2]).rearrange("p c q -> p (c q)"),
                                            ALU.subtract).then_inc(ht_lo_done, 1)
                if inside(t, 0, NT):
                    aggregate(t, 0, k % 2, aggr1)
                if inside(t, -1, NT):
                    dve.wait_ge(x1_ready, t)
                    statistics(t - 1, 1, (k - 1) % 2, x1[:, (k - 1) % 4, :], stats2)
                    dve.wait_ge(stats2, t)
                if inside(t, -3, NT):
                    dve.wait_ge(logits_ready, t - 2)
                    nc.vector.tensor_copy(logits[:, bass.ds(t - 3, 1), :].rearrange("p a e -> p (a e)"),
                                          lg[:, (k - 3) % 2, 0:E]).then_inc(logits_copied, 1)
                if inside(t, -1, NT):
                    aggregate(t - 1, 1, (k - 1) % 2, aggr2)
                if inside(t, 0, NT):
                    if inside(t, -2, NT):
                        dve.wait_ge(x1_ready, t - 1)
                    normalise(t, 0, k % 2, prj[:, k % 2, :], branch[:, k % 2, :], rstd1, branch_ready)
                if inside(t, -1, NT):
                    if not (isinstance(t, int) and t < 3):
                        dve.wait_ge(ht_ready, t - 2)
                    normalise(t - 1, 1, (k - 1) % 2, x1[:, (k - 1) % 4, :], hn[:, (k - 1) % 2, :], rstd2, hn_ready)
            stepped(dve, 4, 2, 4, STEPS, step)

            dve.wait_ge(logits_copied, NT)
            nc.vector.tensor_reduce(top[:, :, 0], logits[:], AX_X, ALU.max).then_inc(route, 1)
            dve.wait_ge(route, 1)
            nc.vector.tensor_tensor(logits[:], logits[:], top[:].to_broadcast([P, NT, E]), ALU.subtract).then_inc(route, 1)
            dve.wait_ge(exp_done, 1)
            nc.vector.reduce_sum(total[:, :, 0], logits[:], AX_X).then_inc(route, 1)
            dve.wait_ge(route, 3)
            nc.vector.reciprocal(top[:], total[:]).then_inc(route, 1)
            dve.wait_ge(route, 4)
            dve.wait_ge(marks_set, 2)
            nc.vector.tensor_tensor(scores[:, :, 0:E], logits[:], top[:].to_broadcast([P, NT, E]), ALU.mult).then_inc(route, 1)
            dve.wait_ge(route, 5)
            for t in range(NT):
                nc.vector.max(best[:, t, :], scores[:, t, 0:E]).then_inc(route, 1)
            dve.wait_ge(route, 5 + NT)
            nc.vector.memset(best[:, :, TOPK:TOPK + 1], -1.0).then_inc(route, 1)
            nc.vector.memset(best[:, :, TOPK + 1:TOPK + 2], -2.0).then_inc(route, 1)
            dve.wait_ge(route, 7 + NT)
            for t in range(NT):
                nc.vector.match_replace(rest[:, t, :], best[:, t, :], scores[:, t, :], 0.0).then_inc(route, 1)
            dve.wait_ge(route, 7 + 2 * NT)
            nc.vector.tensor_tensor(cw[:], scores[:, :, 0:E], rest[:, :, 0:E], ALU.subtract).then_inc(cw_ready, 1)

        @block.tensor
        def _(pe):
            def turn_attention(t, k):
                pe.wait_ge(a_copied, t + 1)
                if inside(t, -2, NT):
                    pe.wait_ge(at_lo_done, t - 1)
                for c in range(KC):
                    last = nc.tensor.transpose(tps[:, k % 2, c * P:(c + 1) * P], a_in[:, k % 2, c * P:(c + 1) * P], ident[:])
                last.then_inc(at_ready, 1)
            turn_attention(0, 0)

            def step(t, k):
                if inside(t, AHEAD, NT):
                    turn_attention(t + 1, k + 1)
                if inside(t, 0, NT):
                    pe.wait_ge(at_lo_done, t + 1)
                    if isinstance(t, int) and t == 0:
                        pe.wait_ge(w_lo_done, 1)
                    if inside(t, -2, NT):
                        pe.wait_ge(branch_ready, t - 1)
                    j = k % 2
                    three_passes(nc, prj[:, j, :], lambda c: (at_hi[:, j, c], at_lo[:, j, c], w_hi[:, c, 0:D],
                                                              w_lo[:, c, 0:D]), KC).then_inc(proj_ready, 1)
                if inside(t, -2, NT):
                    pe.wait_ge(hn_ready, t - 1)
                    if not (isinstance(t, int) and t < 4):
                        pe.wait_ge(ht_lo_done, t - 3)
                    for c in range(KC):
                        last = nc.tensor.transpose(tps[:, 2 + k % 2, c * P:(c + 1) * P],
                                                   hn[:, k % 2, c * P:(c + 1) * P], ident[:])
                    last.then_inc(ht_ready, 1)
                if inside(t, -3, NT):
                    pe.wait_ge(ht_lo_done, t - 2)
                    if not (isinstance(t, int) and t < 5):
                        pe.wait_ge(logits_copied, t - 4)
                    j = (k - 3) % 2
                    three_passes(nc, lg[:, j, 0:E], lambda c: (ht_hi[:, j, c], ht_lo[:, j, c], w_hi[:, c, D:D + E],
                                                               w_lo[:, c, D:D + E]), KC).then_inc(logits_ready, 1)
            stepped(pe, 4, 2, 4, STEPS, step)
            pe.wait_ge(cw_ready, 1)
            for b in range(NTB):
                for q in range(NTB):
                    last = nc.tensor.transpose(tps[0:E, b, q * P:(q + 1) * P], cw[:, b * NTB + q, :], ident[:])
                last.then_inc(cwT_turned, 1)


def stage_experts(nc, w_dram, cw_dram, x1_dram, out_dram, rows, ln_consts, h_hi, h_lo):
    with ExitStack() as ctx:
        sb = lambda n, s, d: ctx.enter_context(nc.sbuf_tensor(n, s, d))
        pb = lambda n, s: ctx.enter_context(nc.psum_tensor(n, s, F32))
        sem = lambda n: ctx.enter_context(nc.semaphore(n))

        GATE, UP, DOWN = 0, 1, 2
        SPLITS = 6
        SPLIT_AT = {2: [0], 3: [1], 4: [2], 5: [3], 6: [4, 5]}
        w_raw = sb("m_w_raw", [P, 2, 3, NB], F32)
        w_hi = [sb(f"m_w_hi{i}", [P, 2, 3, NB], F32R) for i in range(2)]
        w_lo = [sb(f"m_w_lo{i}", [P, 2, 3, NB], F32R) for i in range(2)]
        cwb = sb("cwb", [P, 2, 2, NB], F32)
        gate = sb("m_gate", [P, 2, NB], F32)
        gated = sb("m_gated", [P, 2, NB], F32)
        act_f = sb("m_act", [P, 2, NB], F32)
        act_hi = sb("m_act_hi", [P, 2, 2, NB], F32R)
        act_lo = sb("m_act_lo", [P, 2, 2, NB], F32R)
        x1 = sb("m_x1", [P, 4, D], F32)
        fin = sb("m_fin", [P, 2, D], F32)
        st = sb("m_st", [P, NTB, 6], F32)
        mv = sb("m_mv", [P, NTB, 2], F32)
        rstd = sb("m_rstd", [P, NTB, 1], F32)
        veps = sb("m_veps", [P, NTB, 1], F32)
        gp = pb("m_gp", [P, 2, NB])
        up = pb("m_up", [P, 2, NB])
        yp = pb("m_yp", [P, NTB, NB])

        w_landed, w_hi_done, w_split = sem("m_w_landed"), sem("m_w_hi_done"), sem("m_w_split")
        cw_landed = [sem(f"m_cw_landed{i}") for i in range(2)]
        g_ready, u_ready, gate_done, gated_done = sem("m_g_ready"), sem("m_u_ready"), sem("m_gate_done"), sem("m_gated_done")
        act_done, act_hi_done, act_lo_done = sem("m_act_done"), sem("m_act_hi_done"), sem("m_act_lo_done")
        y_cleared, y_ready, y_added = sem("m_y_cleared"), sem("m_y_ready"), sem("m_y_added")
        stats, aggr, rstd_done, fin_ready, out_ready = (sem("m_stats"), sem("m_aggr"), sem("m_rstd_done"),
                                                        sem("m_fin_ready"), sem("m_out_ready"))
        veps_done = sem("m_veps_done")
        x1_landed = [sem(f"m_x1_landed{i}") for i in range(4)]
        out_stored = [sem(f"m_out_stored{i}") for i in range(4)]
        block = ctx.enter_context(nc.Block())

        UNITS = PAIRS * NTB
        LAST_PAIR = UNITS - NTB

        def units(eng, step):
            stepped(eng, NTB, (UNITS - 2 * NTB) // (2 * NTB), 2 * NTB, UNITS, step)

        def from_unit(u, least):
            return not isinstance(u, int) or u >= least

        @block.sync
        def _(sp):
            w_quarters = w_dram.rearrange("p a (q n) -> p (a q) n", q=NTB)
            sp.dma_start(w_raw[:].rearrange("p c m n -> p (c m n)"), w_dram[:, 0, :]).then_inc(w_landed, 16)
            for s in range(4):
                sp.dma_start(x1[:, s, :], x1_dram[s]).then_inc(x1_landed[s], 16)

            def step(u, k):
                if from_unit(u, 2):
                    sp.wait_ge(act_done, u * 2 - 2)
                tb = k % NTB
                for c in range(2):
                    g0 = (u - tb) * (2 * P // GROUP // NTB) + c * (P // GROUP)
                    sp.dma_start(cwb[:, k % 2, c, :],
                                 cw_dram[bass.ds(g0, P // GROUP), tb * NB:(tb + 1) * NB].unsqueeze(1)
                                 .to_broadcast([P // GROUP, GROUP, NB])).then_inc(cw_landed[k % 2], 16)
                if tb == 0 and not (isinstance(u, int) and u >= LAST_PAIR):
                    sp.wait_ge(w_split, u * 3 + 2 * SPLITS)
                    sp.dma_start(w_raw[:].rearrange("p c m n -> p (c m n)"),
                                 w_quarters[:, bass.ds(u + NTB, NTB), :].rearrange("p a n -> p (a n)")).then_inc(w_landed, 16)
            units(sp, step)
            for t in range(NT):
                sp.wait_ge(out_ready, t + 1)
                sp.dma_start(out_dram[t], x1[:, t % 4, :]).then_inc(out_stored[t % 4], 16)
                if t >= 2 and t + 2 < NT:
                    sp.wait_ge(out_stored[(t - 2) % 4], 16 * ((t - 2) // 4 + 1))
                    sp.dma_start(x1[:, (t + 2) % 4, :], x1_dram[t + 2]).then_inc(x1_landed[(t + 2) % 4], 16)
            for s in range(4):
                sp.wait_ge(out_stored[s], 16 * NT // 4)

        @block.gpsimd
        def _(pool):
            pool.wait_ge(w_split, 2 * SPLITS)

            def split_piece(u0, k, i):
                c, m = i // 3, i % 3
                dst = (k // NTB + 1) % 2
                if i == 0:
                    pool.wait_ge(w_landed, u0 * 4 + 32)
                    if from_unit(u0, 1):
                        pool.wait_ge(y_ready, u0 * 4)
                nc.gpsimd.tensor_copy(w_hi[dst][:, c, m, :], w_raw[:, c, m, :]).then_inc(w_hi_done, 2)
                pool.wait_ge(w_hi_done, u0 * 3 + (2 * SPLITS + 2 * (i + 1)))
                nc.gpsimd.tensor_tensor(w_lo[dst][:, c, m, :], w_raw[:, c, m, :], f32(w_hi[dst][:, c, m, :]),
                                        ALU.subtract).then_inc(w_split, 2)

            def step(u, k):
                for c in range(2):
                    n = u * 2 + c
                    if c == 0:
                        pool.wait_ge(cw_landed[k % 2], (u - k % 2) * 16 + 32)
                    pool.wait_ge(gated_done, n + 1)
                    if from_unit(u, 1):
                        pool.wait_ge(act_lo_done, n - 1)
                    nc.gpsimd.tensor_tensor(act_f[:, c, :], gated[:, c, :], cwb[:, k % 2, c, :],
                                            ALU.mult).then_inc(act_done, 1)
                    if not (isinstance(u, int) and u >= LAST_PAIR):
                        for i in SPLIT_AT.get(2 * (k % NTB) + c, ()):
                            split_piece(u - k % NTB, k, i)
                if isinstance(u, int) and u > LAST_PAIR:
                    finish(u - LAST_PAIR - 1)

            def finish(tb):
                pool.wait_ge(aggr, NTB * (tb + 1))
                if tb:
                    pool.wait_ge(rstd_done, tb)
                nc.gpsimd.tensor_scalar(veps[:], mv[:, :, 1:2], EPS, None, ALU.add).then_inc(veps_done, 1)
                pool.wait_ge(veps_done, tb + 1)
                nc.gpsimd.tensor_tensor(rstd[:], veps[:], ln_consts[:, 1:2].to_broadcast([P, NTB]).unsqueeze(2),
                                        ALU.pow).then_inc(rstd_done, 1)
                for t in range(NTB * tb, NTB * (tb + 1)):
                    pool.wait_ge(fin_ready, t + 1)
                    pool.wait_ge(x1_landed[t % 4], 16 * (t // 4 + 1))
                    nc.gpsimd.tensor_tensor(x1[:, t % 4, :], x1[:, t % 4, :], fin[:, t % 2, :],
                                            ALU.add).then_inc(out_ready, 1)
            units(pool, step)
            finish(NTB - 1)

        @block.scalar
        def _(act):
            act.wait_ge(w_landed, 16)
            for i in range(SPLITS):
                nc.scalar.activation(w_hi[0][:, i // 3, i % 3, :], w_raw[:, i // 3, i % 3, :],
                                     ACT.Copy).then_inc(w_hi_done, 2)

            def step(u, k):
                for c in range(2):
                    n = u * 2 + c
                    act.wait_ge(g_ready, n + 1)
                    if from_unit(u, 1):
                        act.wait_ge(gated_done, n - 1)
                    nc.scalar.activation(gate[:, c, :], gp[:, c, :], ACT.Silu).then_inc(gate_done, 1)
                    act.wait_ge(act_done, n + 1)
                    if c == 0 and from_unit(u, 2):
                        act.wait_ge(y_ready, u * 4 - 4)
                    nc.scalar.activation(act_hi[:, k % 2, c, :], act_f[:, c, :], ACT.Copy).then_inc(act_hi_done, 1)
            units(act, step)

        @block.vector
        def _(dve):
            nc.vector.memset(rows[:], 0.0).then_inc(y_cleared, 1)
            for i in range(SPLITS):
                dve.wait_ge(w_hi_done, 2 * (i + 1))
                nc.vector.tensor_tensor(w_lo[0][:, i // 3, i % 3, :], w_raw[:, i // 3, i % 3, :],
                                        f32(w_hi[0][:, i // 3, i % 3, :]), ALU.subtract).then_inc(w_split, 2)
            dve.wait_ge(y_cleared, 1)

            def add_up(u, tb):
                for s in range(NTB):
                    dve.wait_ge(y_ready, u * 4 + (s + 1))
                    t = NTB * tb + s
                    nc.vector.tensor_tensor(rows[:, t, :], yp[:, s, :], rows[:, t, :], ALU.add).then_inc(y_added, 1)

            def finish(tb):
                tiles = range(NTB * tb, NTB * (tb + 1))
                for t in tiles:
                    dve.wait_ge(y_added, 4 * LAST_PAIR + t + 1)
                    nc.vector.bn_stats(st[:, t % NTB], rows[:, t, :]).then_inc(stats, 1)
                for t in tiles:
                    dve.wait_ge(stats, t + 1)
                    nc.vector.bn_aggr(mv[:, t % NTB], st[:, t % NTB]).then_inc(aggr, 1)
                dve.wait_ge(rstd_done, tb + 1)
                for t in tiles:
                    if t >= 2:
                        dve.wait_ge(out_ready, t - 1)
                    j = t % NTB
                    nc.vector.tensor_scalar(fin[:, t % 2, :], rows[:, t, :], mv[:, j, 0:1], rstd[:, j, 0:1],
                                            ALU.subtract, ALU.mult).then_inc(fin_ready, 1)

            def step(u, k):
                for c in range(2):
                    n = u * 2 + c
                    dve.wait_ge(gate_done, n + 1)
                    dve.wait_ge(u_ready, n + 1)
                    if from_unit(u, 1):
                        dve.wait_ge(act_done, n - 1)
                    nc.vector.tensor_tensor(gated[:, c, :], up[:, c, :], gate[:, c, :], ALU.mult).then_inc(gated_done, 1)
                    dve.wait_ge(act_hi_done, n + 1)
                    nc.vector.tensor_tensor(act_lo[:, k % 2, c, :], act_f[:, c, :], f32(act_hi[:, k % 2, c, :]),
                                            ALU.subtract).then_inc(act_lo_done, 1)
                    if c == 0 and from_unit(u, 1):
                        add_up(u - 1, (k - 1) % NTB)
                if isinstance(u, int) and u > LAST_PAIR:
                    finish(u - LAST_PAIR - 1)
            units(dve, step)
            add_up(UNITS - 1, NTB - 1)
            finish(NTB - 1)

        @block.tensor
        def _(pe):
            def hidden(u, k, c):
                w, tb = (k // NTB) % 2, k % NTB
                n = u * 2 + c
                if c == 0 and tb == 0:
                    pe.wait_ge(w_split, u * 3 + 2 * SPLITS)
                if from_unit(u, 1):
                    pe.wait_ge(gated_done, n - 1)
                toks = slice(tb * NB, (tb + 1) * NB)
                for m, bank, ready in ((GATE, gp, g_ready), (UP, up, u_ready)):
                    three_passes(nc, bank[:, c, :],
                                 lambda kc: (w_hi[w][:, c, m, kc * P:(kc + 1) * P], w_lo[w][:, c, m, kc * P:(kc + 1) * P],
                                             h_hi[:, kc, toks], h_lo[:, kc, toks]), KC).then_inc(ready, 1)

            def down(u, k):
                w = (k // NTB) % 2
                pe.wait_ge(act_lo_done, u * 2 + 2)
                for s in range(NTB):
                    if from_unit(u, 1):
                        pe.wait_ge(y_added, u * 4 + (s - 3))
                    tile = slice(s * P, (s + 1) * P)
                    three_passes(nc, yp[:, s, :],
                                 lambda c: (act_hi[:, k % 2, c, tile], act_lo[:, k % 2, c, tile],
                                            w_hi[w][:, c, DOWN, :], w_lo[w][:, c, DOWN, :]), 2).then_inc(y_ready, 1)

            def step(u, k):
                hidden(u, k, 0)
                if from_unit(u, 1):
                    down(u - 1, k - 1)
                hidden(u, k, 1)
            units(pe, step)
            down(UNITS - 1, UNITS - 1)


def build_layer(nc, x, wqkv, wproj, wgate, wexp, out):
    qk_dram = nc.dram_tensor("qk_parts", [4, D, T], F32, kind="Internal").ap()
    x1_dram = nc.dram_tensor("x1_tiles", [NT, P, D], F32, kind="Internal").ap()
    cw_dram = nc.dram_tensor("routing", [NGROUPS, T], F32, kind="Internal").ap()
    x_tiles = x.rearrange("(n p) d -> n p d", p=P)
    out_tiles = out.rearrange("(n p) d -> n p d", p=P)
    with ExitStack() as ctx:
        rows = ctx.enter_context(nc.sbuf_tensor("rows", [P, NT, D], F32))
        ident = ctx.enter_context(nc.sbuf_tensor("ident", [P, P], F32))
        ln_consts = ctx.enter_context(nc.sbuf_tensor("ln_consts", [P, 2], F32))
        with ExitStack() as early:
            v_all = early.enter_context(nc.sbuf_tensor("v_all", [P, H, NT, VW], F32R))
            stage_embed_qkv(nc, x_tiles, wqkv, rows, v_all, ident, ln_consts, qk_dram)
            stage_attention(nc, rows, v_all, ident, qk_dram)
        h_hi = ctx.enter_context(nc.sbuf_tensor("h_hi", [P, KC, T], F32R))
        h_lo = ctx.enter_context(nc.sbuf_tensor("h_lo", [P, KC, T], F32R))
        stage_project_route(nc, x_tiles, wproj, wgate, rows, ident, ln_consts, h_hi, h_lo, x1_dram, cw_dram)
        stage_experts(nc, wexp, cw_dram, x1_dram, out_tiles, rows, ln_consts, h_hi, h_lo)


def kernel(L0_attn_x, L0_attn_W_qkv, L0_attn_W_proj, L0_ffn_gate_w, L0_ffn_w_gate, L0_ffn_w_up, L0_ffn_w_down):
    import concourse.bacc as bacc
    from concourse.bass_utils import run_bass_kernel_spmd

    def contraction_first(w):
        return np.ascontiguousarray(np.asarray(w).T.reshape(KC, P, -1).transpose(1, 0, 2))

    def hidden_chunks(w):
        w = np.asarray(w).reshape(CHUNKS, P, KC, P)
        return w.transpose(3, 0, 2, 1).reshape(P, CHUNKS, NB)

    down = np.asarray(L0_ffn_w_down).transpose(0, 2, 1).reshape(CHUNKS, P, D).transpose(1, 0, 2)
    experts = np.stack([hidden_chunks(L0_ffn_w_gate), hidden_chunks(L0_ffn_w_up), down], axis=2)
    arrays = {
        "x": np.ascontiguousarray(np.asarray(L0_attn_x).reshape(T, D)),
        "wqkv": contraction_first(L0_attn_W_qkv),
        "wproj": contraction_first(L0_attn_W_proj),
        "wgate": contraction_first(L0_ffn_gate_w),
        "wexp": np.ascontiguousarray(experts.reshape(P, PAIRS, 2 * 3 * NB)),
    }
    nc = bacc.Bacc("TRN2", target_bir_lowering=False, num_devices=1)
    aps = {n: nc.dram_tensor(n, a.shape, mybir.dt.from_np(a.dtype), kind="ExternalInput").ap() for n, a in arrays.items()}
    out = nc.dram_tensor("out", (T, D), F32, kind="ExternalOutput").ap()
    build_layer(nc, out=out, **aps)
    r = run_bass_kernel_spmd(nc, [arrays], core_ids=[0])
    return r.results[0]["out"].reshape(np.asarray(L0_attn_x).shape)
```

```python
from contextlib import ExitStack

import numpy as np

import concourse.bass as bass
from concourse import mybir

F32 = mybir.dt.float32
F32R = mybir.dt.float32r
ALU = mybir.AluOpType
ACT = mybir.ActivationFunctionType
AX_X = mybir.AxisListType.X

P = 128
T, D, H = 2048, 512, 16
HD = D // H
E, F, TOPK = 16, 352, 6
KC = D // P
NT = T // P
NB = 512
NTB = T // NB
EPS = 1e-5
SCALE = float(1.0 / np.sqrt(D))
MASKED = -1e30
LOWEST = -3e38
VW = 2 * HD + 1
PIECE = 256
VPIECES = D // PIECE
QK_PIECES = 2 * D // PIECE
PIECE_UNITS = PIECE // P * NTB
CHUNKS = E * F // P
PAIRS = CHUNKS // 2
SPLITS = 6
GROUP = 32
NGROUPS = E * F // GROUP
GPE = F // GROUP
assert F % GROUP == 0 and E * F % (2 * P) == 0 and D == NB


def stepped(eng, first, loops, unroll, total, step):
    for t in range(first):
        step(t, t)
    with eng.Fori(0, loops) as i:
        for k in range(unroll):
            step(i * unroll + (first + k), first + k)
    for t in range(first + loops * unroll, total):
        step(t, t)


def inside(t, offset, total):
    return not isinstance(t, int) or 0 <= t + offset < total


def f32(ap):
    return ap.bitcast(F32)


def one(ap, t):
    return ap[bass.ds(t, 1)].rearrange("a p d -> (a p) d")


def three_passes(nc, out, pairs, chunks, part=None):
    for c in part or range(chunks):
        a_hi, a_lo, b_hi, b_lo = pairs(c)
        for n, (a, b) in enumerate(((a_hi, b_hi), (a_hi, b_lo), (a_lo, b_hi))):
            last = nc.tensor.matmul(out, a, b, start=c == n == 0, stop=c == chunks - 1 and n == 2)
    return last


def stage_embed_qkv(nc, x_dram, wqkv_dram, rows, v_all, ident, ln_consts, qk_dram):
    with ExitStack() as ctx:
        sb = lambda n, s, d: ctx.enter_context(nc.sbuf_tensor(n, s, d))
        pb = lambda n, s: ctx.enter_context(nc.psum_tensor(n, s, F32))
        sem = lambda n: ctx.enter_context(nc.semaphore(n))

        w_raw = rows[:, 0:12, :].rearrange("p a b -> p (a b)").rearrange("p (k n) -> p k n", k=KC)
        x_in = rows[:, 12:16, :]
        xn = sb("xn", [P, 2, D], F32)
        st = sb("e_st", [P, 2, 6], F32)
        mv = sb("e_mv", [P, 2, 2], F32)
        rstd = sb("e_rstd", [P, 2, 1], F32)
        veps = sb("e_veps", [P, 1], F32)
        xt_hi = sb("xt_hi", [P, 2, KC, P], F32R)
        xt_lo = sb("xt_lo", [P, 2, KC, P], F32R)
        xT_hi = sb("xT_hi", [P, KC, T], F32R)
        xT_lo = sb("xT_lo", [P, KC, T], F32R)
        w_hi = sb("e_w_hi", [P, 3, KC, PIECE], F32R)
        w_lo = sb("e_w_lo", [P, 3, KC, PIECE], F32R)
        qk_hi = sb("qk_hi", [P, 2, NB], F32R)
        qk_lo = sb("qk_lo", [P, 2, NB], F32R)
        tp = pb("e_tp", [P, 2, KC, P])
        vp = pb("e_vp", [P, 2, NB])
        qp = pb("e_qp", [P, 2, NB])

        ident_made, ones_set = sem("e_ident_made"), sem("e_ones_set")
        x_landed = [sem(f"e_x_landed{i}") for i in range(4)]
        wv_landed, wqk_landed = [sem(f"e_wv_landed{v}") for v in range(VPIECES)], sem("e_wqk_landed")
        stats, aggr, rstd_done = sem("e_stats"), sem("e_aggr"), sem("e_rstd_done")
        veps_done = sem("e_veps_done")
        xn_ready, tp_ready = sem("e_xn_ready"), sem("e_tp_ready")
        xt_hi_done, xt_lo_done, xT_copied = sem("e_xt_hi_done"), sem("e_xt_lo_done"), [sem(f"e_xT_copied{i}") for i in range(2)]
        v_ready, v_hi_done, v_lo_done = sem("e_v_ready"), sem("e_v_hi_done"), sem("e_v_lo_done")
        wv_hi_done, wv_lo_done = sem("e_wv_hi_done"), sem("e_wv_lo_done")
        wqk_hi_done, wqk_lo_done = sem("e_wqk_hi_done"), sem("e_wqk_lo_done")
        unit_ready, unit_hi_done, unit_lo_done = sem("e_unit_ready"), sem("e_unit_hi"), sem("e_unit_lo")
        parked = [sem(f"e_parked{i}") for i in range(2)]
        block = ctx.enter_context(nc.Block())

        def slot_of(q):
            return (VPIECES + q) % 3

        def qk_units(eng, unit):
            for q in range(QK_PIECES):
                for f in range(PIECE // P):
                    base = (q * (PIECE // P) + f) * NTB
                    if base == 0:
                        for n in range(NTB):
                            unit(n, n % 2, q, f, n)
                    else:
                        with eng.Fori(0, NTB // 2) as i:
                            for k in range(2):
                                unit(i * 2 + (base + k), k, q, f, i * 2 + k)

        @block.sync
        def _(sp):
            for s in range(4):
                sp.dma_start(x_in[:, s, :], x_dram[s]).then_inc(x_landed[s], 16)
                if s < VPIECES:
                    cols = slice(2 * D + s * PIECE, 2 * D + (s + 1) * PIECE)
                    sp.dma_start(w_raw[:, :, cols], wqkv_dram[:, :, cols]).then_inc(wv_landed[s], 16)

            def tile(t, k):
                if inside(t, 4, NT):
                    sp.wait_ge(xn_ready, t + 1)
                    sp.dma_start(x_in[:, k % 4, :], one(x_dram, t + 4)).then_inc(x_landed[k % 4], 16)
                sp.wait_ge(xt_lo_done, t + 1)
                toks = bass.ds(t * P, P)
                sp.dma_start(f32(xT_hi[:, :, toks]), f32(xt_hi[:, k % 2])).then_inc(xT_copied[k % 2], 16)
                sp.dma_start(f32(xT_lo[:, :, toks]), f32(xt_lo[:, k % 2])).then_inc(xT_copied[k % 2], 16)
                if isinstance(t, int) and t == 3:
                    sp.dma_start(w_raw[:, :, 0:2 * D], wqkv_dram[:, :, 0:2 * D]).then_inc(wqk_landed, 16)
            stepped(sp, 4, 2, 4, NT, tile)

            def park(n, k, q, f, tb):
                which, row = q // 2, (q % 2) * PIECE + f * P
                sp.wait_ge(unit_lo_done, n + 1)
                for part, src in enumerate((qk_hi, qk_lo)):
                    sp.dma_start(qk_dram[2 * which + part, row:row + P, bass.ds(tb * NB, NB)],
                                 f32(src[:, k, :])).then_inc(parked[k], 16)
            qk_units(sp, park)
            for k in range(2):
                sp.wait_ge(parked[k], 16 * QK_PIECES * PIECE_UNITS)

        @block.gpsimd
        def _(pool):
            nc.gpsimd.memset(ident[:], 0.0).then_inc(ident_made, 1)
            pool.wait_ge(ident_made, 1)
            nc.gpsimd.affine_select(out=ident[:], in_=ident[:], compare_op=ALU.not_equal, fill=1.0, base=0,
                                    pattern=[[-1, P]], channel_multiplier=1).then_inc(ident_made, 1)
            nc.gpsimd.memset(ln_consts[:, 0:1], EPS).then_inc(ident_made, 1)
            nc.gpsimd.memset(ln_consts[:, 1:2], -0.5).then_inc(ident_made, 1)
            pool.wait_ge(ident_made, 4)
            nc.gpsimd.memset(f32(v_all[:, :, :, 2 * HD:VW]), 1.0).then_inc(ones_set, 1)

            def inverse_deviation(t, k):
                pool.wait_ge(aggr, t + 1)
                if inside(t, -1, NT):
                    pool.wait_ge(rstd_done, t)
                nc.gpsimd.tensor_tensor(veps[:], mv[:, k % 2, 1:2], ln_consts[:, 0:1], ALU.add).then_inc(veps_done, 1)
                pool.wait_ge(veps_done, t + 1)
                nc.gpsimd.tensor_tensor(rstd[:, k % 2], veps[:], ln_consts[:, 1:2], ALU.pow).then_inc(rstd_done, 1)

            def split(q, chunk):
                done = wqk_hi_count[0] = wqk_hi_count[0] + 1
                raw = w_raw[:, chunk, q * PIECE:(q + 1) * PIECE]
                nc.gpsimd.tensor_copy(w_hi[:, slot_of(q), chunk], raw).then_inc(wqk_hi_done, 1)
                pool.wait_ge(wqk_hi_done, done)
                nc.gpsimd.tensor_tensor(w_lo[:, slot_of(q), chunk], raw, f32(w_hi[:, slot_of(q), chunk]),
                                        ALU.subtract).then_inc(wqk_lo_done, 1)
            wqk_hi_count = [0]

            def step(t, k):
                inverse_deviation(t, k)
                if isinstance(t, int) and t >= NT - KC:
                    if t == NT - KC:
                        pool.wait_ge(wqk_landed, 16)
                    split(0, slice(t - (NT - KC), t - (NT - KC) + 1))
            stepped(pool, 4, 2, 4, NT, step)

            for q in range(1, QK_PIECES):
                if 1 <= q <= VPIECES:
                    pool.wait_ge(v_ready, NT)
                if q > VPIECES:
                    pool.wait_ge(unit_ready, (q - 2) * PIECE_UNITS)
                split(q, slice(0, KC))

        @block.scalar
        def _(act):
            for v in range(VPIECES):
                act.wait_ge(wv_landed[v], 16)
                nc.scalar.activation(w_hi[:, v], w_raw[:, :, 2 * D + v * PIECE:2 * D + (v + 1) * PIECE],
                                     ACT.Copy).then_inc(wv_hi_done, 1)
            act.wait_ge(ones_set, 1)

            def high_parts(t, k):
                if inside(t, 0, NT):
                    act.wait_ge(tp_ready, t + 1)
                    if inside(t, -2, NT):
                        act.wait_ge(xT_copied[k % 2], (t - k % 2) * 16)
                        act.wait_ge(v_ready, t - 1)
                    nc.scalar.activation(xt_hi[:, k % 2], tp[:, k % 2], ACT.Copy).then_inc(xt_hi_done, 1)
                if inside(t, -1, NT):
                    act.wait_ge(v_ready, t)
                    nc.scalar.activation(v_all[:, :, bass.ds(t - 1, 1), 0:HD].rearrange("p h a c -> p (h a) c"),
                                         vp[:, (k - 1) % 2, :].rearrange("p (h c) -> p h c", h=H),
                                         ACT.Copy).then_inc(v_hi_done, 1)
            stepped(act, 4, 2, 4, NT + 1, high_parts)

            def unit_high(n, k, q, f, tb):
                act.wait_ge(unit_ready, n + 1)
                if not isinstance(n, int) or n >= 2:
                    act.wait_ge(parked[k], (n - k) * 16)
                nc.scalar.activation(qk_hi[:, k, :], qp[:, k, :], ACT.Copy).then_inc(unit_hi_done, 1)
            qk_units(act, unit_high)

        @block.vector
        def _(dve):
            def statistics(t, k):
                s, j = k % 4, k % 2
                dve.wait_ge(x_landed[s], (t - s) * 4 + 16)
                nc.vector.bn_stats(st[:, j], x_in[:, s, :]).then_inc(stats, 1)

            def aggregate(t, k):
                nc.vector.bn_aggr(mv[:, k % 2], st[:, k % 2]).then_inc(aggr, 1)

            def normalise(t, k):
                dve.wait_ge(rstd_done, t + 1)
                if inside(t, -2, NT):
                    dve.wait_ge(tp_ready, t - 1)
                nc.vector.tensor_scalar(xn[:, k % 2], x_in[:, k % 4, :], mv[:, k % 2, 0:1], rstd[:, k % 2, 0:1],
                                        ALU.subtract, ALU.mult).then_inc(xn_ready, 1)

            def low_parts(t, k):
                if inside(t, 2, NT):
                    statistics(t + 2, k + 2)
                    dve.wait_ge(stats, t + 3)
                if inside(t, 1, NT):
                    normalise(t + 1, k + 1)
                if inside(t, 2, NT):
                    aggregate(t + 2, k + 2)
                if inside(t, 0, NT):
                    dve.wait_ge(xt_hi_done, t + 1)
                    nc.vector.tensor_tensor(xt_lo[:, k % 2], tp[:, k % 2], f32(xt_hi[:, k % 2]),
                                            ALU.subtract).then_inc(xt_lo_done, 1)
                if inside(t, -1, NT):
                    dve.wait_ge(v_hi_done, t)
                    v_tile = v_all[:, :, bass.ds(t - 1, 1), :].rearrange("p h a c -> p (h a) c")
                    nc.vector.tensor_tensor(v_tile[:, :, HD:2 * HD],
                                            vp[:, (k - 1) % 2, :].rearrange("p (h c) -> p h c", h=H),
                                            f32(v_tile[:, :, 0:HD]), ALU.subtract).then_inc(v_lo_done, 1)
            for t in range(2):
                statistics(t, t)
                dve.wait_ge(stats, t + 1)
                aggregate(t, t)
            normalise(0, 0)
            for v in range(VPIECES):
                dve.wait_ge(wv_hi_done, v + 1)
                nc.vector.tensor_tensor(w_lo[:, v], w_raw[:, :, 2 * D + v * PIECE:2 * D + (v + 1) * PIECE],
                                        f32(w_hi[:, v]), ALU.subtract).then_inc(wv_lo_done, 1)
            stepped(dve, 4, 2, 4, NT + 1, low_parts)

            def unit_low(n, k, q, f, tb):
                dve.wait_ge(unit_hi_done, n + 1)
                nc.vector.tensor_tensor(qk_lo[:, k, :], qp[:, k, :], f32(qk_hi[:, k, :]),
                                        ALU.subtract).then_inc(unit_lo_done, 1)
            qk_units(dve, unit_low)

        @block.tensor
        def _(pe):
            pe.wait_ge(ident_made, 2)

            def transpose_tile(t, k):
                pe.wait_ge(xn_ready, t + 1)
                if inside(t, -2, NT):
                    pe.wait_ge(xt_lo_done, t - 1)
                for c in range(KC):
                    last = nc.tensor.transpose(tp[:, k % 2, c, :], xn[:, k % 2, c * P:(c + 1) * P], ident[:])
                last.then_inc(tp_ready, 1)

            def values(t, k):
                if inside(t, 1, NT):
                    transpose_tile(t + 1, k + 1)
                pe.wait_ge(xt_lo_done, t + 1)
                if isinstance(t, int) and t == 0:
                    pe.wait_ge(wv_lo_done, VPIECES)
                if inside(t, -2, NT):
                    pe.wait_ge(v_lo_done, t - 1)
                for v in range(VPIECES):
                    last = three_passes(nc, vp[:, k % 2, v * PIECE:(v + 1) * PIECE],
                                        lambda c: (xt_hi[:, k % 2, c], xt_lo[:, k % 2, c], w_hi[:, v, c], w_lo[:, v, c]), KC)
                last.then_inc(v_ready, 1)
            transpose_tile(0, 0)
            stepped(pe, 4, 2, 4, NT, values)

            def unit(n, k, q, f, tb):
                if isinstance(n, int) and n == 0:
                    for slot in range(2):
                        pe.wait_ge(xT_copied[slot], 32 * NT // 2)
                pe.wait_ge(wqk_lo_done, KC + q)
                if not isinstance(n, int) or n >= 2:
                    pe.wait_ge(unit_lo_done, n - 1)
                cols, toks = slice(f * P, (f + 1) * P), bass.ds(tb * NB, NB)
                three_passes(nc, qp[:, k, :],
                             lambda c: (w_hi[:, slot_of(q), c, cols], w_lo[:, slot_of(q), c, cols],
                                        xT_hi[:, c, toks], xT_lo[:, c, toks]), KC).then_inc(unit_ready, 1)
            qk_units(pe, unit)


S_TILES = [(j, kp, 2 * P * max(0, kp - 2 * j)) for j in range(NTB) for kp in range(2 * j + 2)]
NS = len(S_TILES)
J_FIRST = [next(t for t, s in enumerate(S_TILES) if s[0] == j) for j in range(NTB)]
J_LAST = [max(t for t, s in enumerate(S_TILES) if s[0] == j) for j in range(NTB)]
LAG = 4
RING = 5
PIECES = [(qb, kb) for qb in range(NT) for kb in range(qb // 4 + 1)]
NPC = len(PIECES)
QA = 12
NPC_A = sum(1 for qb, _ in PIECES if qb < QA)
PIECES_AT = [0, 0, 0, 0, 3, 2, 3, 2, 3, 2, 2, 2, 3, 4, 3, 2, 3, 2, 2, 2] 
PIECES_AT_A = next(t for t in range(NS) if sum(PIECES_AT[:t]) >= NPC_A)
assert sum(PIECES_AT) == NPC and NS == len(PIECES_AT) and NS % RING == 0
SHARED_AT = {3: 'max_b', 5: 3, 9: 0, 13: 1, 15: 'max_a', 17: 2} 
KQ_LOADS = 6
FW = HD + 2
CONSTS = 11
HI_DVE = {1, 2, 3, 9, 15} 
PE_ORDER = 'SpHpLr' 
DVE_ORDER = 'phpplr' 
ACT_ORDER = 'EHC' 
LO_POOL = {0, 2, 3, 4, 5, 6, 7, 9, 10, 11, 12, 13, 14, 16} 


def count_before(which, t):
    return sum(1 for s in which if s < t)


def stage_attention(nc, rows, v_all, ident, qk_dram):
    with ExitStack() as ctx:
        sb = lambda n, s, d: ctx.enter_context(nc.sbuf_tensor(n, s, d))
        pb = lambda n, s: ctx.enter_context(nc.psum_tensor(n, s, F32))
        sem = lambda n: ctx.enter_context(nc.semaphore(n))

        K_ROWS, ROW_MAX = 3 * HD, 3 * HD
        ks = [sb(f"k_stack{p}", [P, T], F32R) for p in range(2)]
        qs = [sb(f"q_stack{p}", [P, T], F32R) for p in range(2)]
        vs = [sb(f"v_head{p}", [P, NT, VW], F32R) for p in range(2)]
        prob = sb("prob", [P, RING, 2, NB], F32)
        prob_hi = sb("prob_hi", [P, RING, 2, NB], F32R)
        prob_lo = sb("prob_lo", [P, RING, 2, NB], F32R)
        o_sb = sb("o_sb", [VW, 2, NB], F32)
        fold = sb("fold", [VW, HD + 2], F32)
        neg_ident = sb("neg_ident", [P, P], F32)
        ident_r = sb("ident_r", [P, P], F32R)
        mask_q = sb("mask_q", [P, P], F32R)
        mask_k = sb("mask_k", [P, 2 * P], F32R)
        mask_f = sb("mask_f", [P, 2 * P], F32)
        part_max = sb("part_max", [P, NT, NTB], F32)
        row_max = sb("row_max", [P, NT], F32)
        max_rows = sb("max_rows", [QA, P], F32R)
        max_rows_b = sb("max_rows_b", [NT - QA, P], F32R)
        recip = sb("recip", [P, NTB, 1], F32)

        mp = pb("a_mp", [P, 2, NB])
        sp_ = pb("a_sp", [P, 2, 2, NB])
        op = pb("a_op", [P, NB])
        shared = pb("a_shared", [P, NB])

        consts, dve_consts = sem("a_consts"), sem("a_dve_consts")
        kq_landed = [sem(f"a_kq_landed{p}") for p in range(2)]
        v_landed = [sem(f"a_v_landed{p}") for p in range(2)]
        max_a_landed = [sem(f"a_max_a_landed{p}") for p in range(2)]
        max_b_landed = [sem(f"a_max_b_landed{p}") for p in range(2)]
        piece_ready, piece_done = sem("a_piece_ready"), sem("a_piece_done")
        row_max_a, row_max_b = sem("a_row_max_a"), sem("a_row_max_b")
        max_a_out, max_b_out = sem("a_max_a_out"), sem("a_max_b_out")
        scores_ready, prob_ready = sem("a_scores_ready"), sem("a_prob_ready")
        hi_act, hi_dve = sem("a_hi_act"), sem("a_hi_dve")
        lo_dve, lo_pool = sem("a_lo_dve"), sem("a_lo_pool")
        pv_done, out_copied = sem("a_pv_done"), sem("a_out_copied")
        max_turned, out_turned, out_stored = sem("a_max_turned"), sem("a_out_turned"), sem("a_out_stored")
        recip_done = sem("a_recip_done")
        block = ctx.enter_context(nc.Block())

        def heads(eng, head):
            head(0, 0, 0, True, False)
            with eng.Fori(0, (H - 2) // 2) as i:
                head(i * 2 + 1, 1, i, False, False)
                head(i * 2 + 2, 0, i + 1, False, False)
            head(H - 1, 1, (H - 1) // 2, False, True)

        def wait_hi(eng, h, t):
            if t in HI_DVE:
                eng.wait_ge(hi_dve, h * len(HI_DVE) + (count_before(HI_DVE, t) + 1))
            else:
                eng.wait_ge(hi_act, h * (NS - len(HI_DVE)) + (t - count_before(HI_DVE, t) + 1))

        def wait_lo(eng, h, t):
            if t in LO_POOL:
                eng.wait_ge(lo_pool, h * len(LO_POOL) + (count_before(LO_POOL, t) + 1))
            else:
                eng.wait_ge(lo_dve, h * (NS - len(LO_POOL)) + (t - count_before(LO_POOL, t) + 1))

        @block.sync
        def _(sp):
            def load_head(h, p):
                for dst, parts in ((ks[p], (2, 3, 2)), (qs[p], (0, 0, 1))):
                    for n, part in enumerate(parts):
                        sp.dma_start(f32(dst[n * HD:(n + 1) * HD, :]),
                                     qk_dram[part, bass.ds(h * HD, HD), :]).then_inc(kq_landed[p], 16)
            def load_v(h, p):
                sp.dma_start(f32(vs[p][:]), f32(v_all[:, bass.ds(h, 1), :, :]).rearrange("p a t c -> p (a t) c")
                             ).then_inc(v_landed[p], 16)

            def send_max_a(p):
                sp.dma_start(f32(qs[p][ROW_MAX:ROW_MAX + 1, 0:QA * P]).rearrange("a (t q) -> a t q", t=QA),
                             f32(max_rows[:, :])).then_inc(max_a_landed[p], 16)

            def send_max_b(p):
                sp.dma_start(f32(qs[p][ROW_MAX:ROW_MAX + 1, QA * P:T]).rearrange("a (t q) -> a t q", t=NT - QA),
                             f32(max_rows_b[:, :])).then_inc(max_b_landed[p], 16)

            load_head(0, 0)
            load_v(0, 0)
            sp.wait_ge(max_a_out, 1)
            send_max_a(0)
            sp.wait_ge(max_b_out, 1)
            send_max_b(0)

            def head(h, p, visit, first, last):
                if not last:
                    if not first:
                        sp.wait_ge(scores_ready, h * NS)
                    load_head(h + 1, 1 - p)
                    if not first:
                        sp.wait_ge(pv_done, h * NS)
                    load_v(h + 1, 1 - p)
                if not first:
                    sp.wait_ge(max_b_out, h + 1)
                    send_max_b(p)
                if not last:
                    sp.wait_ge(max_a_out, h + 2)
                    send_max_a(1 - p)
            heads(sp, head)

        @block.gpsimd
        def _(pool):
            made = [0]

            def make(ins):
                made[0] += 1
                ins.then_inc(consts, 1)
                pool.wait_ge(consts, made[0])

            make(nc.gpsimd.memset(fold[:], 0.0))
            for off in (0, HD):
                make(nc.gpsimd.affine_select(out=fold[:, 0:HD], in_=fold[:, 0:HD], compare_op=ALU.not_equal, fill=1.0,
                                             base=-off, pattern=[[-1, HD]], channel_multiplier=1))
            make(nc.gpsimd.memset(fold[2 * HD:VW, HD:HD + 1], 1.0))
            make(nc.gpsimd.tensor_copy(ident_r[:], ident[:]))
            make(nc.gpsimd.memset(mask_f[:], 0.0))
            make(nc.gpsimd.affine_select(out=mask_f[:, 0:P], in_=mask_f[:, 0:P], compare_op=ALU.is_ge, fill=MASKED,
                                         base=0, pattern=[[-1, P]], channel_multiplier=1))
            make(nc.gpsimd.tensor_copy(mask_q[:], mask_f[:, 0:P]))
            make(nc.gpsimd.memset(mask_f[:, 0:P], 0.0))
            make(nc.gpsimd.affine_select(out=mask_f[:], in_=mask_f[:], compare_op=ALU.is_ge, fill=MASKED,
                                         base=-P, pattern=[[1, 2 * P]], channel_multiplier=-1))
            make(nc.gpsimd.tensor_copy(mask_k[:], mask_f[:]))
            assert made[0] == CONSTS

            def head(h, p, visit, first, last):
                for t in sorted(LO_POOL):
                    j, kp, c0 = S_TILES[t]
                    pool.wait_ge(prob_ready, h * NS + (t + 1))
                    wait_hi(pool, h, t)
                    nc.gpsimd.tensor_tensor(prob_lo[:, t % RING, :, c0:NB], prob[:, t % RING, :, c0:NB],
                                            f32(prob_hi[:, t % RING, :, c0:NB]), ALU.subtract).then_inc(lo_pool, 1)
            heads(pool, head)

        @block.scalar
        def _(act):
            def copy_out(g, j, done):
                act.wait_ge(pv_done, done)
                if not (isinstance(g, int) and g < 2):
                    act.wait_ge(out_turned, g - 1)
                nc.scalar.activation(o_sb[:, j % 2, :], op[0:VW, :], ACT.Copy).then_inc(out_copied, 1)

            def high_part(h, t):
                if t not in HI_DVE:
                    c0 = S_TILES[t][2]
                    act.wait_ge(prob_ready, h * NS + (t + 1))
                    nc.scalar.activation(prob_hi[:, t % RING, :, c0:NB], prob[:, t % RING, :, c0:NB],
                                         ACT.Copy).then_inc(hi_act, 1)

            def head(h, p, visit, first, last):
                for t, (j, kp, c0) in enumerate(S_TILES):
                    for step in ACT_ORDER:
                        if step == "E":
                            act.wait_ge(scores_ready, h * NS + (t + 1))
                            if not (first and t < RING):
                                act.wait_ge(pv_done, h * NS + (t + 1 - RING))
                            nc.scalar.activation(prob[:, t % RING, :, c0:NB], sp_[:, t % 2, :, c0:NB], ACT.Exp,
                                                 scale=SCALE).then_inc(prob_ready, 1)
                        if step == "H":
                            high_part(h, t)
                        if step == "C":
                            if t == J_LAST[-1] + LAG - NS and not first:
                                copy_out(h * NTB - 1, NTB - 1, h * NS)
                            for jj in range(NTB - 1):
                                if t == J_LAST[jj] + LAG:
                                    copy_out(h * NTB + jj, jj, h * NS + (J_LAST[jj] + 1))
            heads(act, head)
            copy_out(H * NTB - 1, NTB - 1, H * NS)

        @block.vector
        def _(dve):
            nc.vector.memset(part_max[:], LOWEST).then_inc(dve_consts, 1)
            nc.vector.tensor_scalar(neg_ident[:], ident[:], -1.0, None, ALU.mult).then_inc(dve_consts, 1)
            for p in range(2):
                nc.vector.memset(f32(ks[p][ROW_MAX:ROW_MAX + 1, :]), 1.0).then_inc(dve_consts, 1)
            dve.wait_ge(dve_consts, 4)

            def piece(h, n):
                qb, kb = PIECES[n]
                width = min(NB, (qb + 1) * P - kb * NB)
                dve.wait_ge(piece_ready, h * NPC + (n + 1))
                nc.vector.reduce_max(part_max[:, qb, kb:kb + 1], mp[:, n % 2, 0:width], AX_X).then_inc(piece_done, 1)

            def row_maxima(h, part):
                tiles, count, done = ((slice(0, QA), NPC_A, row_max_a) if part == "a" else
                                      (slice(QA, NT), NPC, row_max_b))
                dve.wait_ge(piece_done, h * NPC + count)
                nc.vector.tensor_reduce(row_max[:, tiles], part_max[:, tiles, :], AX_X, ALU.max).then_inc(done, 1)

            def maxima_out(h, part):
                dst, done = (max_rows, max_a_out) if part == "a" else (max_rows_b, max_b_out)
                dve.wait_ge(max_turned, h * 2 + (1 if part == "a" else 2))
                nc.vector.tensor_copy(dst[:, :], shared[0:dst.shape[0], 0:P]).then_inc(done, 1)

            def store_out(h, g, j):
                dve.wait_ge(out_turned, g + 1)
                turned = shared[:, 0:NTB * FW].rearrange("p (a c) -> p a c", c=FW)
                nc.vector.reciprocal(recip[:], turned[:, :, HD:HD + 1]).then_inc(recip_done, 1)
                dve.wait_ge(recip_done, g + 1)
                nc.vector.tensor_tensor(rows[:, NTB * j:NTB * (j + 1), bass.ds(h * HD, HD)], turned[:, :, 0:HD],
                                        recip[:].to_broadcast([P, NTB, HD]), ALU.mult).then_inc(out_stored, 1)

            def high_part(h, t):
                if t in HI_DVE:
                    c0 = S_TILES[t][2]
                    dve.wait_ge(prob_ready, h * NS + (t + 1))
                    nc.vector.tensor_copy(prob_hi[:, t % RING, :, c0:NB], prob[:, t % RING, :, c0:NB]).then_inc(hi_dve, 1)

            def low_part(h, t):
                if t in LO_POOL:
                    return
                c0 = S_TILES[t][2]
                wait_hi(dve, h, t)
                nc.vector.tensor_tensor(prob_lo[:, t % RING, :, c0:NB], prob[:, t % RING, :, c0:NB],
                                        f32(prob_hi[:, t % RING, :, c0:NB]), ALU.subtract).then_inc(lo_dve, 1)

            for n in range(NPC_A):
                piece(0, n)
            row_maxima(0, "a")
            maxima_out(0, "a")
            for n in range(NPC_A, NPC):
                piece(0, n)
            row_maxima(0, "b")
            maxima_out(0, "b")

            def head(h, p, visit, first, last):
                for t, (j, kp, c0) in enumerate(S_TILES):
                    if t == 0 and not first:
                        row_maxima(h, "b")
                    if t == PIECES_AT_A and not last:
                        row_maxima(h + 1, "a")
                    pieces = [] if last else list(range(sum(PIECES_AT[:t]), sum(PIECES_AT[:t + 1])))
                    for step in DVE_ORDER:
                        if step in "pr":
                            for _ in range(len(pieces) if step == "r" else min(1, len(pieces))):
                                piece(h + 1, pieces.pop(0))
                        if step in "hl":
                            part = {"h": high_part, "l": low_part}[step]
                            if t >= 1:
                                part(h, t - 1)
                            elif not first:
                                part(h - 1, NS - 1)
                    what = SHARED_AT.get(t)
                    if what == "max_b" and not first:
                        maxima_out(h, "b")
                    if what == "max_a" and not last:
                        maxima_out(h + 1, "a")
                    if what == NTB - 1 and not first:
                        store_out(h - 1, h * NTB - 1, NTB - 1)
                    if what in range(NTB - 1):
                        store_out(h, h * NTB + what, what)
            heads(dve, head)
            high_part(H - 1, NS - 1)
            low_part(H - 1, NS - 1)
            store_out(H - 1, H * NTB - 1, NTB - 1)

        @block.tensor
        def _(pe):
            def piece(h, p, n):
                qb, kb = PIECES[n]
                k0, k1 = kb * NB, min((kb + 1) * NB, (qb + 1) * P)
                if not (isinstance(h, int) and h == 0 and n < 2):
                    pe.wait_ge(piece_done, h * NPC + (n - 1))
                diagonal = k1 == (qb + 1) * P
                last = nc.tensor.matmul(mp[:, n % 2, 0:k1 - k0], qs[p][0:K_ROWS, qb * P:(qb + 1) * P],
                                        ks[p][0:K_ROWS, k0:k1], start=True, stop=not diagonal)
                if diagonal:
                    last = nc.tensor.matmul(mp[:, n % 2, k1 - k0 - P:k1 - k0], ident_r[:], mask_q[:],
                                            start=False, stop=True)
                last.then_inc(piece_ready, 1)

            def turn_maxima(h, part):
                tiles, done = (slice(0, QA), row_max_a) if part == "a" else (slice(QA, NT), row_max_b)
                pe.wait_ge(done, h + 1)
                nc.tensor.matmul(shared[0:tiles.stop - tiles.start, 0:P], row_max[:, tiles], neg_ident[:],
                                 start=True, stop=True).then_inc(max_turned, 1)

            def turn_out(g, j):
                pe.wait_ge(out_copied, g + 1)
                for q in range(NTB):
                    last = nc.tensor.matmul(shared[:, q * FW:q * FW + HD + 1], o_sb[:, j % 2, q * P:(q + 1) * P],
                                            fold[:, 0:HD + 1], start=True, stop=True)
                last.then_inc(out_turned, 1)

            def times_v(h, p, t, parts=(0, 1)):
                j, kp, c0 = S_TILES[t]
                if parts[0] == 0 and t == J_FIRST[j] and not (isinstance(h, int) and h == 0 and j == 0):
                    pe.wait_ge(out_copied, h * NTB + j)
                for part in parts:
                    (wait_hi, wait_lo)[part](pe, h, t)
                    for b in range(2):
                        cols = slice(c0 + (P if b and kp >= 2 * j else 0), NB)
                        last = nc.tensor.matmul(op[0:VW, cols], vs[p][:, 2 * kp + b, :],
                                                (prob_hi, prob_lo)[part][:, t % RING, b, cols],
                                                start=t == J_FIRST[j] and part == b == 0,
                                                stop=t == J_LAST[j] and part == b == 1)
                if parts[-1] == 1:
                    last.then_inc(pv_done, 1)

            def scores(h, p, t):
                j, kp, c0 = S_TILES[t]
                if not (isinstance(h, int) and h == 0 and t < 2):
                    pe.wait_ge(prob_ready, h * NS + (t - 1))
                for b in range(2):
                    kb = 2 * kp + b
                    diagonal = kp >= 2 * j
                    last = nc.tensor.matmul(sp_[:, t % 2, b, c0:NB], ks[p][0:ROW_MAX + 1, kb * P:(kb + 1) * P],
                                            qs[p][0:ROW_MAX + 1, j * NB + c0:(j + 1) * NB], start=True, stop=not diagonal)
                    if diagonal:
                        mask = mask_k[:, :] if b else mask_k[:, P:2 * P]
                        last = nc.tensor.matmul(sp_[:, t % 2, b, c0:c0 + mask.shape[1]], ident_r[:], mask,
                                                start=False, stop=True)
                last.then_inc(scores_ready, 1)

            pe.wait_ge(consts, CONSTS)
            pe.wait_ge(dve_consts, 4)
            pe.wait_ge(kq_landed[0], 16 * KQ_LOADS)
            for n in range(NPC_A):
                piece(0, 0, n)
            turn_maxima(0, "a")
            for n in range(NPC_A, NPC):
                piece(0, 0, n)
            pe.wait_ge(max_a_out, 1)
            turn_maxima(0, "b")

            def head(h, p, visit, first, last):
                for t, (j, kp, c0) in enumerate(S_TILES):
                    if t == 0:
                        pe.wait_ge(max_a_landed[p], visit * 16 + 16)
                    if t == J_FIRST[NTB - 1]:
                        pe.wait_ge(max_b_landed[p], visit * 16 + 16)
                    pieces = [] if last else list(range(sum(PIECES_AT[:t]), sum(PIECES_AT[:t + 1])))
                    if pieces and pieces[0] == 0:
                        pe.wait_ge(kq_landed[1 - p], (visit + p) * (16 * KQ_LOADS) + 16 * KQ_LOADS)
                    if t == LAG:
                        pe.wait_ge(v_landed[p], visit * 16 + 16)
                    for step in PE_ORDER:
                        if step == "S":
                            scores(h, p, t)
                        if step in "pr":
                            for _ in range(len(pieces) if step == "r" else min(1, len(pieces))):
                                piece(h + 1, 1 - p, pieces.pop(0))
                        if step in "HL":
                            if t >= LAG:
                                times_v(h, p, t - LAG, ("HL".index(step),))
                            elif not first:
                                times_v(h - 1, 1 - p, NS - LAG + t, ("HL".index(step),))
                    what = SHARED_AT.get(t)
                    if what == "max_b" and not first:
                        pe.wait_ge(out_stored, h * NTB - 1)
                        turn_maxima(h, "b")
                    if what == NTB - 1 and not first:
                        pe.wait_ge(max_b_out, h + 1)
                        turn_out(h * NTB - 1, NTB - 1)
                    if what == 0:
                        if first:
                            pe.wait_ge(max_b_out, 1)
                        else:
                            pe.wait_ge(out_stored, h * NTB)
                        turn_out(h * NTB, 0)
                    if what == 1:
                        pe.wait_ge(out_stored, h * NTB + 1)
                        turn_out(h * NTB + 1, 1)
                    if what == "max_a" and not last:
                        pe.wait_ge(out_stored, h * NTB + 2)
                        turn_maxima(h + 1, "a")
                    if what == 2:
                        if last:
                            pe.wait_ge(out_stored, h * NTB + 2)
                        else:
                            pe.wait_ge(max_a_out, h + 2)
                        turn_out(h * NTB + 2, 2)
            heads(pe, head)
            for t in range(NS - LAG, NS):
                times_v(H - 1, (H - 1) % 2, t)
            pe.wait_ge(out_stored, H * NTB - 1)
            turn_out(H * NTB - 1, NTB - 1)


def stage_project(nc, x_dram, wproj_dram, wgate_dram, wexp_dram, rows, ident, ln_consts, h_hi, h_lo, x1_dram,
                  x1, logits, wexp_raw, wexp_hi, wexp_lo):
    with ExitStack() as ctx:
        sb = lambda n, s, d: ctx.enter_context(nc.sbuf_tensor(n, s, d))
        pb = lambda n, s: ctx.enter_context(nc.psum_tensor(n, s, F32))
        sem = lambda n: ctx.enter_context(nc.semaphore(n))

        w_raw = wexp_raw[:].rearrange("p c m n -> p (c m n)")[:, 0:KC * (D + E)].rearrange("p (k n) -> p k n", k=KC)
        w_hi = sb("p_w_hi", [P, KC, D + E], F32R)
        w_lo = sb("p_w_lo", [P, KC, D + E], F32R)
        a_in = sb("a_in", [P, 2, D], F32)
        at_hi = sb("at_hi", [P, 2, KC, P], F32R)
        at_lo = sb("at_lo", [P, 2, KC, P], F32R)
        ht_hi = sb("ht_hi", [P, 2, KC, P], F32R)
        ht_lo = sb("ht_lo", [P, 2, KC, P], F32R)
        x_in = sb("p_x_in", [P, 4, D], F32)
        branch = sb("branch", [P, 2, D], F32)
        hn = sb("hn", [P, 2, D], F32)
        st = sb("p_st", [P, 2, 2, 6], F32)
        mv = sb("p_mv", [P, 2, 2, 2], F32)
        rstd = sb("p_rstd", [P, 2, 2, 1], F32)
        veps = sb("p_veps", [P, 2, 1], F32)
        tps = pb("p_tps", [P, 4, NB])
        prj = pb("p_prj", [P, 2, NB])
        lg = pb("p_lg", [P, 2, NB])

        w_landed, w_hi_done, w_lo_done = sem("p_w_landed"), sem("p_w_hi_done"), sem("p_w_lo_done")
        x_landed = [sem(f"p_x_landed{i}") for i in range(4)]
        x1_stored = [sem(f"p_x1_stored{i}") for i in range(4)]
        a_copied, at_ready, at_hi_done, at_lo_done = (sem("p_a_copied"), sem("p_at_ready"), sem("p_at_hi_done"),
                                                      sem("p_at_lo_done"))
        veps_done = [sem(f"p_veps_done{i}") for i in range(2)]
        proj_ready, x1_ready = sem("p_proj_ready"), sem("p_x1_ready")
        stats1, aggr1, rstd1, branch_ready = sem("p_stats1"), sem("p_aggr1"), sem("p_rstd1"), sem("p_branch_ready")
        stats2, aggr2, rstd2, hn_ready = sem("p_stats2"), sem("p_aggr2"), sem("p_rstd2"), sem("p_hn_ready")
        ht_ready, ht_hi_done, ht_lo_done, h_copied = (sem("p_ht_ready"), sem("p_ht_hi_done"), sem("p_ht_lo_done"),
                                                      [sem(f"p_h_copied{i}") for i in range(2)])
        logits_ready, logits_copied = sem("p_logits_ready"), sem("p_logits_copied")
        wexp_landed, wexp_hi_done, wexp_lo_done = sem("p_wexp_landed"), sem("p_wexp_hi_done"), sem("p_wexp_lo_done")
        block = ctx.enter_context(nc.Block())

        STEPS = NT + 3
        SPLIT_FROM = STEPS - SPLITS

        @block.sync
        def _(sp):
            sp.dma_start(w_raw[:, :, 0:D], wproj_dram).then_inc(w_landed, 16)
            sp.dma_start(w_raw[:, :, D:D + E], wgate_dram).then_inc(w_landed, 16)
            for s in range(4):
                sp.dma_start(x_in[:, s, :], x_dram[s]).then_inc(x_landed[s], 16)

            def step(t, k):
                if inside(t, 0, NT):
                    store(t, k)
                if isinstance(t, int) and t == 3:
                    sp.wait_ge(w_lo_done, 1)
                    sp.dma_start(wexp_raw[:].rearrange("p c m n -> p (c m n)"), wexp_dram[:, 0, :]).then_inc(wexp_landed, 16)
                if inside(t, -2, NT):
                    sp.wait_ge(ht_lo_done, t - 1)
                    toks = bass.ds((t - 2) * P, P)
                    sp.dma_start(f32(h_hi[:, :, toks]), f32(ht_hi[:, k % 2])).then_inc(h_copied[k % 2], 16)
                    sp.dma_start(f32(h_lo[:, :, toks]), f32(ht_lo[:, k % 2])).then_inc(h_copied[k % 2], 16)

            def store(t, k):
                sp.wait_ge(x1_ready, t + 1)
                sp.dma_start(one(x1_dram, t), x1[:, k % 4, :]).then_inc(x1_stored[k % 4], 16)
                if inside(t, 4, NT):
                    sp.dma_start(x_in[:, k % 4, :], one(x_dram, t + 4)).then_inc(x_landed[k % 4], 16)
            stepped(sp, 4, 2, 4, STEPS, step)
            for s in range(4):
                sp.wait_ge(x1_stored[s], 16 * NT // 4)
            for slot in range(2):
                sp.wait_ge(h_copied[slot], 32 * NT // 2)

        @block.gpsimd
        def _(pool):
            def inverse_deviation(t, which, j, aggr, done):
                pool.wait_ge(aggr, t + 1)
                if inside(t, -1, NT):
                    pool.wait_ge(done, t)
                nc.gpsimd.tensor_tensor(veps[:, which], mv[:, which, j, 1:2], ln_consts[:, 0:1], ALU.add).then_inc(veps_done[which], 1)
                pool.wait_ge(veps_done[which], t + 1)
                nc.gpsimd.tensor_tensor(rstd[:, which, j], veps[:, which], ln_consts[:, 1:2], ALU.pow).then_inc(done, 1)

            def step(t, k):
                if inside(t, 0, NT):
                    inverse_deviation(t, 0, k % 2, aggr1, rstd1)
                if inside(t, -1, NT):
                    inverse_deviation(t - 1, 1, (k - 1) % 2, aggr2, rstd2)
                if inside(t, 0, NT):
                    pool.wait_ge(branch_ready, t + 1)
                    pool.wait_ge(x_landed[k % 4], (t - k % 4) * 4 + 16)
                    if inside(t, -4, NT):
                        pool.wait_ge(x1_stored[k % 4], (t - k % 4) * 4)
                    nc.gpsimd.tensor_tensor(x1[:, k % 4, :], branch[:, k % 2, :], x_in[:, k % 4, :],
                                            ALU.add).then_inc(x1_ready, 1)
                if isinstance(t, int) and t >= SPLIT_FROM:
                    i = t - SPLIT_FROM
                    pool.wait_ge(wexp_hi_done, i + 1)
                    nc.gpsimd.tensor_tensor(wexp_lo[:, i // 3, i % 3, :], wexp_raw[:, i // 3, i % 3, :],
                                            f32(wexp_hi[:, i // 3, i % 3, :]), ALU.subtract).then_inc(wexp_lo_done, 1)
            stepped(pool, 4, 2, 4, STEPS, step)

        @block.scalar
        def _(act):

            def copy_in(t, k):
                if inside(t, -2, NT):
                    act.wait_ge(at_ready, t - 1)
                nc.scalar.activation(a_in[:, k % 2, :], rows[:, bass.ds(t, 1), :].rearrange("p a d -> p (a d)"),
                                     ACT.Copy).then_inc(a_copied, 1)

            def attention_high(t, k):
                act.wait_ge(at_ready, t + 1)
                if inside(t, -2, NT):
                    act.wait_ge(proj_ready, t - 1)
                nc.scalar.activation(at_hi[:, k % 2].rearrange("p c q -> p (c q)"), tps[:, k % 2, :],
                                     ACT.Copy).then_inc(at_hi_done, 1)
            copy_in(0, 0)
            copy_in(1, 1)
            act.wait_ge(w_landed, 32)
            nc.scalar.activation(w_hi[:], w_raw[:], ACT.Copy).then_inc(w_hi_done, 1)
            attention_high(0, 0)

            def step(t, k):
                if inside(t, 1, NT):
                    attention_high(t + 1, k + 1)
                if inside(t, 2, NT):
                    copy_in(t + 2, k + 2)
                if inside(t, -2, NT):
                    act.wait_ge(ht_ready, t - 1)
                    if inside(t, -4, NT):
                        act.wait_ge(h_copied[k % 2], (t - k % 2) * 16 - 32)
                        act.wait_ge(logits_ready, t - 3)
                    nc.scalar.activation(ht_hi[:, k % 2].rearrange("p c q -> p (c q)"), tps[:, 2 + k % 2, :],
                                         ACT.Copy).then_inc(ht_hi_done, 1)
                if isinstance(t, int) and t >= SPLIT_FROM:
                    i = t - SPLIT_FROM
                    if i == 0:
                        act.wait_ge(wexp_landed, 16)
                    nc.scalar.activation(wexp_hi[:, i // 3, i % 3, :], wexp_raw[:, i // 3, i % 3, :],
                                         ACT.Copy).then_inc(wexp_hi_done, 1)
            stepped(act, 4, 2, 4, STEPS, step)

        @block.vector
        def _(dve):
            dve.wait_ge(w_hi_done, 1)
            nc.vector.tensor_tensor(w_lo[:], w_raw[:], f32(w_hi[:]), ALU.subtract).then_inc(w_lo_done, 1)

            def attention_low(t, k):
                dve.wait_ge(at_hi_done, t + 1)
                nc.vector.tensor_tensor(at_lo[:, k % 2].rearrange("p c q -> p (c q)"), tps[:, k % 2, :],
                                        f32(at_hi[:, k % 2]).rearrange("p c q -> p (c q)"),
                                        ALU.subtract).then_inc(at_lo_done, 1)

            def statistics(t, which, j, src, stats):
                nc.vector.bn_stats(st[:, which, j], src).then_inc(stats, 1)

            def aggregate(t, which, j, aggr):
                nc.vector.bn_aggr(mv[:, which, j], st[:, which, j]).then_inc(aggr, 1)

            def normalise(t, which, j, src, dst, rstd_done, done):
                dve.wait_ge(rstd_done, t + 1)
                nc.vector.tensor_scalar(dst, src, mv[:, which, j, 0:1], rstd[:, which, j, 0:1],
                                        ALU.subtract, ALU.mult).then_inc(done, 1)
            attention_low(0, 0)

            def step(t, k):
                if inside(t, 1, NT):
                    attention_low(t + 1, k + 1)
                if inside(t, 0, NT):
                    dve.wait_ge(proj_ready, t + 1)
                    statistics(t, 0, k % 2, prj[:, k % 2, :], stats1)
                    dve.wait_ge(stats1, t + 1)
                if inside(t, -2, NT):
                    dve.wait_ge(ht_hi_done, t - 1)
                    nc.vector.tensor_tensor(ht_lo[:, k % 2].rearrange("p c q -> p (c q)"), tps[:, 2 + k % 2, :],
                                            f32(ht_hi[:, k % 2]).rearrange("p c q -> p (c q)"),
                                            ALU.subtract).then_inc(ht_lo_done, 1)
                if inside(t, 0, NT):
                    aggregate(t, 0, k % 2, aggr1)
                if inside(t, -1, NT):
                    dve.wait_ge(x1_ready, t)
                    statistics(t - 1, 1, (k - 1) % 2, x1[:, (k - 1) % 4, :], stats2)
                    dve.wait_ge(stats2, t)
                if inside(t, -3, NT):
                    dve.wait_ge(logits_ready, t - 2)
                    nc.vector.tensor_copy(logits[:, bass.ds(t - 3, 1), :].rearrange("p a e -> p (a e)"),
                                          lg[:, (k - 3) % 2, 0:E]).then_inc(logits_copied, 1)
                if inside(t, -1, NT):
                    aggregate(t - 1, 1, (k - 1) % 2, aggr2)
                if inside(t, 0, NT):
                    if inside(t, -2, NT):
                        dve.wait_ge(x1_ready, t - 1)
                    normalise(t, 0, k % 2, prj[:, k % 2, :], branch[:, k % 2, :], rstd1, branch_ready)
                if inside(t, -1, NT):
                    if not (isinstance(t, int) and t < 3):
                        dve.wait_ge(ht_ready, t - 2)
                    normalise(t - 1, 1, (k - 1) % 2, x1[:, (k - 1) % 4, :], hn[:, (k - 1) % 2, :], rstd2, hn_ready)
            stepped(dve, 4, 2, 4, STEPS, step)

        @block.tensor
        def _(pe):
            def turn_attention(t, k):
                pe.wait_ge(a_copied, t + 1)
                if inside(t, -2, NT):
                    pe.wait_ge(at_lo_done, t - 1)
                for c in range(KC):
                    last = nc.tensor.transpose(tps[:, k % 2, c * P:(c + 1) * P], a_in[:, k % 2, c * P:(c + 1) * P], ident[:])
                last.then_inc(at_ready, 1)
            turn_attention(0, 0)

            def step(t, k):
                if inside(t, 1, NT):
                    turn_attention(t + 1, k + 1)
                if inside(t, 0, NT):
                    pe.wait_ge(at_lo_done, t + 1)
                    if isinstance(t, int) and t == 0:
                        pe.wait_ge(w_lo_done, 1)
                    if inside(t, -2, NT):
                        pe.wait_ge(branch_ready, t - 1)
                    j = k % 2
                    three_passes(nc, prj[:, j, :], lambda c: (at_hi[:, j, c], at_lo[:, j, c], w_hi[:, c, 0:D],
                                                              w_lo[:, c, 0:D]), KC).then_inc(proj_ready, 1)
                if inside(t, -2, NT):
                    pe.wait_ge(hn_ready, t - 1)
                    if not (isinstance(t, int) and t < 4):
                        pe.wait_ge(ht_lo_done, t - 3)
                    for c in range(KC):
                        last = nc.tensor.transpose(tps[:, 2 + k % 2, c * P:(c + 1) * P],
                                                   hn[:, k % 2, c * P:(c + 1) * P], ident[:])
                    last.then_inc(ht_ready, 1)
                if inside(t, -3, NT):
                    pe.wait_ge(ht_lo_done, t - 2)
                    if not (isinstance(t, int) and t < 5):
                        pe.wait_ge(logits_copied, t - 4)
                    j = (k - 3) % 2
                    three_passes(nc, lg[:, j, 0:E], lambda c: (ht_hi[:, j, c], ht_lo[:, j, c], w_hi[:, c, D:D + E],
                                                               w_lo[:, c, D:D + E]), KC).then_inc(logits_ready, 1)
            stepped(pe, 4, 2, 4, STEPS, step)


def router_views(buffer):
    flat, views, at = buffer[:].rearrange("p a d -> p (a d)"), [], 0
    for width in (E, E + 2, E + 2, 8, 1, 1):
        views.append(flat[:, at:at + NT * width].rearrange("p (t e) -> p t e", t=NT))
        at += NT * width
    assert at <= 2 * D
    return views


def stage_experts(nc, w_dram, cw_dram, x1_dram, out_dram, rows, ident, ln_consts, h_hi, h_lo, x1, spare, w_raw,
                  w_hi0, w_lo0):
    with ExitStack() as ctx:
        sb = lambda n, s, d: ctx.enter_context(nc.sbuf_tensor(n, s, d))
        pb = lambda n, s: ctx.enter_context(nc.psum_tensor(n, s, F32))
        sem = lambda n: ctx.enter_context(nc.semaphore(n))

        GATE, UP, DOWN = 0, 1, 2
        SPLIT_AT = {2: [0], 3: [1], 4: [2], 5: [3], 6: [4, 5]}
        w_hi = [w_hi0, sb("m_w_hi1", [P, 2, 3, NB], F32R)]
        w_lo = [w_lo0, sb("m_w_lo1", [P, 2, 3, NB], F32R)]
        cwb = sb("cwb", [P, 2, 2, NB], F32)
        gate = sb("m_gate", [P, 2, NB], F32)
        gated = sb("m_gated", [P, 2, NB], F32)
        act_f = sb("m_act", [P, 2, NB], F32)
        act_hi = sb("m_act_hi", [P, 2, 2, NB], F32R)
        act_lo = sb("m_act_lo", [P, 2, 2, NB], F32R)
        logits, scores, rest, best, top, total = router_views(spare)
        cw = logits
        cwT = x1[0:E].rearrange("p a d -> p (a d)")
        st = sb("m_st", [P, NTB, 6], F32)
        mv = sb("m_mv", [P, NTB, 2], F32)
        rstd = sb("m_rstd", [P, NTB, 1], F32)
        veps = sb("m_veps", [P, NTB, 1], F32)
        gp = pb("m_gp", [P, 2, NB])
        up = pb("m_up", [P, 2, NB])
        yp = pb("m_yp", [P, NTB, NB])

        w_landed, w_hi_done, w_split = sem("m_w_landed"), sem("m_w_hi_done"), sem("m_w_split")
        cw_landed = [sem(f"m_cw_landed{i}") for i in range(2)]
        g_ready, u_ready, gate_done, gated_done = sem("m_g_ready"), sem("m_u_ready"), sem("m_gate_done"), sem("m_gated_done")
        act_done, act_hi_done, act_lo_done = sem("m_act_done"), sem("m_act_hi_done"), sem("m_act_lo_done")
        rows_cleared, y_ready, y_added = sem("m_rows_cleared"), sem("m_y_ready"), sem("m_y_added")
        stats, aggr, rstd_done, ln_ready, out_ready = (sem("m_stats"), sem("m_aggr"), sem("m_rstd_done"),
                                                        sem("m_ln_ready"), sem("m_out_ready"))
        veps_done = sem("m_veps_done")
        last_x1_landed, last_out_ready, last_out_stored = (sem("m_last_x1_landed"), sem("m_last_out_ready"),
                                                           sem("m_last_out_stored"))
        x1_landed = [sem(f"m_x1_landed{i}") for i in range(4)]
        out_stored = [sem(f"m_out_stored{i}") for i in range(4)]
        marks_set, route, exp_done = sem("m_marks_set"), sem("m_route"), sem("m_exp_done")
        cw_ready, cwT_turned, cwT_ready = sem("m_cw_ready"), sem("m_cwT_turned"), sem("m_cwT_ready")
        cw_first, cw_stored = sem("m_cw_first"), sem("m_cw_stored")
        block = ctx.enter_context(nc.Block())

        UNITS = PAIRS * NTB
        LAST_PAIR = UNITS - NTB

        def units(eng, step):
            stepped(eng, NTB, (UNITS - 2 * NTB) // (2 * NTB), 2 * NTB, UNITS, step)

        def from_unit(u, least):
            return not isinstance(u, int) or u >= least

        @block.sync
        def _(sp):
            w_quarters = w_dram.rearrange("p a (q n) -> p (a q) n", q=NTB)

            def load_raw(u):
                sp.dma_start(w_raw[:].rearrange("p c m n -> p (c m n)"),
                             w_quarters[:, bass.ds(u + NTB, NTB), :].rearrange("p a n -> p (a n)")).then_inc(w_landed, 16)
            load_raw(0)
            sp.wait_ge(cwT_ready, NTB)
            groups = cw_dram.rearrange("(e g) t -> e g t", g=GPE)
            for e0, e1, stored in ((0, 1, cw_first), (1, E, cw_stored)):
                sp.dma_start(groups[e0:e1], cwT[e0:e1].unsqueeze(1).to_broadcast([e1 - e0, GPE, T])).then_inc(stored, 16)
            sp.wait_ge(cw_first, 16)

            def step(u, k):
                if from_unit(u, 2):
                    sp.wait_ge(act_done, u * 2 - 2)
                tb = k % NTB
                for c in range(2):
                    g0 = (u - tb) * (2 * P // GROUP // NTB) + c * (P // GROUP)
                    sp.dma_start(cwb[:, k % 2, c, :],
                                 cw_dram[bass.ds(g0, P // GROUP), tb * NB:(tb + 1) * NB].unsqueeze(1)
                                 .to_broadcast([P // GROUP, GROUP, NB])).then_inc(cw_landed[k % 2], 16)
                if tb == 0 and from_unit(u, 1) and not (isinstance(u, int) and u >= LAST_PAIR):
                    sp.wait_ge(w_split, u * 3)
                    load_raw(u)
                if isinstance(u, int) and u == NTB - 1:
                    sp.wait_ge(cw_stored, 16)
                if isinstance(u, int) and u == LAST_PAIR:
                    for s in range(4):
                        sp.dma_start(x1[:, s, :], x1_dram[s]).then_inc(x1_landed[s], 16)
                    for s in range(2):
                        sp.dma_start(spare[:, s, :], x1_dram[NT - 2 + s]).then_inc(last_x1_landed, 16)
            units(sp, step)
            for t in range(NT - 2):
                sp.wait_ge(out_ready, t + 1)
                sp.dma_start(out_dram[t], x1[:, t % 4, :]).then_inc(out_stored[t % 4], 16)
                if 2 <= t < NT - 4:
                    sp.wait_ge(out_stored[(t - 2) % 4], 16 * ((t - 2) // 4 + 1))
                    sp.dma_start(x1[:, (t + 2) % 4, :], x1_dram[t + 2]).then_inc(x1_landed[(t + 2) % 4], 16)
            for s in range(2):
                sp.wait_ge(last_out_ready, s + 1)
                sp.dma_start(out_dram[NT - 2 + s], spare[:, s, :]).then_inc(last_out_stored, 16)
            for s in range(4):
                sp.wait_ge(out_stored[s], 16 * len(range(s, NT - 2, 4)))
            sp.wait_ge(last_out_stored, 32)

        @block.gpsimd
        def _(pool):
            nc.gpsimd.memset(scores[:, :, E:E + 1], -1.0).then_inc(marks_set, 1)
            nc.gpsimd.memset(scores[:, :, E + 1:E + 2], -2.0).then_inc(marks_set, 1)
            nc.gpsimd.memset(rows[:, NT - NTB:NT, :], 0.0).then_inc(rows_cleared, 1)

            def split_piece(u0, k, i):
                c, m = i // 3, i % 3
                dst = (k // NTB + 1) % 2
                if i == 0:
                    pool.wait_ge(w_landed, u0 * 4 + 16)
                    if from_unit(u0, 1):
                        pool.wait_ge(y_ready, u0 * 4)
                nc.gpsimd.tensor_copy(w_hi[dst][:, c, m, :], w_raw[:, c, m, :]).then_inc(w_hi_done, 2)
                pool.wait_ge(w_hi_done, u0 * 3 + 2 * (i + 1))
                nc.gpsimd.tensor_tensor(w_lo[dst][:, c, m, :], w_raw[:, c, m, :], f32(w_hi[dst][:, c, m, :]),
                                        ALU.subtract).then_inc(w_split, 2)

            def step(u, k):
                for c in range(2):
                    n = u * 2 + c
                    if c == 0:
                        pool.wait_ge(cw_landed[k % 2], (u - k % 2) * 16 + 32)
                    pool.wait_ge(gated_done, n + 1)
                    if from_unit(u, 1):
                        pool.wait_ge(act_lo_done, n - 1)
                    nc.gpsimd.tensor_tensor(act_f[:, c, :], gated[:, c, :], cwb[:, k % 2, c, :],
                                            ALU.mult).then_inc(act_done, 1)
                    if not (isinstance(u, int) and u >= LAST_PAIR):
                        for i in SPLIT_AT.get(2 * (k % NTB) + c, ()):
                            split_piece(u - k % NTB, k, i)
                    if isinstance(u, int) and u > LAST_PAIR and c:
                        deviation(u - LAST_PAIR - 1)
                        residual(u - LAST_PAIR - 1)

            def deviation(tb):
                pool.wait_ge(aggr, NTB * (tb + 1))
                if tb:
                    pool.wait_ge(rstd_done, tb)
                nc.gpsimd.tensor_scalar(veps[:], mv[:, :, 1:2], EPS, None, ALU.add).then_inc(veps_done, 1)
                pool.wait_ge(veps_done, tb + 1)
                nc.gpsimd.tensor_tensor(rstd[:], veps[:], ln_consts[:, 1:2].to_broadcast([P, NTB]).unsqueeze(2),
                                        ALU.pow).then_inc(rstd_done, 1)

            def residual(tb):
                for t in range(NTB * tb, min(NTB * (tb + 1), NT - 2)):
                    pool.wait_ge(ln_ready, t + 1)
                    pool.wait_ge(x1_landed[t % 4], 16 * (t // 4 + 1))
                    nc.gpsimd.tensor_tensor(x1[:, t % 4, :], x1[:, t % 4, :], rows[:, t, :],
                                            ALU.add).then_inc(out_ready, 1)
            units(pool, step)
            deviation(NTB - 1)
            residual(NTB - 1)

        @block.scalar
        def _(act):
            act.wait_ge(route, 2)
            nc.scalar.activation(logits, logits, ACT.Exp).then_inc(exp_done, 1)

            def silu(u, c):
                act.wait_ge(g_ready, u * 2 + (c + 1))
                if from_unit(u, 1):
                    act.wait_ge(gated_done, u * 2 + (c - 1))
                nc.scalar.activation(gate[:, c, :], gp[:, c, :], ACT.Silu).then_inc(gate_done, 1)

            def high_part(u, k, c):
                act.wait_ge(act_done, u * 2 + (c + 1))
                if c == 0 and from_unit(u, 2):
                    act.wait_ge(y_ready, u * 4 - 4)
                nc.scalar.activation(act_hi[:, k % 2, c, :], act_f[:, c, :], ACT.Copy).then_inc(act_hi_done, 1)

            def step(u, k):
                if isinstance(u, int) and u == 0:
                    silu(0, 0)
                    for b in range(NTB):
                        act.wait_ge(cwT_turned, b + 1)
                        nc.scalar.activation(cwT[:, b * NB:(b + 1) * NB], yp[0:E, b, :], ACT.Copy).then_inc(cwT_ready, 1)
                    silu(0, 1)
                for c in range(2):
                    if from_unit(u, 1):
                        silu(u, c)
                    high_part(u, k, c)
            units(act, step)

        @block.vector
        def _(dve):
            nc.vector.tensor_reduce(top[:, :, 0], logits, AX_X, ALU.max).then_inc(route, 1)
            dve.wait_ge(route, 1)
            nc.vector.tensor_tensor(logits, logits, top.to_broadcast([P, NT, E]), ALU.subtract).then_inc(route, 1)
            dve.wait_ge(exp_done, 1)
            nc.vector.reduce_sum(total[:, :, 0], logits, AX_X).then_inc(route, 1)
            dve.wait_ge(route, 3)
            nc.vector.reciprocal(top, total).then_inc(route, 1)
            dve.wait_ge(route, 4)
            dve.wait_ge(marks_set, 2)
            nc.vector.tensor_tensor(scores[:, :, 0:E], logits, top.to_broadcast([P, NT, E]), ALU.mult).then_inc(route, 1)
            dve.wait_ge(route, 5)
            for t in range(NT):
                nc.vector.max(best[:, t, :], scores[:, t, 0:E]).then_inc(route, 1)
            dve.wait_ge(route, 5 + NT)
            nc.vector.memset(best[:, :, TOPK:TOPK + 1], -1.0).then_inc(route, 1)
            nc.vector.memset(best[:, :, TOPK + 1:TOPK + 2], -2.0).then_inc(route, 1)
            dve.wait_ge(route, 7 + NT)
            for t in range(NT):
                nc.vector.match_replace(rest[:, t, :], best[:, t, :], scores[:, t, :], 0.0).then_inc(route, 1)
            dve.wait_ge(route, 7 + 2 * NT)
            nc.vector.tensor_tensor(cw, scores[:, :, 0:E], rest[:, :, 0:E], ALU.subtract).then_inc(cw_ready, 1)

            def add_up(u, tb):
                if isinstance(u, int) and u == NTB - 2:
                    dve.wait_ge(rows_cleared, 1)
                for s in range(NTB):
                    dve.wait_ge(y_ready, u * 4 + (s + 1))
                    t = NTB * tb + s
                    if isinstance(u, int) and u < NTB - 1:
                        nc.vector.tensor_copy(rows[:, t, :], yp[:, s, :]).then_inc(y_added, 1)
                    else:
                        nc.vector.tensor_tensor(rows[:, t, :], yp[:, s, :], rows[:, t, :], ALU.add).then_inc(y_added, 1)

            def statistics(tb):
                tiles = range(NTB * tb, NTB * (tb + 1))
                for t in tiles:
                    dve.wait_ge(y_added, 4 * LAST_PAIR + t + 1)
                    nc.vector.bn_stats(st[:, t % NTB], rows[:, t, :]).then_inc(stats, 1)
                for t in tiles:
                    dve.wait_ge(stats, t + 1)
                    nc.vector.bn_aggr(mv[:, t % NTB], st[:, t % NTB]).then_inc(aggr, 1)

            def normalise(tb):
                dve.wait_ge(rstd_done, tb + 1)
                for t in range(NTB * tb, NTB * (tb + 1)):
                    j = t % NTB
                    nc.vector.tensor_scalar(rows[:, t, :], rows[:, t, :], mv[:, j, 0:1], rstd[:, j, 0:1],
                                            ALU.subtract, ALU.mult).then_inc(ln_ready, 1)

            def times_gate(u, c):
                dve.wait_ge(gate_done, u * 2 + (c + 1))
                dve.wait_ge(u_ready, u * 2 + (c + 1))
                if from_unit(u, 1):
                    dve.wait_ge(act_done, u * 2 + (c - 1))
                nc.vector.tensor_tensor(gated[:, c, :], up[:, c, :], gate[:, c, :], ALU.mult).then_inc(gated_done, 1)

            def step(u, k):
                if isinstance(u, int) and u == 0:
                    times_gate(0, 0)
                    times_gate(0, 1)
                for c in range(2):
                    if from_unit(u, 1):
                        times_gate(u, c)
                    if isinstance(u, int) and u > LAST_PAIR and c:
                        statistics(u - LAST_PAIR - 1)
                    dve.wait_ge(act_hi_done, u * 2 + (c + 1))
                    nc.vector.tensor_tensor(act_lo[:, k % 2, c, :], act_f[:, c, :], f32(act_hi[:, k % 2, c, :]),
                                            ALU.subtract).then_inc(act_lo_done, 1)
                    if c == 0 and from_unit(u, 1):
                        add_up(u - 1, (k - 1) % NTB)
                    if isinstance(u, int) and u > LAST_PAIR and c:
                        normalise(u - LAST_PAIR - 1)
            units(dve, step)
            add_up(UNITS - 1, NTB - 1)
            statistics(NTB - 1)
            normalise(NTB - 1)
            dve.wait_ge(last_x1_landed, 32)
            for s in range(2):
                dve.wait_ge(ln_ready, NT - 1 + s)
                nc.vector.tensor_tensor(spare[:, s, :], spare[:, s, :], rows[:, NT - 2 + s, :], ALU.add
                                        ).then_inc(last_out_ready, 1)

        @block.tensor
        def _(pe):
            def hidden(u, k, c):
                w, tb = (k // NTB) % 2, k % NTB
                n = u * 2 + c
                if c == 0 and tb == 0 and from_unit(u, 1):
                    pe.wait_ge(w_split, u * 3)
                if from_unit(u, 1):
                    pe.wait_ge(gated_done, n - 1)
                toks = slice(tb * NB, (tb + 1) * NB)
                for m, bank, ready in ((GATE, gp, g_ready), (UP, up, u_ready)):
                    three_passes(nc, bank[:, c, :],
                                 lambda kc: (w_hi[w][:, c, m, kc * P:(kc + 1) * P], w_lo[w][:, c, m, kc * P:(kc + 1) * P],
                                             h_hi[:, kc, toks], h_lo[:, kc, toks]), KC).then_inc(ready, 1)

            def down(u, k, halves=(0, 1)):
                w = (k // NTB) % 2
                pe.wait_ge(act_lo_done, u * 2 + (halves[-1] + 1))
                for s in range(NTB):
                    if halves[0]:
                        pass
                    elif from_unit(u, 1):
                        pe.wait_ge(y_added, u * 4 + (s - 3))
                    elif s == 0:
                        pe.wait_ge(cwT_ready, NTB)
                    tile = slice(s * P, (s + 1) * P)
                    last = three_passes(nc, yp[:, s, :],
                                        lambda c: (act_hi[:, k % 2, c, tile], act_lo[:, k % 2, c, tile],
                                                   w_hi[w][:, c, DOWN, :], w_lo[w][:, c, DOWN, :]), 2, halves)
                    if halves[-1] == 1:
                        last.then_inc(y_ready, 1)

            def turn_routing():
                pe.wait_ge(cw_ready, 1)
                for b in range(NTB):
                    for q in range(NTB):
                        last = nc.tensor.transpose(yp[0:E, b, q * P:(q + 1) * P], cw[:, b * NTB + q, :], ident[:])
                    last.then_inc(cwT_turned, 1)

            def step(u, k):
                hidden(u, k, 0)
                if isinstance(u, int) and u == 0:
                    turn_routing()
                if from_unit(u, 1):
                    down(u - 1, k - 1)
                hidden(u, k, 1)
            units(pe, step)
            for half in range(2):
                down(UNITS - 1, UNITS - 1, (half,))


def build_layer(nc, x, wqkv, wproj, wgate, wexp, out):
    qk_dram = nc.dram_tensor("qk_parts", [4, D, T], F32, kind="Internal").ap()
    x1_dram = nc.dram_tensor("x1_tiles", [NT, P, D], F32, kind="Internal").ap()
    cw_dram = nc.dram_tensor("routing", [NGROUPS, T], F32, kind="Internal").ap()
    x_tiles = x.rearrange("(n p) d -> n p d", p=P)
    out_tiles = out.rearrange("(n p) d -> n p d", p=P)
    with ExitStack() as ctx:
        rows = ctx.enter_context(nc.sbuf_tensor("rows", [P, NT, D], F32))
        ident = ctx.enter_context(nc.sbuf_tensor("ident", [P, P], F32))
        ln_consts = ctx.enter_context(nc.sbuf_tensor("ln_consts", [P, 2], F32))
        with ExitStack() as early:
            v_all = early.enter_context(nc.sbuf_tensor("v_all", [P, H, NT, VW], F32R))
            stage_embed_qkv(nc, x_tiles, wqkv, rows, v_all, ident, ln_consts, qk_dram)
            stage_attention(nc, rows, v_all, ident, qk_dram)
        h_hi = ctx.enter_context(nc.sbuf_tensor("h_hi", [P, KC, T], F32R))
        h_lo = ctx.enter_context(nc.sbuf_tensor("h_lo", [P, KC, T], F32R))
        wexp_raw = ctx.enter_context(nc.sbuf_tensor("wexp_raw", [P, 2, 3, NB], F32))
        wexp_hi = ctx.enter_context(nc.sbuf_tensor("wexp_hi", [P, 2, 3, NB], F32R))
        wexp_lo = ctx.enter_context(nc.sbuf_tensor("wexp_lo", [P, 2, 3, NB], F32R))
        x1 = ctx.enter_context(nc.sbuf_tensor("x1", [P, 4, D], F32))
        spare = ctx.enter_context(nc.sbuf_tensor("spare", [P, 2, D], F32))
        stage_project(nc, x_tiles, wproj, wgate, wexp, rows, ident, ln_consts, h_hi, h_lo, x1_dram, x1,
                      router_views(spare)[0], wexp_raw, wexp_hi, wexp_lo)
        stage_experts(nc, wexp, cw_dram, x1_dram, out_tiles, rows, ident, ln_consts, h_hi, h_lo, x1, spare,
                      wexp_raw, wexp_hi, wexp_lo)


def kernel(L0_attn_x, L0_attn_W_qkv, L0_attn_W_proj, L0_ffn_gate_w, L0_ffn_w_gate, L0_ffn_w_up, L0_ffn_w_down):
    import concourse.bacc as bacc
    from concourse.bass_utils import run_bass_kernel_spmd

    def contraction_first(w):
        return np.ascontiguousarray(np.asarray(w).T.reshape(KC, P, -1).transpose(1, 0, 2))

    def hidden_chunks(w):
        w = np.asarray(w).reshape(CHUNKS, P, KC, P)
        return w.transpose(3, 0, 2, 1).reshape(P, CHUNKS, NB)

    down = np.asarray(L0_ffn_w_down).transpose(0, 2, 1).reshape(CHUNKS, P, D).transpose(1, 0, 2)
    experts = np.stack([hidden_chunks(L0_ffn_w_gate), hidden_chunks(L0_ffn_w_up), down], axis=2)
    arrays = {
        "x": np.ascontiguousarray(np.asarray(L0_attn_x).reshape(T, D)),
        "wqkv": contraction_first(L0_attn_W_qkv),
        "wproj": contraction_first(L0_attn_W_proj),
        "wgate": contraction_first(L0_ffn_gate_w),
        "wexp": np.ascontiguousarray(experts.reshape(P, PAIRS, 2 * 3 * NB)),
    }
    nc = bacc.Bacc("TRN2", target_bir_lowering=False, num_devices=1)
    aps = {n: nc.dram_tensor(n, a.shape, mybir.dt.from_np(a.dtype), kind="ExternalInput").ap() for n, a in arrays.items()}
    out = nc.dram_tensor("out", (T, D), F32, kind="ExternalOutput").ap()
    build_layer(nc, out=out, **aps)
    r = run_bass_kernel_spmd(nc, [arrays], core_ids=[0])
    return r.results[0]["out"].reshape(np.asarray(L0_attn_x).shape)
```

```python
from contextlib import ExitStack

import numpy as np

import concourse.bass as bass
from concourse import mybir

F32 = mybir.dt.float32
F32R = mybir.dt.float32r
ALU = mybir.AluOpType
ACT = mybir.ActivationFunctionType
AX_X = mybir.AxisListType.X

P = 128
T, D, H = 2048, 512, 16
HD = D // H
E, F, TOPK = 16, 352, 6
KC = D // P
NT = T // P
NB = 512
NTB = T // NB
EPS = 1e-5
SCALE = float(1.0 / np.sqrt(D))
MASKED = -1e30
LOWEST = -3e38
VW = 2 * HD + 1
PIECE = 256
VPIECES = D // PIECE
QK_PIECES = 2 * D // PIECE
PIECE_UNITS = PIECE // P * NTB
CHUNKS = E * F // P
PAIRS = CHUNKS // 2
SPLITS = 6
GROUP = 32
NGROUPS = E * F // GROUP
GPE = F // GROUP
assert F % GROUP == 0 and E * F % (2 * P) == 0 and D == NB


def stepped(eng, first, loops, unroll, total, step):
    for t in range(first):
        step(t, t)
    with eng.Fori(0, loops) as i:
        for k in range(unroll):
            step(i * unroll + (first + k), first + k)
    for t in range(first + loops * unroll, total):
        step(t, t)


def inside(t, offset, total):
    return not isinstance(t, int) or 0 <= t + offset < total


def f32(ap):
    return ap.bitcast(F32)


def one(ap, t):
    return ap[bass.ds(t, 1)].rearrange("a p d -> (a p) d")


def three_passes(nc, out, pairs, chunks, part=None):
    for c in part or range(chunks):
        a_hi, a_lo, b_hi, b_lo = pairs(c)
        for n, (a, b) in enumerate(((a_hi, b_hi), (a_hi, b_lo), (a_lo, b_hi))):
            last = nc.tensor.matmul(out, a, b, start=c == n == 0, stop=c == chunks - 1 and n == 2)
    return last


def attention_constants(nc, pool, step, ident, fold, ident_r, mask_q, mask_k, mask_f):
    count = [0]

    def make(ins):
        count[0] += 1
        ins.then_inc(step, 1)
        pool.wait_ge(step, count[0])

    make(nc.gpsimd.memset(fold[:], 0.0))
    for off in (0, HD):
        make(nc.gpsimd.affine_select(out=fold[:, 0:HD], in_=fold[:, 0:HD], compare_op=ALU.not_equal, fill=1.0,
                                     base=-off, pattern=[[-1, HD]], channel_multiplier=1))
    make(nc.gpsimd.memset(fold[2 * HD:VW, HD:HD + 1], 1.0))
    make(nc.gpsimd.tensor_copy(ident_r[:], ident[:]))
    make(nc.gpsimd.memset(mask_f[:], 0.0))
    make(nc.gpsimd.affine_select(out=mask_f[:, 0:P], in_=mask_f[:, 0:P], compare_op=ALU.is_ge, fill=MASKED,
                                 base=0, pattern=[[-1, P]], channel_multiplier=1))
    make(nc.gpsimd.tensor_copy(mask_q[:], mask_f[:, 0:P]))
    make(nc.gpsimd.memset(mask_f[:, 0:P], 0.0))
    make(nc.gpsimd.affine_select(out=mask_f[:], in_=mask_f[:], compare_op=ALU.is_ge, fill=MASKED,
                                 base=-P, pattern=[[1, 2 * P]], channel_multiplier=-1))
    make(nc.gpsimd.tensor_copy(mask_k[:], mask_f[:]))


def stage_embed_qkv(nc, x_dram, wqkv_dram, rows, v_all, ident, ln_consts, qk_dram, multi, head0_landed, parked, masks):
    with ExitStack() as ctx:
        sb = lambda n, s, d: ctx.enter_context(nc.sbuf_tensor(n, s, d))
        pb = lambda n, s: ctx.enter_context(nc.psum_tensor(n, s, F32))
        sem = lambda n: ctx.enter_context(nc.semaphore(n))

        w_raw = rows[:, 0:12, :].rearrange("p a b -> p (a b)").rearrange("p (k n) -> p k n", k=KC)
        x_in = rows[:, 12:16, :]
        xn = sb("xn", [P, 2, D], F32)
        st = sb("e_st", [P, 2, 6], F32)
        mv = sb("e_mv", [P, 2, 2], F32)
        rstd = sb("e_rstd", [P, 2, 1], F32)
        veps = sb("e_veps", [P, 1], F32)
        xt_hi, xt_lo = (multi[:, 0, i * T // 2:(i + 1) * T // 2].rearrange("p (s c q) -> p s c q", s=2, c=KC)
                        for i in range(2))
        xT_hi = sb("xT_hi", [P, KC, T], F32R)
        xT_lo = sb("xT_lo", [P, KC, T], F32R)
        w_hi = sb("e_w_hi", [P, 3, KC, PIECE], F32R)
        w_lo = sb("e_w_lo", [P, 3, KC, PIECE], F32R)
        qk_hi, qk_lo = x_in[:, 0:2, :].bitcast(F32R), x_in[:, 2:4, :].bitcast(F32R)
        tp = pb("e_tp", [P, 2, KC, P])
        vp = pb("e_vp", [P, 2, NB])
        qp = pb("e_qp", [P, 2, NB])

        ident_made, ones_set, masks_step = sem("e_ident_made"), sem("e_ones_set"), sem("e_masks_step")
        x_landed = [sem(f"e_x_landed{i}") for i in range(4)]
        wv_landed, wqk_landed = [sem(f"e_wv_landed{v}") for v in range(VPIECES)], sem("e_wqk_landed")
        stats, aggr, rstd_done = sem("e_stats"), sem("e_aggr"), sem("e_rstd_done")
        veps_done = sem("e_veps_done")
        xn_ready, tp_ready = sem("e_xn_ready"), sem("e_tp_ready")
        xt_hi_done, xt_lo_done, xT_copied = sem("e_xt_hi_done"), sem("e_xt_lo_done"), [sem(f"e_xT_copied{i}") for i in range(2)]
        v_ready, v_hi_done, v_lo_done = sem("e_v_ready"), sem("e_v_hi_done"), sem("e_v_lo_done")
        wv_hi_done, wv_lo_done = sem("e_wv_hi_done"), sem("e_wv_lo_done")
        wqk_hi_done, wqk_lo_done = sem("e_wqk_hi_done"), sem("e_wqk_lo_done")
        unit_ready, unit_hi_done, unit_lo_done = sem("e_unit_ready"), sem("e_unit_hi"), sem("e_unit_lo")
        block = ctx.enter_context(nc.Block())

        def slot_of(q):
            return (VPIECES + q) % 3

        def qk_units(eng, unit, before=lambda n: None):
            for q in range(QK_PIECES):
                for f in range(PIECE // P):
                    base = (q * (PIECE // P) + f) * NTB
                    before(base)
                    if base == 0:
                        for n in range(NTB):
                            unit(n, n % 2, q, f, n)
                    else:
                        with eng.Fori(0, NTB // 2) as i:
                            for k in range(2):
                                unit(i * 2 + (base + k), k, q, f, i * 2 + k)

        @block.sync
        def _(sp):
            for s in range(4):
                sp.dma_start(x_in[:, s, :], x_dram[s]).then_inc(x_landed[s], 16)
                if s < VPIECES:
                    cols = slice(2 * D + s * PIECE, 2 * D + (s + 1) * PIECE)
                    sp.dma_start(w_raw[:, :, cols], wqkv_dram[:, :, cols]).then_inc(wv_landed[s], 16)

            def tile(t, k):
                if inside(t, 4, NT):
                    sp.wait_ge(xn_ready, t + 1)
                    sp.dma_start(x_in[:, k % 4, :], one(x_dram, t + 4)).then_inc(x_landed[k % 4], 16)
                sp.wait_ge(xt_lo_done, t + 1)
                toks = bass.ds(t * P, P)
                sp.dma_start(f32(xT_hi[:, :, toks]), f32(xt_hi[:, k % 2])).then_inc(xT_copied[k % 2], 16)
                sp.dma_start(f32(xT_lo[:, :, toks]), f32(xt_lo[:, k % 2])).then_inc(xT_copied[k % 2], 16)
                if isinstance(t, int) and t == 3:
                    sp.dma_start(w_raw[:, :, 0:2 * D], wqkv_dram[:, :, 0:2 * D]).then_inc(wqk_landed, 16)
            stepped(sp, 4, 2, 4, NT, tile)

            def park(n, k, q, f, tb):
                which, row = 1 - q // 2, (q % 2) * PIECE + f * P
                sp.wait_ge(unit_lo_done, n + 1)
                for part, src in enumerate((qk_hi, qk_lo)):
                    sp.dma_start(qk_dram[2 * which + part, row:row + P, bass.ds(tb * NB, NB)],
                                 f32(src[:, k, :])).then_inc(parked[k], 16)

            def first_head(n):
                for at, stack, parts in ((PIECE_UNITS, 0, (2, 3, 2)), (3 * PIECE_UNITS, 1, (0, 0, 1))):
                    if n == at:
                        for k in range(2):
                            sp.wait_ge(parked[k], 16 * n)
                        for i, part in enumerate(parts):
                            sp.dma_start(f32(multi[i * HD:(i + 1) * HD, stack, :]), qk_dram[part, 0:HD, :]
                                         ).then_inc(head0_landed, 16)
            qk_units(sp, park, first_head)

        @block.gpsimd
        def _(pool):
            nc.gpsimd.memset(ident[:], 0.0).then_inc(ident_made, 1)
            pool.wait_ge(ident_made, 1)
            nc.gpsimd.affine_select(out=ident[:], in_=ident[:], compare_op=ALU.not_equal, fill=1.0, base=0,
                                    pattern=[[-1, P]], channel_multiplier=1).then_inc(ident_made, 1)
            nc.gpsimd.memset(ln_consts[:, 0:1], EPS).then_inc(ident_made, 1)
            nc.gpsimd.memset(ln_consts[:, 1:2], -0.5).then_inc(ident_made, 1)
            pool.wait_ge(ident_made, 4)
            nc.gpsimd.memset(f32(v_all[:, :, :, 2 * HD:VW]), 1.0).then_inc(ones_set, 1)

            def inverse_deviation(t, k):
                pool.wait_ge(aggr, t + 1)
                if inside(t, -1, NT):
                    pool.wait_ge(rstd_done, t)
                nc.gpsimd.tensor_tensor(veps[:], mv[:, k % 2, 1:2], ln_consts[:, 0:1], ALU.add).then_inc(veps_done, 1)
                pool.wait_ge(veps_done, t + 1)
                nc.gpsimd.tensor_tensor(rstd[:, k % 2], veps[:], ln_consts[:, 1:2], ALU.pow).then_inc(rstd_done, 1)

            def split(q, chunk):
                done = wqk_hi_count[0] = wqk_hi_count[0] + 1
                src = (q + QK_PIECES // 2) % QK_PIECES
                raw = w_raw[:, chunk, src * PIECE:(src + 1) * PIECE]
                nc.gpsimd.tensor_copy(w_hi[:, slot_of(q), chunk], raw).then_inc(wqk_hi_done, 1)
                pool.wait_ge(wqk_hi_done, done)
                nc.gpsimd.tensor_tensor(w_lo[:, slot_of(q), chunk], raw, f32(w_hi[:, slot_of(q), chunk]),
                                        ALU.subtract).then_inc(wqk_lo_done, 1)
            wqk_hi_count = [0]

            def step(t, k):
                inverse_deviation(t, k)
                if isinstance(t, int) and t >= NT - KC:
                    if t == NT - KC:
                        pool.wait_ge(wqk_landed, 16)
                    split(0, slice(t - (NT - KC), t - (NT - KC) + 1))
            stepped(pool, 4, 2, 4, NT, step)

            for q in range(1, QK_PIECES):
                if 1 <= q <= VPIECES:
                    pool.wait_ge(v_ready, NT)
                if q > VPIECES:
                    pool.wait_ge(unit_ready, (q - 2) * PIECE_UNITS)
                split(q, slice(0, KC))
            attention_constants(nc, pool, masks_step, ident, mask_f=xn[:, 0, 0:2 * P], **masks)

        @block.scalar
        def _(act):
            for v in range(VPIECES):
                act.wait_ge(wv_landed[v], 16)
                nc.scalar.activation(w_hi[:, v], w_raw[:, :, 2 * D + v * PIECE:2 * D + (v + 1) * PIECE],
                                     ACT.Copy).then_inc(wv_hi_done, 1)
            act.wait_ge(ones_set, 1)

            def high_parts(t, k):
                if inside(t, 0, NT):
                    act.wait_ge(tp_ready, t + 1)
                    if inside(t, -2, NT):
                        act.wait_ge(xT_copied[k % 2], (t - k % 2) * 16)
                        act.wait_ge(v_ready, t - 1)
                    nc.scalar.activation(xt_hi[:, k % 2], tp[:, k % 2], ACT.Copy).then_inc(xt_hi_done, 1)
                if inside(t, -1, NT):
                    act.wait_ge(v_ready, t)
                    nc.scalar.activation(v_all[:, :, bass.ds(t - 1, 1), 0:HD].rearrange("p h a c -> p (h a) c"),
                                         vp[:, (k - 1) % 2, :].rearrange("p (h c) -> p h c", h=H),
                                         ACT.Copy).then_inc(v_hi_done, 1)
            stepped(act, 4, 2, 4, NT + 1, high_parts)

            def unit_high(n, k, q, f, tb):
                act.wait_ge(unit_ready, n + 1)
                if not isinstance(n, int) or n >= 2:
                    act.wait_ge(parked[k], (n - k) * 16)
                nc.scalar.activation(qk_hi[:, k, :], qp[:, k, :], ACT.Copy).then_inc(unit_hi_done, 1)
            qk_units(act, unit_high)

        @block.vector
        def _(dve):
            def statistics(t, k):
                s, j = k % 4, k % 2
                dve.wait_ge(x_landed[s], (t - s) * 4 + 16)
                nc.vector.bn_stats(st[:, j], x_in[:, s, :]).then_inc(stats, 1)

            def aggregate(t, k):
                nc.vector.bn_aggr(mv[:, k % 2], st[:, k % 2]).then_inc(aggr, 1)

            def normalise(t, k):
                dve.wait_ge(rstd_done, t + 1)
                if inside(t, -2, NT):
                    dve.wait_ge(tp_ready, t - 1)
                nc.vector.tensor_scalar(xn[:, k % 2], x_in[:, k % 4, :], mv[:, k % 2, 0:1], rstd[:, k % 2, 0:1],
                                        ALU.subtract, ALU.mult).then_inc(xn_ready, 1)

            def low_parts(t, k):
                if inside(t, 2, NT):
                    statistics(t + 2, k + 2)
                    dve.wait_ge(stats, t + 3)
                if inside(t, 1, NT):
                    normalise(t + 1, k + 1)
                if inside(t, 2, NT):
                    aggregate(t + 2, k + 2)
                if inside(t, 0, NT):
                    dve.wait_ge(xt_hi_done, t + 1)
                    nc.vector.tensor_tensor(xt_lo[:, k % 2], tp[:, k % 2], f32(xt_hi[:, k % 2]),
                                            ALU.subtract).then_inc(xt_lo_done, 1)
                if inside(t, -1, NT):
                    dve.wait_ge(v_hi_done, t)
                    v_tile = v_all[:, :, bass.ds(t - 1, 1), :].rearrange("p h a c -> p (h a) c")
                    nc.vector.tensor_tensor(v_tile[:, :, HD:2 * HD],
                                            vp[:, (k - 1) % 2, :].rearrange("p (h c) -> p h c", h=H),
                                            f32(v_tile[:, :, 0:HD]), ALU.subtract).then_inc(v_lo_done, 1)
            for t in range(2):
                statistics(t, t)
                dve.wait_ge(stats, t + 1)
                aggregate(t, t)
            normalise(0, 0)
            for v in range(VPIECES):
                dve.wait_ge(wv_hi_done, v + 1)
                nc.vector.tensor_tensor(w_lo[:, v], w_raw[:, :, 2 * D + v * PIECE:2 * D + (v + 1) * PIECE],
                                        f32(w_hi[:, v]), ALU.subtract).then_inc(wv_lo_done, 1)
            stepped(dve, 4, 2, 4, NT + 1, low_parts)

            def unit_low(n, k, q, f, tb):
                dve.wait_ge(unit_hi_done, n + 1)
                nc.vector.tensor_tensor(qk_lo[:, k, :], qp[:, k, :], f32(qk_hi[:, k, :]),
                                        ALU.subtract).then_inc(unit_lo_done, 1)
            qk_units(dve, unit_low)

        @block.tensor
        def _(pe):
            pe.wait_ge(ident_made, 2)

            def transpose_tile(t, k):
                pe.wait_ge(xn_ready, t + 1)
                if inside(t, -2, NT):
                    pe.wait_ge(xt_lo_done, t - 1)
                for c in range(KC):
                    last = nc.tensor.transpose(tp[:, k % 2, c, :], xn[:, k % 2, c * P:(c + 1) * P], ident[:])
                last.then_inc(tp_ready, 1)

            def values(t, k):
                if inside(t, 1, NT):
                    transpose_tile(t + 1, k + 1)
                pe.wait_ge(xt_lo_done, t + 1)
                if isinstance(t, int) and t == 0:
                    pe.wait_ge(wv_lo_done, VPIECES)
                if inside(t, -2, NT):
                    pe.wait_ge(v_lo_done, t - 1)
                for v in range(VPIECES):
                    last = three_passes(nc, vp[:, k % 2, v * PIECE:(v + 1) * PIECE],
                                        lambda c: (xt_hi[:, k % 2, c], xt_lo[:, k % 2, c], w_hi[:, v, c], w_lo[:, v, c]), KC)
                last.then_inc(v_ready, 1)
            transpose_tile(0, 0)
            stepped(pe, 4, 2, 4, NT, values)

            def unit(n, k, q, f, tb):
                if isinstance(n, int) and n == 0:
                    for slot in range(2):
                        pe.wait_ge(xT_copied[slot], 32 * NT // 2)
                pe.wait_ge(wqk_lo_done, KC + q)
                if not isinstance(n, int) or n >= 2:
                    pe.wait_ge(unit_lo_done, n - 1)
                cols, toks = slice(f * P, (f + 1) * P), bass.ds(tb * NB, NB)
                three_passes(nc, qp[:, k, :],
                             lambda c: (w_hi[:, slot_of(q), c, cols], w_lo[:, slot_of(q), c, cols],
                                        xT_hi[:, c, toks], xT_lo[:, c, toks]), KC).then_inc(unit_ready, 1)
            qk_units(pe, unit)


S_TILES = [(j, kp, 2 * P * max(0, kp - 2 * j)) for j in range(NTB) for kp in range(2 * j + 2)]
NS = len(S_TILES)
J_FIRST = [next(t for t, s in enumerate(S_TILES) if s[0] == j) for j in range(NTB)]
J_LAST = [max(t for t, s in enumerate(S_TILES) if s[0] == j) for j in range(NTB)]
LAG = 4
RING = 5
PIECES = [(qb, kb) for qb in range(NT) for kb in range(qb // 4 + 1)]
NPC = len(PIECES)
QA = 12
NPC_A = sum(1 for qb, _ in PIECES if qb < QA)
PIECES_AT = (0, 0, 0, 0, 2, 2, 3, 3, 4, 1, 1, 3, 3, 3, 3, 2, 3, 2, 3, 2)
PIECES_AT_A = next(t for t in range(NS) if sum(PIECES_AT[:t]) >= NPC_A)
assert sum(PIECES_AT) == NPC and NS == len(PIECES_AT) and NS % RING == 0
SHARED_AT = {3: "max_b", 5: 3, 9: 0, 13: 1, 15: "max_a", 17: 2}
KQ_LOADS = 6
FW = HD + 2
HI_DVE, HI_DVE_LAST = {0, 2, 3, 9, 18}, {1, 2, 3, 5, 7, 8, 9, 11, 13, 15, 17, 19}
LO_POOL, LO_POOL_LAST = set(range(NS)) - {0, 7, 15, 18}, {0, 4, 8, 10, 11, 12, 14, 16, 18}
FIRST_AT = (0, 1, 2)


def first_pieces(t):
    if t not in FIRST_AT:
        return range(0)
    i, left = FIRST_AT.index(t), NPC - NPC_A
    return range(NPC_A + i * left // len(FIRST_AT), NPC_A + (i + 1) * left // len(FIRST_AT))


def load_projection(sp, flat, wproj_dram, wgate_dram, landed):
    for src, at, n in ((wproj_dram, 0, KC * D), (wgate_dram, KC * D, KC * E)):
        sp.dma_start(flat[:, at:at + n].rearrange("p (k n) -> p k n", k=KC), src).then_inc(landed, 16)


def hi_dve_tiles(h):
    return HI_DVE_LAST if isinstance(h, int) and h == H - 1 else HI_DVE


def lo_pool_tiles(h):
    return LO_POOL_LAST if isinstance(h, int) and h == H - 1 else LO_POOL


def count_before(which, t):
    return sum(1 for s in which if s < t)


def stage_attention(nc, rows, v_all, ident, qk_dram, multi, head0_landed, parked, masks, flat, wproj_dram, wgate_dram,
                    wproj_landed):
    with ExitStack() as ctx:
        sb = lambda n, s, d: ctx.enter_context(nc.sbuf_tensor(n, s, d))
        pb = lambda n, s: ctx.enter_context(nc.psum_tensor(n, s, F32))
        sem = lambda n: ctx.enter_context(nc.semaphore(n))

        K_ROWS, ROW_MAX = 3 * HD, 3 * HD
        ks = [multi[:, 0, :], sb("k_stack1", [P, T], F32R)]
        qs = [multi[:, 1, :], sb("q_stack1", [P, T], F32R)]
        vs = [sb(f"v_head{p}", [P, NT, VW], F32R) for p in range(2)]
        prob = sb("prob", [P, RING, 2, NB], F32)
        prob_hi = sb("prob_hi", [P, RING, 2, NB], F32R)
        prob_lo = sb("prob_lo", [P, RING, 2, NB], F32R)
        o_sb = sb("o_sb", [VW, 2, NB], F32)
        fold, ident_r, mask_q, mask_k = (masks[n] for n in ("fold", "ident_r", "mask_q", "mask_k"))
        part_max = sb("part_max", [P, NT, NTB], F32)
        row_max = sb("row_max", [P, NT], F32)
        max_rows = sb("max_rows", [QA, P], F32R)
        max_rows_b = sb("max_rows_b", [NT - QA, P], F32R)
        recip = sb("recip", [P, NTB, 1], F32)

        mp = pb("a_mp", [P, 2, NB])
        sp_ = pb("a_sp", [P, 2, 2, NB])
        op = pb("a_op", [P, NB])
        shared = pb("a_shared", [P, NB])

        ones_set, maxima_cleared = sem("a_ones_set"), sem("a_maxima_cleared")
        kq_landed = [head0_landed, sem("a_kq_landed1")]
        v_landed = [sem(f"a_v_landed{p}") for p in range(2)]
        max_a_landed = [sem(f"a_max_a_landed{p}") for p in range(2)]
        max_b_landed = [sem(f"a_max_b_landed{p}") for p in range(2)]
        piece_ready, piece_done = sem("a_piece_ready"), sem("a_piece_done")
        row_max_a, row_max_b = sem("a_row_max_a"), sem("a_row_max_b")
        max_a_out, max_b_out = sem("a_max_a_out"), sem("a_max_b_out")
        scores_ready, prob_ready = sem("a_scores_ready"), sem("a_prob_ready")
        hi_act, hi_dve = sem("a_hi_act"), sem("a_hi_dve")
        lo_dve, lo_pool = sem("a_lo_dve"), sem("a_lo_pool")
        pv_done, out_copied = sem("a_pv_done"), sem("a_out_copied")
        max_turned, out_turned, out_stored = sem("a_max_turned"), sem("a_out_turned"), sem("a_out_stored")
        recip_done = sem("a_recip_done")
        block = ctx.enter_context(nc.Block())

        def heads(eng, head):
            head(0, 0, 0, True, False)
            with eng.Fori(0, (H - 2) // 2) as i:
                head(i * 2 + 1, 1, i, False, False)
                head(i * 2 + 2, 0, i + 1, False, False)
            head(H - 1, 1, (H - 1) // 2, False, True)

        def wait_hi(eng, h, t):
            tiles = hi_dve_tiles(h)
            if t in tiles:
                eng.wait_ge(hi_dve, h * len(HI_DVE) + (count_before(tiles, t) + 1))
            else:
                eng.wait_ge(hi_act, h * (NS - len(HI_DVE)) + (t - count_before(tiles, t) + 1))

        def wait_lo(eng, h, t):
            tiles = lo_pool_tiles(h)
            if t in tiles:
                eng.wait_ge(lo_pool, h * len(LO_POOL) + (count_before(tiles, t) + 1))
            else:
                eng.wait_ge(lo_dve, h * (NS - len(LO_POOL)) + (t - count_before(tiles, t) + 1))

        @block.sync
        def _(sp):
            def load_head(h, p):
                for dst, parts in ((ks[p], (2, 3, 2)), (qs[p], (0, 0, 1))):
                    for n, part in enumerate(parts):
                        sp.dma_start(f32(dst[n * HD:(n + 1) * HD, :]),
                                     qk_dram[part, bass.ds(h * HD, HD), :]).then_inc(kq_landed[p], 16)
            def load_v(h, p):
                sp.dma_start(f32(vs[p][:]), f32(v_all[:, bass.ds(h, 1), :, :]).rearrange("p a t c -> p (a t) c")
                             ).then_inc(v_landed[p], 16)

            def send_max_a(p):
                sp.dma_start(f32(qs[p][ROW_MAX:ROW_MAX + 1, 0:QA * P]).rearrange("a (t q) -> a t q", t=QA),
                             f32(max_rows[:, :])).then_inc(max_a_landed[p], 16)

            def send_max_b(p):
                sp.dma_start(f32(qs[p][ROW_MAX:ROW_MAX + 1, QA * P:T]).rearrange("a (t q) -> a t q", t=NT - QA),
                             f32(max_rows_b[:, :])).then_inc(max_b_landed[p], 16)

            load_v(0, 0)
            for k in range(2):
                sp.wait_ge(parked[k], 16 * QK_PIECES * PIECE_UNITS)
            sp.wait_ge(max_a_out, 1)
            send_max_a(0)

            def head(h, p, visit, first, last):
                if not last:
                    if not first:
                        sp.wait_ge(scores_ready, h * NS)
                    load_head(h + 1, 1 - p)
                    if not first:
                        sp.wait_ge(pv_done, h * NS)
                    load_v(h + 1, 1 - p)
                if last:
                    sp.wait_ge(scores_ready, h * NS)
                    load_projection(sp, flat, wproj_dram, wgate_dram, wproj_landed)
                sp.wait_ge(max_b_out, h + 1)
                send_max_b(p)
                if not last:
                    sp.wait_ge(max_a_out, h + 2)
                    send_max_a(1 - p)
            heads(sp, head)

        @block.gpsimd
        def _(pool):
            for p in range(2):
                nc.gpsimd.memset(f32(ks[p][ROW_MAX:ROW_MAX + 1, :]), 1.0).then_inc(ones_set, 1)

            def head(h, p, visit, first, last):
                for t in sorted(lo_pool_tiles(h)):
                    j, kp, c0 = S_TILES[t]
                    pool.wait_ge(prob_ready, h * NS + (t + 1))
                    wait_hi(pool, h, t)
                    nc.gpsimd.tensor_tensor(prob_lo[:, t % RING, :, c0:NB], prob[:, t % RING, :, c0:NB],
                                            f32(prob_hi[:, t % RING, :, c0:NB]), ALU.subtract).then_inc(lo_pool, 1)
            heads(pool, head)

        @block.scalar
        def _(act):
            def copy_out(g, j, done):
                act.wait_ge(pv_done, done)
                if not (isinstance(g, int) and g < 2):
                    act.wait_ge(out_turned, g - 1)
                nc.scalar.activation(o_sb[:, j % 2, :], op[0:VW, :], ACT.Copy).then_inc(out_copied, 1)

            def high_part(h, t):
                if t not in hi_dve_tiles(h):
                    c0 = S_TILES[t][2]
                    act.wait_ge(prob_ready, h * NS + (t + 1))
                    nc.scalar.activation(prob_hi[:, t % RING, :, c0:NB], prob[:, t % RING, :, c0:NB],
                                         ACT.Copy).then_inc(hi_act, 1)

            def head(h, p, visit, first, last):
                for t, (j, kp, c0) in enumerate(S_TILES):
                    if t == J_LAST[-1] + LAG - NS and not first:
                        copy_out(h * NTB - 1, NTB - 1, h * NS)
                    for jj in range(NTB - 1):
                        if t == J_LAST[jj] + LAG:
                            copy_out(h * NTB + jj, jj, h * NS + (J_LAST[jj] + 1))
                    act.wait_ge(scores_ready, h * NS + (t + 1))
                    if not (first and t < RING):
                        act.wait_ge(pv_done, h * NS + (t + 1 - RING))
                    nc.scalar.activation(prob[:, t % RING, :, c0:NB], sp_[:, t % 2, :, c0:NB], ACT.Exp,
                                         scale=SCALE).then_inc(prob_ready, 1)
                    high_part(h, t)
            heads(act, head)
            copy_out(H * NTB - 1, NTB - 1, H * NS)

        @block.vector
        def _(dve):
            nc.vector.memset(part_max[:], LOWEST).then_inc(maxima_cleared, 1)
            dve.wait_ge(maxima_cleared, 1)

            def piece(h, n):
                qb, kb = PIECES[n]
                width = min(NB, (qb + 1) * P - kb * NB)
                dve.wait_ge(piece_ready, h * NPC + (n + 1))
                nc.vector.reduce_max(part_max[:, qb, kb:kb + 1], mp[:, n % 2, 0:width], AX_X).then_inc(piece_done, 1)

            def row_maxima(h, part):
                tiles, count, done = ((slice(0, QA), NPC_A, row_max_a) if part == "a" else
                                      (slice(QA, NT), NPC, row_max_b))
                dve.wait_ge(piece_done, h * NPC + count)
                nc.vector.tensor_reduce(row_max[:, tiles], part_max[:, tiles, :], AX_X, ALU.max).then_inc(done, 1)

            def maxima_out(h, part):
                dst, done = (max_rows, max_a_out) if part == "a" else (max_rows_b, max_b_out)
                dve.wait_ge(max_turned, h * 2 + (1 if part == "a" else 2))
                nc.vector.tensor_scalar(dst[:, :], shared[0:dst.shape[0], 0:P], -1.0, None, ALU.mult).then_inc(done, 1)

            def store_out(h, g, j):
                dve.wait_ge(out_turned, g + 1)
                turned = shared[:, 0:NTB * FW].rearrange("p (a c) -> p a c", c=FW)
                nc.vector.reciprocal(recip[:], turned[:, :, HD:HD + 1]).then_inc(recip_done, 1)
                dve.wait_ge(recip_done, g + 1)
                nc.vector.tensor_tensor(rows[:, NTB * j:NTB * (j + 1), bass.ds(h * HD, HD)], turned[:, :, 0:HD],
                                        recip[:].to_broadcast([P, NTB, HD]), ALU.mult).then_inc(out_stored, 1)

            def high_part(h, t):
                if t in hi_dve_tiles(h):
                    c0 = S_TILES[t][2]
                    dve.wait_ge(prob_ready, h * NS + (t + 1))
                    nc.vector.tensor_copy(prob_hi[:, t % RING, :, c0:NB], prob[:, t % RING, :, c0:NB]).then_inc(hi_dve, 1)

            def low_part(h, t):
                if t in lo_pool_tiles(h):
                    return
                c0 = S_TILES[t][2]
                wait_hi(dve, h, t)
                nc.vector.tensor_tensor(prob_lo[:, t % RING, :, c0:NB], prob[:, t % RING, :, c0:NB],
                                        f32(prob_hi[:, t % RING, :, c0:NB]), ALU.subtract).then_inc(lo_dve, 1)

            for n in range(NPC_A):
                piece(0, n)
            row_maxima(0, "a")
            maxima_out(0, "a")

            def head(h, p, visit, first, last):
                for t, (j, kp, c0) in enumerate(S_TILES):
                    if first:
                        for n in first_pieces(t):
                            piece(0, n)
                    if t == (FIRST_AT[-1] + 1 if first else 0):
                        row_maxima(h, "b")
                    if t == PIECES_AT_A and not last:
                        row_maxima(h + 1, "a")
                    pieces = [] if last else list(range(sum(PIECES_AT[:t]), sum(PIECES_AT[:t + 1])))
                    for n in pieces[:1]:
                        piece(h + 1, n)
                    if t >= 1:
                        high_part(h, t - 1)
                    elif not first:
                        high_part(h - 1, NS - 1)
                    for n in pieces[1:3]:
                        piece(h + 1, n)
                    if t >= 1:
                        low_part(h, t - 1)
                    elif not first:
                        low_part(h - 1, NS - 1)
                    for n in pieces[3:]:
                        piece(h + 1, n)
                    what = SHARED_AT.get(t)
                    if what == "max_b":
                        maxima_out(h, "b")
                    if what == "max_a" and not last:
                        maxima_out(h + 1, "a")
                    if what == NTB - 1 and not first:
                        store_out(h - 1, h * NTB - 1, NTB - 1)
                    if what in range(NTB - 1):
                        store_out(h, h * NTB + what, what)
            heads(dve, head)
            high_part(H - 1, NS - 1)
            low_part(H - 1, NS - 1)
            store_out(H - 1, H * NTB - 1, NTB - 1)

        @block.tensor
        def _(pe):
            def piece(h, p, n):
                qb, kb = PIECES[n]
                k0, k1 = kb * NB, min((kb + 1) * NB, (qb + 1) * P)
                if not (isinstance(h, int) and h == 0 and n < 2):
                    pe.wait_ge(piece_done, h * NPC + (n - 1))
                diagonal = k1 == (qb + 1) * P
                last = nc.tensor.matmul(mp[:, n % 2, 0:k1 - k0], qs[p][0:K_ROWS, qb * P:(qb + 1) * P],
                                        ks[p][0:K_ROWS, k0:k1], start=True, stop=not diagonal)
                if diagonal:
                    last = nc.tensor.matmul(mp[:, n % 2, k1 - k0 - P:k1 - k0], ident_r[:], mask_q[:],
                                            start=False, stop=True)
                last.then_inc(piece_ready, 1)

            def turn_maxima(h, part):
                tiles, done = (slice(0, QA), row_max_a) if part == "a" else (slice(QA, NT), row_max_b)
                pe.wait_ge(done, h + 1)
                nc.tensor.matmul(shared[0:tiles.stop - tiles.start, 0:P], row_max[:, tiles], ident[:],
                                 start=True, stop=True).then_inc(max_turned, 1)

            def turn_out(g, j):
                pe.wait_ge(out_copied, g + 1)
                for q in range(NTB):
                    last = nc.tensor.matmul(shared[:, q * FW:q * FW + HD + 1], o_sb[:, j % 2, q * P:(q + 1) * P],
                                            fold[:, 0:HD + 1], start=True, stop=True)
                last.then_inc(out_turned, 1)

            def times_v(h, p, t, parts=(0, 1)):
                j, kp, c0 = S_TILES[t]
                if parts[0] == 0 and t == J_FIRST[j] and not (isinstance(h, int) and h == 0 and j == 0):
                    pe.wait_ge(out_copied, h * NTB + j)
                for part in parts:
                    (wait_hi, wait_lo)[part](pe, h, t)
                    for b in range(2):
                        cols = slice(c0 + (P if b and kp >= 2 * j else 0), NB)
                        last = nc.tensor.matmul(op[0:VW, cols], vs[p][:, 2 * kp + b, :],
                                                (prob_hi, prob_lo)[part][:, t % RING, b, cols],
                                                start=t == J_FIRST[j] and part == b == 0,
                                                stop=t == J_LAST[j] and part == b == 1)
                if parts[-1] == 1:
                    last.then_inc(pv_done, 1)

            def scores(h, p, t):
                j, kp, c0 = S_TILES[t]
                if not (isinstance(h, int) and h == 0 and t < 2):
                    pe.wait_ge(prob_ready, h * NS + (t - 1))
                for b in range(2):
                    kb = 2 * kp + b
                    diagonal = kp >= 2 * j
                    last = nc.tensor.matmul(sp_[:, t % 2, b, c0:NB], ks[p][0:ROW_MAX + 1, kb * P:(kb + 1) * P],
                                            qs[p][0:ROW_MAX + 1, j * NB + c0:(j + 1) * NB], start=True, stop=not diagonal)
                    if diagonal:
                        mask = mask_k[:, :] if b else mask_k[:, P:2 * P]
                        last = nc.tensor.matmul(sp_[:, t % 2, b, c0:c0 + mask.shape[1]], ident_r[:], mask,
                                                start=False, stop=True)
                last.then_inc(scores_ready, 1)

            pe.wait_ge(kq_landed[0], 16 * KQ_LOADS)
            for n in range(NPC_A):
                piece(0, 0, n)
            turn_maxima(0, "a")

            def head(h, p, visit, first, last):
                for t, (j, kp, c0) in enumerate(S_TILES):
                    if t == J_FIRST[NTB - 1]:
                        pe.wait_ge(max_b_landed[p], visit * 16 + 16)
                    pieces = [] if last else list(range(sum(PIECES_AT[:t]), sum(PIECES_AT[:t + 1])))
                    if pieces and pieces[0] == 0:
                        pe.wait_ge(kq_landed[1 - p], (visit + p) * (16 * KQ_LOADS) + 16 * KQ_LOADS)
                    if t == LAG:
                        pe.wait_ge(v_landed[p], visit * 16 + 16)
                    if first:
                        for n in first_pieces(t):
                            piece(0, 0, n)
                    if t == 0:
                        if first:
                            pe.wait_ge(ones_set, 2)
                        pe.wait_ge(max_a_landed[p], visit * 16 + 16)
                    scores(h, p, t)
                    for part, ahead in ((0, pieces[:1]), (1, pieces[1:2])):
                        for n in ahead:
                            piece(h + 1, 1 - p, n)
                        if t >= LAG:
                            times_v(h, p, t - LAG, (part,))
                        elif not first:
                            times_v(h - 1, 1 - p, NS - LAG + t, (part,))
                    for n in pieces[2:]:
                        piece(h + 1, 1 - p, n)
                    what = SHARED_AT.get(t)
                    if what == "max_b":
                        if first:
                            pe.wait_ge(max_a_out, 1)
                        else:
                            pe.wait_ge(out_stored, h * NTB - 1)
                        turn_maxima(h, "b")
                    if what == NTB - 1 and not first:
                        pe.wait_ge(max_b_out, h + 1)
                        turn_out(h * NTB - 1, NTB - 1)
                    if what == 0:
                        if first:
                            pe.wait_ge(max_b_out, 1)
                        else:
                            pe.wait_ge(out_stored, h * NTB)
                        turn_out(h * NTB, 0)
                    if what == 1:
                        pe.wait_ge(out_stored, h * NTB + 1)
                        turn_out(h * NTB + 1, 1)
                    if what == "max_a" and not last:
                        pe.wait_ge(out_stored, h * NTB + 2)
                        turn_maxima(h + 1, "a")
                    if what == 2:
                        if last:
                            pe.wait_ge(out_stored, h * NTB + 2)
                        else:
                            pe.wait_ge(max_a_out, h + 2)
                        turn_out(h * NTB + 2, 2)
            heads(pe, head)
            for t in range(NS - LAG, NS):
                times_v(H - 1, (H - 1) % 2, t)
            pe.wait_ge(out_stored, H * NTB - 1)
            turn_out(H * NTB - 1, NTB - 1)


def stage_project(nc, x_dram, w_landed, w_proj, w_gate, wexp_dram, rows, ident, ln_consts, h_hi, h_lo, x1_dram,
                  x1, wg_hi, wg_lo, wexp_raw, wexp_hi, wexp_lo, x1_stored, h_copied):
    with ExitStack() as ctx:
        sb = lambda n, s, d: ctx.enter_context(nc.sbuf_tensor(n, s, d))
        pb = lambda n, s: ctx.enter_context(nc.psum_tensor(n, s, F32))
        sem = lambda n: ctx.enter_context(nc.semaphore(n))

        w_hi = sb("p_w_hi", [P, KC, D], F32R)
        w_lo = sb("p_w_lo", [P, KC, D], F32R)
        a_in = sb("a_in", [P, 2, D], F32)
        at_hi = sb("at_hi", [P, 2, KC, P], F32R)
        at_lo = sb("at_lo", [P, 2, KC, P], F32R)
        ht_hi = sb("ht_hi", [P, 2, KC, P], F32R)
        ht_lo = sb("ht_lo", [P, 2, KC, P], F32R)
        x_in = sb("p_x_in", [P, 4, D], F32)
        branch = sb("branch", [P, 2, D], F32)
        hn = sb("hn", [P, 2, D], F32)
        st = sb("p_st", [P, 2, 2, 6], F32)
        mv = sb("p_mv", [P, 2, 2, 2], F32)
        rstd = sb("p_rstd", [P, 2, 2, 1], F32)
        veps = sb("p_veps", [P, 2, 1], F32)
        tps = pb("p_tps", [P, 4, NB])
        prj = pb("p_prj", [P, 2, NB])

        w_hi_done, w_lo_done = sem("p_w_hi_done"), sem("p_w_lo_done")
        x_landed = [sem(f"p_x_landed{i}") for i in range(4)]
        a_copied, at_ready, at_hi_done, at_lo_done = (sem("p_a_copied"), sem("p_at_ready"), sem("p_at_hi_done"),
                                                      sem("p_at_lo_done"))
        veps_done = [sem(f"p_veps_done{i}") for i in range(2)]
        proj_ready, x1_ready = sem("p_proj_ready"), sem("p_x1_ready")
        stats1, aggr1, rstd1, branch_ready = sem("p_stats1"), sem("p_aggr1"), sem("p_rstd1"), sem("p_branch_ready")
        stats2, aggr2, rstd2, hn_ready = sem("p_stats2"), sem("p_aggr2"), sem("p_rstd2"), sem("p_hn_ready")
        ht_ready, ht_hi_done, ht_lo_done = sem("p_ht_ready"), sem("p_ht_hi_done"), sem("p_ht_lo_done")
        wexp_landed, wexp_hi_done, wexp_lo_done = sem("p_wexp_landed"), sem("p_wexp_hi_done"), sem("p_wexp_lo_done")
        block = ctx.enter_context(nc.Block())

        STEPS = NT + 2
        SPLIT_FROM = STEPS - SPLITS

        @block.sync
        def _(sp):
            for s in range(4):
                sp.dma_start(x_in[:, s, :], x_dram[s]).then_inc(x_landed[s], 16)

            def step(t, k):
                if isinstance(t, int) and t == 3:
                    sp.wait_ge(w_lo_done, KC + 1)
                    sp.dma_start(wexp_raw[:].rearrange("p c m n -> p (c m n)"), wexp_dram[:, 0, :]).then_inc(wexp_landed, 16)
                if inside(t, -2, NT):
                    sp.wait_ge(ht_lo_done, t - 1)
                    toks = bass.ds((t - 2) * P, P)
                    sp.dma_start(f32(h_hi[:, :, toks]), f32(ht_hi[:, k % 2])).then_inc(h_copied[k % 2], 16)
                    sp.dma_start(f32(h_lo[:, :, toks]), f32(ht_lo[:, k % 2])).then_inc(h_copied[k % 2], 16)
                if inside(t, 0, NT):
                    store(t, k)

            def store(t, k):
                sp.wait_ge(x1_ready, t + 1)
                sp.dma_start(one(x1_dram, t), x1[:, k % 4, :]).then_inc(x1_stored[k % 4], 16)
                if inside(t, 4, NT):
                    sp.dma_start(x_in[:, k % 4, :], one(x_dram, t + 4)).then_inc(x_landed[k % 4], 16)
            stepped(sp, 4, 2, 4, STEPS, step)

        @block.gpsimd
        def _(pool):
            def inverse_deviation(t, which, j, aggr, done):
                pool.wait_ge(aggr, t + 1)
                if inside(t, -1, NT):
                    pool.wait_ge(done, t)
                nc.gpsimd.tensor_tensor(veps[:, which], mv[:, which, j, 1:2], ln_consts[:, 0:1], ALU.add).then_inc(veps_done[which], 1)
                pool.wait_ge(veps_done[which], t + 1)
                nc.gpsimd.tensor_tensor(rstd[:, which, j], veps[:, which], ln_consts[:, 1:2], ALU.pow).then_inc(done, 1)

            def step(t, k):
                if inside(t, 0, NT):
                    inverse_deviation(t, 0, k % 2, aggr1, rstd1)
                if inside(t, -1, NT):
                    inverse_deviation(t - 1, 1, (k - 1) % 2, aggr2, rstd2)
                if inside(t, 0, NT):
                    pool.wait_ge(branch_ready, t + 1)
                    pool.wait_ge(x_landed[k % 4], (t - k % 4) * 4 + 16)
                    if inside(t, -4, NT):
                        pool.wait_ge(x1_stored[k % 4], (t - k % 4) * 4)
                    nc.gpsimd.tensor_tensor(x1[:, k % 4, :], branch[:, k % 2, :], x_in[:, k % 4, :],
                                            ALU.add).then_inc(x1_ready, 1)
                if isinstance(t, int) and t >= SPLIT_FROM:
                    i = t - SPLIT_FROM
                    pool.wait_ge(wexp_hi_done, i + 1)
                    nc.gpsimd.tensor_tensor(wexp_lo[:, i // 3, i % 3, :], wexp_raw[:, i // 3, i % 3, :],
                                            f32(wexp_hi[:, i // 3, i % 3, :]), ALU.subtract).then_inc(wexp_lo_done, 1)
            stepped(pool, 4, 2, 4, STEPS, step)

        @block.scalar
        def _(act):

            def copy_in(t, k):
                if inside(t, -2, NT):
                    act.wait_ge(at_ready, t - 1)
                nc.scalar.activation(a_in[:, k % 2, :], rows[:, bass.ds(t, 1), :].rearrange("p a d -> p (a d)"),
                                     ACT.Copy).then_inc(a_copied, 1)

            def attention_high(t, k):
                act.wait_ge(at_ready, t + 1)
                if inside(t, -2, NT):
                    act.wait_ge(proj_ready, t - 1)
                nc.scalar.activation(at_hi[:, k % 2].rearrange("p c q -> p (c q)"), tps[:, k % 2, :],
                                     ACT.Copy).then_inc(at_hi_done, 1)
            copy_in(0, 0)
            copy_in(1, 1)
            act.wait_ge(w_landed, 32)
            nc.scalar.activation(w_hi[:, 0], w_proj[:, 0, :], ACT.Copy).then_inc(w_hi_done, 1)
            attention_high(0, 0)
            for c in range(1, KC):
                nc.scalar.activation(w_hi[:, c], w_proj[:, c, :], ACT.Copy).then_inc(w_hi_done, 1)
            nc.scalar.activation(wg_hi[:], w_gate, ACT.Copy).then_inc(w_hi_done, 1)

            def step(t, k):
                if inside(t, 1, NT):
                    attention_high(t + 1, k + 1)
                if inside(t, 2, NT):
                    copy_in(t + 2, k + 2)
                if inside(t, -2, NT):
                    act.wait_ge(ht_ready, t - 1)
                    if inside(t, -4, NT):
                        act.wait_ge(h_copied[k % 2], (t - k % 2) * 16 - 32)
                    nc.scalar.activation(ht_hi[:, k % 2].rearrange("p c q -> p (c q)"), tps[:, 2 + k % 2, :],
                                         ACT.Copy).then_inc(ht_hi_done, 1)
                if isinstance(t, int) and t >= SPLIT_FROM:
                    i = t - SPLIT_FROM
                    if i == 0:
                        act.wait_ge(wexp_landed, 16)
                    nc.scalar.activation(wexp_hi[:, i // 3, i % 3, :], wexp_raw[:, i // 3, i % 3, :],
                                         ACT.Copy).then_inc(wexp_hi_done, 1)
            stepped(act, 4, 2, 4, STEPS, step)

        @block.vector
        def _(dve):

            def attention_low(t, k):
                dve.wait_ge(at_hi_done, t + 1)
                nc.vector.tensor_tensor(at_lo[:, k % 2].rearrange("p c q -> p (c q)"), tps[:, k % 2, :],
                                        f32(at_hi[:, k % 2]).rearrange("p c q -> p (c q)"),
                                        ALU.subtract).then_inc(at_lo_done, 1)

            def statistics(t, which, j, src, stats):
                nc.vector.bn_stats(st[:, which, j], src).then_inc(stats, 1)

            def aggregate(t, which, j, aggr):
                nc.vector.bn_aggr(mv[:, which, j], st[:, which, j]).then_inc(aggr, 1)

            def normalise(t, which, j, src, dst, rstd_done, done):
                dve.wait_ge(rstd_done, t + 1)
                nc.vector.tensor_scalar(dst, src, mv[:, which, j, 0:1], rstd[:, which, j, 0:1],
                                        ALU.subtract, ALU.mult).then_inc(done, 1)
            def weight_low(c, lo, raw, hi):
                dve.wait_ge(w_hi_done, c + 1)
                nc.vector.tensor_tensor(lo, raw, f32(hi), ALU.subtract).then_inc(w_lo_done, 1)
            weight_low(0, w_lo[:, 0], w_proj[:, 0, :], w_hi[:, 0])
            attention_low(0, 0)
            for c in range(1, KC):
                weight_low(c, w_lo[:, c], w_proj[:, c, :], w_hi[:, c])
            weight_low(KC, wg_lo[:], w_gate, wg_hi[:])

            def step(t, k):
                if inside(t, 1, NT):
                    attention_low(t + 1, k + 1)
                if inside(t, 0, NT):
                    dve.wait_ge(proj_ready, t + 1)
                    statistics(t, 0, k % 2, prj[:, k % 2, :], stats1)
                    dve.wait_ge(stats1, t + 1)
                if inside(t, -1, NT):
                    dve.wait_ge(x1_ready, t)
                    statistics(t - 1, 1, (k - 1) % 2, x1[:, (k - 1) % 4, :], stats2)
                if inside(t, 0, NT):
                    aggregate(t, 0, k % 2, aggr1)
                if inside(t, -1, NT):
                    dve.wait_ge(stats2, t)
                if inside(t, -2, NT):
                    dve.wait_ge(ht_hi_done, t - 1)
                    nc.vector.tensor_tensor(ht_lo[:, k % 2].rearrange("p c q -> p (c q)"), tps[:, 2 + k % 2, :],
                                            f32(ht_hi[:, k % 2]).rearrange("p c q -> p (c q)"),
                                            ALU.subtract).then_inc(ht_lo_done, 1)
                if inside(t, -1, NT):
                    aggregate(t - 1, 1, (k - 1) % 2, aggr2)
                if inside(t, 0, NT):
                    if inside(t, -2, NT):
                        dve.wait_ge(x1_ready, t - 1)
                    normalise(t, 0, k % 2, prj[:, k % 2, :], branch[:, k % 2, :], rstd1, branch_ready)
                if inside(t, -1, NT):
                    if not (isinstance(t, int) and t < 3):
                        dve.wait_ge(ht_ready, t - 2)
                    normalise(t - 1, 1, (k - 1) % 2, x1[:, (k - 1) % 4, :], hn[:, (k - 1) % 2, :], rstd2, hn_ready)
            stepped(dve, 4, 2, 4, STEPS, step)

        @block.tensor
        def _(pe):
            def turn_attention(t, k):
                pe.wait_ge(a_copied, t + 1)
                if inside(t, -2, NT):
                    pe.wait_ge(at_lo_done, t - 1)
                for c in range(KC):
                    last = nc.tensor.transpose(tps[:, k % 2, c * P:(c + 1) * P], a_in[:, k % 2, c * P:(c + 1) * P], ident[:])
                last.then_inc(at_ready, 1)
            turn_attention(0, 0)

            def step(t, k):
                if inside(t, 1, NT):
                    turn_attention(t + 1, k + 1)
                if inside(t, 0, NT):
                    pe.wait_ge(at_lo_done, t + 1)
                    first = isinstance(t, int) and t == 0
                    if inside(t, -2, NT):
                        pe.wait_ge(branch_ready, t - 1)
                    j = k % 2
                    for c in range(KC):
                        if first:
                            pe.wait_ge(w_lo_done, c + 1)
                        last = three_passes(nc, prj[:, j, :], lambda c: (at_hi[:, j, c], at_lo[:, j, c],
                                                                         w_hi[:, c], w_lo[:, c]), KC, (c,))
                    last.then_inc(proj_ready, 1)
                if inside(t, -2, NT):
                    pe.wait_ge(hn_ready, t - 1)
                    if not (isinstance(t, int) and t < 4):
                        pe.wait_ge(ht_lo_done, t - 3)
                    for c in range(KC):
                        last = nc.tensor.transpose(tps[:, 2 + k % 2, c * P:(c + 1) * P],
                                                   hn[:, k % 2, c * P:(c + 1) * P], ident[:])
                    last.then_inc(ht_ready, 1)
            stepped(pe, 4, 2, 4, STEPS, step)


def router_views(buffer):
    flat, views, at = buffer[:].rearrange("p a d -> p (a d)"), [], 0
    for width in (E, E + 2, E + 2, 8, 1, 1):
        views.append(flat[:, at:at + NT * width].rearrange("p (t e) -> p t e", t=NT))
        at += NT * width
    assert at <= 2 * D
    return views


def stage_experts(nc, w_dram, cw_dram, x1_dram, out_dram, rows, ident, ln_consts, h_hi, h_lo, x1, spare,
                  wg_hi, wg_lo, x1_stored, h_copied, w_raw,
                  w_hi0, w_lo0):
    with ExitStack() as ctx:
        sb = lambda n, s, d: ctx.enter_context(nc.sbuf_tensor(n, s, d))
        pb = lambda n, s: ctx.enter_context(nc.psum_tensor(n, s, F32))
        sem = lambda n: ctx.enter_context(nc.semaphore(n))

        GATE, UP, DOWN = 0, 1, 2
        ROUTE_STEPS = 7 + 2 * NTB
        SPLIT_AT = {2: [0], 3: [1], 4: [2], 5: [3], 6: [4, 5]}
        w_hi = [w_hi0, sb("m_w_hi1", [P, 2, 3, NB], F32R)]
        w_lo = [w_lo0, sb("m_w_lo1", [P, 2, 3, NB], F32R)]
        cwb = sb("cwb", [P, 2, 2, NB], F32)
        gate = sb("m_gate", [P, 2, NB], F32)
        gated = sb("m_gated", [P, 2, NB], F32)
        act_f = sb("m_act", [P, 2, NB], F32)
        act_hi = sb("m_act_hi", [P, 2, 2, NB], F32R)
        act_lo = sb("m_act_lo", [P, 2, 2, NB], F32R)
        logits, scores, rest, best, top, total = router_views(spare)
        cw = logits
        by_expert = x1[0:E].rearrange("p a d -> p (a d)")
        st = sb("m_st", [P, NTB, 6], F32)
        mv = sb("m_mv", [P, NTB, 2], F32)
        rstd = sb("m_rstd", [P, NTB, 1], F32)
        veps = sb("m_veps", [P, NTB, 1], F32)
        gp = pb("m_gp", [P, 2, NB])
        up = pb("m_up", [P, 2, NB])
        yp = pb("m_yp", [P, NTB, NB])

        w_landed, w_hi_done, w_split = sem("m_w_landed"), sem("m_w_hi_done"), sem("m_w_split")
        cw_landed = [sem(f"m_cw_landed{i}") for i in range(2)]
        g_ready, u_ready, gate_done, gated_done = sem("m_g_ready"), sem("m_u_ready"), sem("m_gate_done"), sem("m_gated_done")
        act_done, act_hi_done, act_lo_done = sem("m_act_done"), sem("m_act_hi_done"), sem("m_act_lo_done")
        rows_cleared, y_ready, y_added = sem("m_rows_cleared"), sem("m_y_ready"), sem("m_y_added")
        stats, aggr, rstd_done, ln_ready, out_ready = (sem("m_stats"), sem("m_aggr"), sem("m_rstd_done"),
                                                        sem("m_ln_ready"), sem("m_out_ready"))
        veps_done = sem("m_veps_done")
        last_x1_landed, last_out_ready, last_out_stored = (sem("m_last_x1_landed"), sem("m_last_out_ready"),
                                                           sem("m_last_out_stored"))
        x1_landed = [sem(f"m_x1_landed{i}") for i in range(4)]
        out_stored = [sem(f"m_out_stored{i}") for i in range(4)]
        marks_set, route, exp_done = sem("m_marks_set"), sem("m_route"), sem("m_exp_done")
        cw_ready, cwT_turned, cwT_ready = sem("m_cw_ready"), sem("m_cwT_turned"), sem("m_cwT_ready")
        cw_first, cw_stored = sem("m_cw_first"), sem("m_cw_stored")
        logits_ready, logits_copied, logits_turned = sem("m_logits_ready"), sem("m_logits_copied"), sem("m_logits_turned")
        block = ctx.enter_context(nc.Block())

        UNITS = PAIRS * NTB
        LAST_PAIR = UNITS - NTB

        def units(eng, step):
            stepped(eng, NTB, (UNITS - 2 * NTB) // (2 * NTB), 2 * NTB, UNITS, step)

        def from_unit(u, least):
            return not isinstance(u, int) or u >= least

        @block.sync
        def _(sp):
            w_quarters = w_dram.rearrange("p a (q n) -> p (a q) n", q=NTB)

            def load_raw(u):
                sp.dma_start(w_raw[:].rearrange("p c m n -> p (c m n)"),
                             w_quarters[:, bass.ds(u + NTB, NTB), :].rearrange("p a n -> p (a n)")).then_inc(w_landed, 16)
            load_raw(0)
            groups = cw_dram.rearrange("(e g) t -> e g t", g=GPE)

            def store_routing(e0, e1, t0, t1, stored, count):
                sp.dma_start(groups[e0:e1, :, t0:t1], by_expert[e0:e1, t0:t1].unsqueeze(1)
                             .to_broadcast([e1 - e0, GPE, t1 - t0])).then_inc(stored, 16)
                sp.wait_ge(stored, 16 * count)

            def step(u, k):
                if from_unit(u, 2):
                    sp.wait_ge(act_done, u * 2 - 2)
                tb = k % NTB
                if isinstance(u, int) and u < NTB:
                    sp.wait_ge(cwT_ready, u + 1)
                    store_routing(0, 1, u * NB, (u + 1) * NB, cw_first, u + 1)
                for c in range(2):
                    g0 = (u - tb) * (2 * P // GROUP // NTB) + c * (P // GROUP)
                    sp.dma_start(cwb[:, k % 2, c, :],
                                 cw_dram[bass.ds(g0, P // GROUP), tb * NB:(tb + 1) * NB].unsqueeze(1)
                                 .to_broadcast([P // GROUP, GROUP, NB])).then_inc(cw_landed[k % 2], 16)
                if tb == 0 and from_unit(u, 1) and not (isinstance(u, int) and u >= LAST_PAIR):
                    sp.wait_ge(w_split, u * 3)
                    load_raw(u)
                if isinstance(u, int) and u == NTB - 1:
                    store_routing(1, E, 0, T, cw_stored, 1)
                if isinstance(u, int) and u == LAST_PAIR:
                    for s in range(4):
                        sp.wait_ge(x1_stored[s], 16 * NT // 4)
                    for s in range(4):
                        sp.dma_start(x1[:, s, :], x1_dram[s]).then_inc(x1_landed[s], 16)
                    for s in range(2):
                        sp.dma_start(spare[:, s, :], x1_dram[NT - 2 + s]).then_inc(last_x1_landed, 16)
            units(sp, step)
            for t in range(NT - 2):
                sp.wait_ge(out_ready, t + 1)
                sp.dma_start(out_dram[t], x1[:, t % 4, :]).then_inc(out_stored[t % 4], 16)
                if 2 <= t < NT - 4:
                    sp.wait_ge(out_stored[(t - 2) % 4], 16 * ((t - 2) // 4 + 1))
                    sp.dma_start(x1[:, (t + 2) % 4, :], x1_dram[t + 2]).then_inc(x1_landed[(t + 2) % 4], 16)
            for s in range(2):
                sp.wait_ge(last_out_ready, s + 1)
                sp.dma_start(out_dram[NT - 2 + s], spare[:, s, :]).then_inc(last_out_stored, 16)
            for s in range(4):
                sp.wait_ge(out_stored[s], 16 * len(range(s, NT - 2, 4)))
            sp.wait_ge(last_out_stored, 32)

        @block.gpsimd
        def _(pool):
            nc.gpsimd.memset(scores[:, :, E:E + 1], -1.0).then_inc(marks_set, 1)
            nc.gpsimd.memset(scores[:, :, E + 1:E + 2], -2.0).then_inc(marks_set, 1)
            nc.gpsimd.memset(rows[:, NT - NTB:NT, :], 0.0).then_inc(rows_cleared, 1)

            def split_piece(u0, k, i):
                c, m = i // 3, i % 3
                dst = (k // NTB + 1) % 2
                if i == 0:
                    pool.wait_ge(w_landed, u0 * 4 + 16)
                    if from_unit(u0, 1):
                        pool.wait_ge(y_ready, u0 * 4)
                nc.gpsimd.tensor_copy(w_hi[dst][:, c, m, :], w_raw[:, c, m, :]).then_inc(w_hi_done, 2)
                pool.wait_ge(w_hi_done, u0 * 3 + 2 * (i + 1))
                nc.gpsimd.tensor_tensor(w_lo[dst][:, c, m, :], w_raw[:, c, m, :], f32(w_hi[dst][:, c, m, :]),
                                        ALU.subtract).then_inc(w_split, 2)

            def step(u, k):
                for c in range(2):
                    n = u * 2 + c
                    if c == 0:
                        pool.wait_ge(cw_landed[k % 2], (u - k % 2) * 16 + 32)
                    pool.wait_ge(gated_done, n + 1)
                    if from_unit(u, 1):
                        pool.wait_ge(act_lo_done, n - 1)
                    nc.gpsimd.tensor_tensor(act_f[:, c, :], gated[:, c, :], cwb[:, k % 2, c, :],
                                            ALU.mult).then_inc(act_done, 1)
                    if not (isinstance(u, int) and u >= LAST_PAIR):
                        for i in SPLIT_AT.get(2 * (k % NTB) + c, ()):
                            split_piece(u - k % NTB, k, i)
                    if isinstance(u, int) and u > LAST_PAIR and c:
                        deviation(u - LAST_PAIR - 1)
                        residual(u - LAST_PAIR - 1)

            def deviation(tb):
                pool.wait_ge(aggr, NTB * (tb + 1))
                if tb:
                    pool.wait_ge(rstd_done, tb)
                nc.gpsimd.tensor_scalar(veps[:], mv[:, :, 1:2], EPS, None, ALU.add).then_inc(veps_done, 1)
                pool.wait_ge(veps_done, tb + 1)
                nc.gpsimd.tensor_tensor(rstd[:], veps[:], ln_consts[:, 1:2].to_broadcast([P, NTB]).unsqueeze(2),
                                        ALU.pow).then_inc(rstd_done, 1)

            def residual(tb):
                for t in range(NTB * tb, min(NTB * (tb + 1), NT - 2)):
                    pool.wait_ge(ln_ready, t + 1)
                    pool.wait_ge(x1_landed[t % 4], 16 * (t // 4 + 1))
                    nc.gpsimd.tensor_tensor(x1[:, t % 4, :], x1[:, t % 4, :], rows[:, t, :],
                                            ALU.add).then_inc(out_ready, 1)
            units(pool, step)
            deviation(NTB - 1)
            residual(NTB - 1)

        @block.scalar
        def _(act):
            def copy_logits(b):
                act.wait_ge(logits_ready, b + 1)
                nc.scalar.activation(by_expert[:, b * NB:(b + 1) * NB], yp[0:E, b, :], ACT.Copy).then_inc(logits_copied, 1)

            def exponentials(b):
                act.wait_ge(route, b * ROUTE_STEPS + 2)
                tiles = slice(b * NTB, (b + 1) * NTB)
                nc.scalar.activation(logits[:, tiles], logits[:, tiles], ACT.Exp).then_inc(exp_done, 1)

            def copy_routing(b):
                act.wait_ge(cwT_turned, b + 1)
                nc.scalar.activation(by_expert[:, b * NB:(b + 1) * NB], yp[0:E, b, :], ACT.Copy).then_inc(cwT_ready, 1)

            for slot in range(4):
                act.wait_ge(x1_stored[slot], 16 * NT // 4)
            copy_logits(0)
            for b in range(1, NTB):
                copy_logits(b)
                exponentials(b - 1)
            exponentials(NTB - 1)

            def silu(u, c):
                act.wait_ge(g_ready, u * 2 + (c + 1))
                if from_unit(u, 1):
                    act.wait_ge(gated_done, u * 2 + (c - 1))
                nc.scalar.activation(gate[:, c, :], gp[:, c, :], ACT.Silu).then_inc(gate_done, 1)

            def high_part(u, k, c):
                act.wait_ge(act_done, u * 2 + (c + 1))
                if c == 0 and from_unit(u, 2):
                    act.wait_ge(y_ready, u * 4 - 4)
                nc.scalar.activation(act_hi[:, k % 2, c, :], act_f[:, c, :], ACT.Copy).then_inc(act_hi_done, 1)

            def step(u, k):
                if isinstance(u, int) and u == 0:
                    for b in range(NTB - 1):
                        copy_routing(b)
                    silu(0, 0)
                    copy_routing(NTB - 1)
                    silu(0, 1)
                for c in range(2):
                    if from_unit(u, 1):
                        silu(u, c)
                    high_part(u, k, c)
            units(act, step)

        @block.vector
        def _(dve):
            def router(b):
                tiles, at = slice(b * NTB, (b + 1) * NTB), b * ROUTE_STEPS
                raw = yp[:, b, 0:NTB * E].rearrange("p (t e) -> p t e", t=NTB)
                dve.wait_ge(logits_turned, b + 1)
                nc.vector.tensor_reduce(top[:, tiles, 0], raw, AX_X, ALU.max).then_inc(route, 1)
                dve.wait_ge(route, at + 1)
                nc.vector.tensor_tensor(logits[:, tiles], raw, top[:, tiles].to_broadcast([P, NTB, E]),
                                        ALU.subtract).then_inc(route, 1)
                dve.wait_ge(exp_done, b + 1)
                nc.vector.reduce_sum(total[:, tiles, 0], logits[:, tiles], AX_X).then_inc(route, 1)
                dve.wait_ge(route, at + 3)
                nc.vector.reciprocal(top[:, tiles], total[:, tiles]).then_inc(route, 1)
                dve.wait_ge(route, at + 4)
                if b == 0:
                    dve.wait_ge(marks_set, 2)
                nc.vector.tensor_tensor(scores[:, tiles, 0:E], logits[:, tiles], top[:, tiles].to_broadcast([P, NTB, E]),
                                        ALU.mult).then_inc(route, 1)
                dve.wait_ge(route, at + 5)
                for t in range(b * NTB, (b + 1) * NTB):
                    nc.vector.max(best[:, t, :], scores[:, t, 0:E]).then_inc(route, 1)
                dve.wait_ge(route, at + 5 + NTB)
                nc.vector.memset(best[:, tiles, TOPK:TOPK + 1], -1.0).then_inc(route, 1)
                nc.vector.memset(best[:, tiles, TOPK + 1:TOPK + 2], -2.0).then_inc(route, 1)
                dve.wait_ge(route, at + 7 + NTB)
                for t in range(b * NTB, (b + 1) * NTB):
                    nc.vector.match_replace(rest[:, t, :], best[:, t, :], scores[:, t, :], 0.0).then_inc(route, 1)
                dve.wait_ge(route, at + 7 + 2 * NTB)
                nc.vector.tensor_tensor(cw[:, tiles], scores[:, tiles, 0:E], rest[:, tiles, 0:E],
                                        ALU.subtract).then_inc(cw_ready, 1)
            for b in range(NTB):
                router(b)

            def add_up(u, tb):
                if isinstance(u, int) and u == NTB - 2:
                    dve.wait_ge(rows_cleared, 1)
                for s in range(NTB):
                    dve.wait_ge(y_ready, u * 4 + (s + 1))
                    t = NTB * tb + s
                    if isinstance(u, int) and u < NTB - 1:
                        nc.vector.tensor_copy(rows[:, t, :], yp[:, s, :]).then_inc(y_added, 1)
                    else:
                        nc.vector.tensor_tensor(rows[:, t, :], yp[:, s, :], rows[:, t, :], ALU.add).then_inc(y_added, 1)

            def statistics(tb):
                tiles = range(NTB * tb, NTB * (tb + 1))
                for t in tiles:
                    dve.wait_ge(y_added, 4 * LAST_PAIR + t + 1)
                    nc.vector.bn_stats(st[:, t % NTB], rows[:, t, :]).then_inc(stats, 1)
                for t in tiles:
                    dve.wait_ge(stats, t + 1)
                    nc.vector.bn_aggr(mv[:, t % NTB], st[:, t % NTB]).then_inc(aggr, 1)

            def normalise(tb):
                dve.wait_ge(rstd_done, tb + 1)
                for t in range(NTB * tb, NTB * (tb + 1)):
                    j = t % NTB
                    nc.vector.tensor_scalar(rows[:, t, :], rows[:, t, :], mv[:, j, 0:1], rstd[:, j, 0:1],
                                            ALU.subtract, ALU.mult).then_inc(ln_ready, 1)

            def times_gate(u, c):
                dve.wait_ge(gate_done, u * 2 + (c + 1))
                dve.wait_ge(u_ready, u * 2 + (c + 1))
                if from_unit(u, 1):
                    dve.wait_ge(act_done, u * 2 + (c - 1))
                nc.vector.tensor_tensor(gated[:, c, :], up[:, c, :], gate[:, c, :], ALU.mult).then_inc(gated_done, 1)

            def step(u, k):
                if isinstance(u, int) and u == 0:
                    times_gate(0, 0)
                    times_gate(0, 1)
                for c in range(2):
                    if from_unit(u, 1):
                        times_gate(u, c)
                    if isinstance(u, int) and u > LAST_PAIR and c:
                        statistics(u - LAST_PAIR - 1)
                    dve.wait_ge(act_hi_done, u * 2 + (c + 1))
                    nc.vector.tensor_tensor(act_lo[:, k % 2, c, :], act_f[:, c, :], f32(act_hi[:, k % 2, c, :]),
                                            ALU.subtract).then_inc(act_lo_done, 1)
                    if c == 0 and from_unit(u, 1):
                        add_up(u - 1, (k - 1) % NTB)
                    if isinstance(u, int) and u > LAST_PAIR and c:
                        normalise(u - LAST_PAIR - 1)
            units(dve, step)
            add_up(UNITS - 1, NTB - 1)
            statistics(NTB - 1)
            normalise(NTB - 1)
            dve.wait_ge(last_x1_landed, 32)
            for s in range(2):
                dve.wait_ge(ln_ready, NT - 1 + s)
                nc.vector.tensor_tensor(spare[:, s, :], spare[:, s, :], rows[:, NT - 2 + s, :], ALU.add
                                        ).then_inc(last_out_ready, 1)

        @block.tensor
        def _(pe):
            def hidden(u, k, c, between=None):
                w, tb = (k // NTB) % 2, k % NTB
                n = u * 2 + c
                if c == 0 and tb == 0 and from_unit(u, 1):
                    pe.wait_ge(w_split, u * 3)
                if from_unit(u, 1):
                    pe.wait_ge(gated_done, n - 1)
                toks = slice(tb * NB, (tb + 1) * NB)
                for m, bank, ready in ((GATE, gp, g_ready), (UP, up, u_ready)):
                    if m == UP and between:
                        between()
                    three_passes(nc, bank[:, c, :],
                                 lambda kc: (w_hi[w][:, c, m, kc * P:(kc + 1) * P], w_lo[w][:, c, m, kc * P:(kc + 1) * P],
                                             h_hi[:, kc, toks], h_lo[:, kc, toks]), KC).then_inc(ready, 1)

            def down(u, k, halves=(0, 1)):
                w = (k // NTB) % 2
                pe.wait_ge(act_lo_done, u * 2 + (halves[-1] + 1))
                for s in range(NTB):
                    if halves[0]:
                        pass
                    elif from_unit(u, 1):
                        pe.wait_ge(y_added, u * 4 + (s - 3))
                    elif s == 0:
                        pe.wait_ge(cwT_ready, NTB)
                    tile = slice(s * P, (s + 1) * P)
                    last = three_passes(nc, yp[:, s, :],
                                        lambda c: (act_hi[:, k % 2, c, tile], act_lo[:, k % 2, c, tile],
                                                   w_hi[w][:, c, DOWN, :], w_lo[w][:, c, DOWN, :]), 2, halves)
                    if halves[-1] == 1:
                        last.then_inc(y_ready, 1)

            def router_logits(b):
                toks = slice(b * NB, (b + 1) * NB)
                for slot in range(2):
                    pe.wait_ge(h_copied[slot], (b + 1) * 32 * NTB // 2)
                three_passes(nc, yp[0:E, b, :], lambda kc: (wg_hi[:, kc, :], wg_lo[:, kc, :], h_hi[:, kc, toks],
                                                            h_lo[:, kc, toks]), KC).then_inc(logits_ready, 1)

            def turn_logits(b):
                pe.wait_ge(logits_copied, b + 1)
                for q in range(NTB):
                    last = nc.tensor.transpose(yp[:, b, q * E:(q + 1) * E],
                                               by_expert[:, b * NB + q * P:b * NB + (q + 1) * P], ident[0:E, 0:E])
                last.then_inc(logits_turned, 1)

            def turn_routing(b):
                pe.wait_ge(cw_ready, b + 1)
                for q in range(NTB):
                    last = nc.tensor.transpose(yp[0:E, b, q * P:(q + 1) * P], cw[:, b * NTB + q, :], ident[:])
                last.then_inc(cwT_turned, 1)

            router_logits(0)
            for b in range(1, NTB):
                router_logits(b)
                turn_logits(b - 1)

            def step(u, k):
                if isinstance(u, int) and u == 0:
                    hidden(u, k, 0, lambda: turn_logits(NTB - 1))
                    for b in range(NTB - 1):
                        turn_routing(b)
                    hidden(u, k, 1)
                    turn_routing(NTB - 1)
                    return
                hidden(u, k, 0)
                down(u - 1, k - 1)
                hidden(u, k, 1)
            units(pe, step)
            for half in range(2):
                down(UNITS - 1, UNITS - 1, (half,))


def build_layer(nc, x, wqkv, wproj, wgate, wexp, out):
    qk_dram = nc.dram_tensor("qk_parts", [4, D, T], F32, kind="Internal").ap()
    x1_dram = nc.dram_tensor("x1_tiles", [NT, P, D], F32, kind="Internal").ap()
    cw_dram = nc.dram_tensor("routing", [NGROUPS, T], F32, kind="Internal").ap()
    x_tiles = x.rearrange("(n p) d -> n p d", p=P)
    out_tiles = out.rearrange("(n p) d -> n p d", p=P)
    with ExitStack() as ctx:
        rows = ctx.enter_context(nc.sbuf_tensor("rows", [P, NT, D], F32))
        ident = ctx.enter_context(nc.sbuf_tensor("ident", [P, P], F32))
        ln_consts = ctx.enter_context(nc.sbuf_tensor("ln_consts", [P, 2], F32))
        with nc.sbuf_tensor("multi", [P, 2, T], F32R) as multi:
            pass
        flat = ctx.enter_context(nc.sbuf_tensor("multi_raw", [P, 2 * T], F32))
        head0_landed = ctx.enter_context(nc.semaphore("head0_landed"))
        wproj_landed = ctx.enter_context(nc.semaphore("wproj_landed"))
        with ExitStack() as early:
            v_all = early.enter_context(nc.sbuf_tensor("v_all", [P, H, NT, VW], F32R))
            masks = {n: early.enter_context(nc.sbuf_tensor(n, shape, dtype)) for n, shape, dtype in (
                ("fold", [VW, HD + 2], F32),
                ("ident_r", [P, P], F32R),
                ("mask_q", [P, P], F32R),
                ("mask_k", [P, 2 * P], F32R),
                )}
            parked = [early.enter_context(nc.semaphore(f"qk_parked{i}")) for i in range(2)]
            stage_embed_qkv(nc, x_tiles, wqkv, rows, v_all, ident, ln_consts, qk_dram, multi, head0_landed, parked,
                            masks)
            stage_attention(nc, rows, v_all, ident, qk_dram, multi, head0_landed, parked, masks, flat, wproj, wgate,
                            wproj_landed)
        h_hi = ctx.enter_context(nc.sbuf_tensor("h_hi", [P, KC, T], F32R))
        h_lo = ctx.enter_context(nc.sbuf_tensor("h_lo", [P, KC, T], F32R))
        wexp_hi = ctx.enter_context(nc.sbuf_tensor("wexp_hi", [P, 2, 3, NB], F32R))
        wexp_lo = ctx.enter_context(nc.sbuf_tensor("wexp_lo", [P, 2, 3, NB], F32R))
        x1 = ctx.enter_context(nc.sbuf_tensor("x1", [P, 4, D], F32))
        wg_hi = ctx.enter_context(nc.sbuf_tensor("wg_hi", [P, KC, E], F32R))
        wg_lo = ctx.enter_context(nc.sbuf_tensor("wg_lo", [P, KC, E], F32R))
        x1_stored = [ctx.enter_context(nc.semaphore(f"x1_stored{i}")) for i in range(4)]
        h_copied = [ctx.enter_context(nc.semaphore(f"h_copied{i}")) for i in range(2)]
        w_proj = flat[:, 0:KC * D].rearrange("p (k n) -> p k n", k=KC)
        w_gate = flat[:, KC * D:KC * (D + E)].rearrange("p (k n) -> p k n", k=KC)
        wexp_raw = flat[:, 0:SPLITS * NB].rearrange("p (c m n) -> p c m n", c=2, m=3)
        spare = flat[:, SPLITS * NB:2 * T].rearrange("p (a d) -> p a d", a=2)
        stage_project(nc, x_tiles, wproj_landed, w_proj, w_gate, wexp, rows, ident, ln_consts, h_hi, h_lo,
                      x1_dram, x1, wg_hi, wg_lo, wexp_raw, wexp_hi, wexp_lo, x1_stored, h_copied)
        stage_experts(nc, wexp, cw_dram, x1_dram, out_tiles, rows, ident, ln_consts, h_hi, h_lo, x1, spare,
                      wg_hi, wg_lo, x1_stored, h_copied, wexp_raw, wexp_hi, wexp_lo)


def kernel(L0_attn_x, L0_attn_W_qkv, L0_attn_W_proj, L0_ffn_gate_w, L0_ffn_w_gate, L0_ffn_w_up, L0_ffn_w_down):
    import concourse.bacc as bacc
    from concourse.bass_utils import run_bass_kernel_spmd

    def contraction_first(w):
        return np.ascontiguousarray(np.asarray(w).T.reshape(KC, P, -1).transpose(1, 0, 2))

    def hidden_chunks(w):
        w = np.asarray(w).reshape(CHUNKS, P, KC, P)
        return w.transpose(3, 0, 2, 1).reshape(P, CHUNKS, NB)

    down = np.asarray(L0_ffn_w_down).transpose(0, 2, 1).reshape(CHUNKS, P, D).transpose(1, 0, 2)
    experts = np.stack([hidden_chunks(L0_ffn_w_gate), hidden_chunks(L0_ffn_w_up), down], axis=2)
    arrays = {
        "x": np.ascontiguousarray(np.asarray(L0_attn_x).reshape(T, D)),
        "wqkv": contraction_first(L0_attn_W_qkv),
        "wproj": contraction_first(L0_attn_W_proj),
        "wgate": contraction_first(L0_ffn_gate_w),
        "wexp": np.ascontiguousarray(experts.reshape(P, PAIRS, 2 * 3 * NB)),
    }
    nc = bacc.Bacc("TRN2", target_bir_lowering=False, num_devices=1)
    aps = {n: nc.dram_tensor(n, a.shape, mybir.dt.from_np(a.dtype), kind="ExternalInput").ap() for n, a in arrays.items()}
    out = nc.dram_tensor("out", (T, D), F32, kind="ExternalOutput").ap()
    build_layer(nc, out=out, **aps)
    r = run_bass_kernel_spmd(nc, [arrays], core_ids=[0])
    return r.results[0]["out"].reshape(np.asarray(L0_attn_x).shape)
```
